# Optimizing a Trainium2 kernel written in Bass

```python
import numpy as np
import jax
import jax.numpy as jnp

def _softmax(x, axis=-1):
    return jax.nn.softmax(x, axis=axis)

def _gelu(x):
    return jax.nn.gelu(x, approximate=True)

def _silu(x):
    return jax.nn.silu(x)

def _sigmoid(x):
    return jax.nn.sigmoid(x)

def _layernorm(x, axis=-1, eps=1e-05):
    m = jnp.mean(x, axis=axis, keepdims=True)
    v = jnp.var(x, axis=axis, keepdims=True)
    return (x - m) / jnp.sqrt(v + eps)

def _scatter_add(tgt, idx, src, axis=0):
    return tgt.at[idx].add(src)

def _segment_sum(src, seg, n):
    return jax.ops.segment_sum(src, seg, n)
kernel_name = 'mk_decoder_postln_d1_seqx_r8_0bb897'

def setup_inputs(seed: int=0):
    np.random.seed(seed)
    _w = jnp.asarray

    def _rec_inputs():
        import jax
        import jax.numpy as jnp
        _rk = jax.random.key(seed)
        x = 7.22e-05 + 1 * jax.random.normal(jax.random.fold_in(_rk, 1), (8, 256, 128), jnp.float32)
        _lenS = 256 - jax.random.randint(jax.random.fold_in(_rk, 7), (8,), 0, max(1, 256 // 4) + 1, jnp.int32)
        _lenS2 = 1601 - jax.random.randint(jax.random.fold_in(_rk, 8), (8,), 0, max(1, 1601 // 4) + 1, jnp.int32)
        _ctx_1024P = jax.random.normal(jax.random.fold_in(_rk, 11), (8, 16, 128), jnp.float32)
        _ctx_1024c = jax.random.dirichlet(jax.random.fold_in(_rk, 511), 0.3 * jnp.ones((16,), jnp.float32), (8, 1601))
        _ctx_1024t = jnp.einsum('bsk,bkd->bsd', _ctx_1024c, _ctx_1024P)
        _ctx_1024t = _ctx_1024t * jax.lax.rsqrt(jnp.mean(jnp.square(_ctx_1024t)) + 1e-12) * 0.953939
        ctx_1024 = 4.13588e-05 + 0.999923 * (_ctx_1024t + 0.3 * jax.random.normal(jax.random.fold_in(_rk, 611), (8, 1601, 128), jnp.float32))
        return (x, ctx_1024)
    x, ctx_1024 = _rec_inputs()

    def _L0_attn_setup():
        import jax, jax.numpy as jnp
        import numpy as np
        import math
        B, S, D = (4, 256, 128)
        H = 16
        HD = D // H
        R = 128
        P = 2 * R
        key = jax.random.key(seed)
        ks = jax.random.split(key, 6)
        x = jax.random.normal(ks[0], (B, S, D), dtype=jnp.float32)
        s = 0.02
        Wk = jax.random.normal(ks[1], (D, D), dtype=jnp.float32) * s
        Wq = jax.random.normal(ks[2], (D, D), dtype=jnp.float32) * s
        Wv = jax.random.normal(ks[3], (D, D), dtype=jnp.float32) * s
        Wp = jax.random.normal(ks[4], (D, D), dtype=jnp.float32) * s
        pos_emb_k = jax.random.normal(ks[5], (P, HD), dtype=jnp.float32) * 0.02
        return {'x': x, 'Wq': Wq, 'Wk': Wk, 'Wv': Wv, 'Wp': Wp, 'pos_emb_k': pos_emb_k}
    _L0_attn_all = _L0_attn_setup()
    _L0_attn_in = {k: v for k, v in _L0_attn_all.items() if k in ('Wq', 'Wk', 'Wv', 'Wp', 'pos_emb_k')}
    del _L0_attn_all

    def _L0_xattn_setup():
        import jax, jax.numpy as jnp
        import numpy as np
        D_MODEL = 128
        NHEADS = 16
        DIM_K = D_MODEL // NHEADS

        def _split(x):
            B, S, _ = x.shape
            return x.reshape(B, S, NHEADS, DIM_K).transpose(0, 2, 1, 3)
        key = jax.random.key(seed)
        ks = jax.random.split(key, 7)
        B, S = (4, 256)
        scale = 1.0 / np.sqrt(D_MODEL)
        return {'Q': jax.random.normal(ks[0], (B, S, D_MODEL), jnp.float32), 'K': jax.random.normal(ks[1], (B, S, D_MODEL), jnp.float32), 'V': jax.random.normal(ks[2], (B, S, D_MODEL), jnp.float32), 'Wq': jax.random.normal(ks[3], (D_MODEL, D_MODEL), jnp.float32) * scale, 'Wk': jax.random.normal(ks[4], (D_MODEL, D_MODEL), jnp.float32) * scale, 'Wv': jax.random.normal(ks[5], (D_MODEL, D_MODEL), jnp.float32) * scale, 'Wo': jax.random.normal(ks[6], (D_MODEL, D_MODEL), jnp.float32) * scale}
    _L0_xattn_all = _L0_xattn_setup()
    _L0_xattn_in = {k: v for k, v in _L0_xattn_all.items() if k in ('Wq', 'Wk', 'Wv', 'Wo')}
    del _L0_xattn_all

    def _L0_ffn_setup():
        import jax, jax.numpy as jnp
        import numpy as np
        N_EXPERTS = 8
        CAP_FACTOR = 1.25
        BATCH, SEQ, DMODEL, DFF = (4, 256, 128, 512)
        key = jax.random.key(seed)
        k0, k1, k2, k3 = jax.random.split(key, 4)
        x = jax.random.normal(k0, (BATCH, SEQ, DMODEL), dtype=jnp.float32)
        Wr = jax.random.normal(k1, (DMODEL, N_EXPERTS), dtype=jnp.float32) * 0.02
        W1 = jax.random.normal(k2, (N_EXPERTS, DMODEL, DFF), dtype=jnp.float32) * 0.02
        W2 = jax.random.normal(k3, (N_EXPERTS, DFF, DMODEL), dtype=jnp.float32) * 0.02
        return {'x': x, 'Wr': Wr, 'W1': W1, 'W2': W2}
    _L0_ffn_all = _L0_ffn_setup()
    _L0_ffn_in = {k: v for k, v in _L0_ffn_all.items() if k in ('Wr', 'W1', 'W2')}
    del _L0_ffn_all
    return {'x': x, 'ctx_1024': ctx_1024, 'L0_attn_Wq': _L0_attn_in['Wq'], 'L0_attn_Wk': _L0_attn_in['Wk'], 'L0_attn_Wv': _L0_attn_in['Wv'], 'L0_attn_Wp': _L0_attn_in['Wp'], 'L0_attn_pos_emb_k': _L0_attn_in['pos_emb_k'], 'L0_xattn_Wq': _L0_xattn_in['Wq'], 'L0_xattn_Wk': _L0_xattn_in['Wk'], 'L0_xattn_Wv': _L0_xattn_in['Wv'], 'L0_xattn_Wo': _L0_xattn_in['Wo'], 'L0_ffn_Wr': _L0_ffn_in['Wr'], 'L0_ffn_W1': _L0_ffn_in['W1'], 'L0_ffn_W2': _L0_ffn_in['W2']}

def reference(x, ctx_1024, L0_attn_Wq, L0_attn_Wk, L0_attn_Wv, L0_attn_Wp, L0_attn_pos_emb_k, L0_xattn_Wq, L0_xattn_Wk, L0_xattn_Wv, L0_xattn_Wo, L0_ffn_Wr, L0_ffn_W1, L0_ffn_W2):
    import jax
    import jax.numpy as jnp

    def _L0_attn_ref(x, Wq, Wk, Wv, Wp, pos_emb_k):
        import jax, jax.numpy as jnp
        import numpy as np
        import math
        B, S, D = (4, 256, 128)
        H = 16
        HD = D // H
        R = 128
        P = 2 * R
        batch, ctx, emb = x.shape

        def heads(w):
            return (x @ w.T).reshape(batch, ctx, H, HD).transpose(0, 2, 1, 3)
        q, k, v = (heads(Wq), heads(Wk), heads(Wv))
        att_rel_pos = jnp.einsum('bhsd,pd->bhsp', q, pos_emb_k)
        i = jnp.arange(ctx)
        att_idxs = jnp.clip(i[None, :] - i[:, None], -R, R - 1) % P
        att_pos = jnp.take_along_axis(att_rel_pos, att_idxs[None, None, :, :].astype(jnp.int32), axis=3)
        attn_val = jnp.einsum('bhsd,bhtd->bhst', q, k) + att_pos
        attn_scale = 1.0 / math.sqrt(HD)
        att = jax.nn.softmax((attn_val + att_pos) * attn_scale, axis=-1)
        y = jnp.einsum('bhst,bhtd->bhsd', att, v)
        y = y.transpose(0, 2, 1, 3).reshape(batch, ctx, emb)
        return y @ Wp.T

    def _L0_xattn_ref(Q, K, V, Wq, Wk, Wv, Wo):
        import jax, jax.numpy as jnp
        import numpy as np
        D_MODEL = 128
        NHEADS = 16
        DIM_K = D_MODEL // NHEADS

        def _split(x):
            B, S, _ = x.shape
            return x.reshape(B, S, NHEADS, DIM_K).transpose(0, 2, 1, 3)
        q = _split(Q @ Wq.T)
        k = _split(K @ Wk.T)
        v = _split(V @ Wv.T)
        scores = jnp.einsum('bhsd,bhtd->bhst', q, k) / jnp.sqrt(jnp.float32(DIM_K))
        attn = jax.nn.softmax(scores, axis=-1)
        out = jnp.einsum('bhst,bhtd->bhsd', attn, v)
        B, H, S, dk = out.shape
        out = out.transpose(0, 2, 1, 3).reshape(B, S, H * dk)
        return out @ Wo.T

    def _L0_ffn_ref(x, Wr, W1, W2):
        import jax, jax.numpy as jnp
        import numpy as np
        N_EXPERTS = 8
        CAP_FACTOR = 1.25
        BATCH, SEQ, DMODEL, DFF = (4, 256, 128, 512)
        B, S, D = x.shape
        E = W1.shape[0]
        cap = int(CAP_FACTOR * B * S / E)
        t = x.reshape(-1, D)
        probs = jax.nn.softmax(t @ Wr, axis=-1)
        idx = jnp.argmax(probs, axis=-1)
        pmax = jnp.max(probs, axis=-1)
        onehot = jax.nn.one_hot(idx, E, dtype=jnp.int32)
        pos = jnp.sum(jnp.cumsum(onehot, axis=0) * onehot, axis=-1) - 1
        kept = pos < cap
        flat = idx * cap + jnp.minimum(pos, cap - 1)
        disp = jnp.zeros((E * cap, D), t.dtype).at[flat].add(t * kept[:, None].astype(t.dtype))
        ein = disp.reshape(E, cap, D)
        h = jax.nn.relu(jnp.einsum('ecd,edf->ecf', ein, W1))
        eout = jnp.einsum('ecf,efd->ecd', h, W2).reshape(E * cap, D)
        comb = jnp.where(kept[:, None], eout[flat], t)
        factor = jnp.where(kept, pmax, jnp.ones_like(pmax))
        out = (comb * factor[:, None]).reshape(B, S, D)
        return out
    x = _layernorm(x + _L0_attn_ref(x, L0_attn_Wq, L0_attn_Wk, L0_attn_Wv, L0_attn_Wp, L0_attn_pos_emb_k), axis=-1)
    x = _layernorm(x + _L0_xattn_ref(x, ctx_1024, ctx_1024, L0_xattn_Wq, L0_xattn_Wk, L0_xattn_Wv, L0_xattn_Wo), axis=-1)
    x = _layernorm(x + _L0_ffn_ref(x, L0_ffn_Wr, L0_ffn_W1, L0_ffn_W2), axis=-1)
    return x

_drawn_inputs = setup_inputs


def setup_inputs(seed=0):
    import zlib

    import numpy as np

    out = dict(_drawn_inputs(seed))
    spreads = {}
    factors = {'L0_attn_Wq': 8.0,
     'L0_attn_Wk': 8.0,
     'L0_attn_Wv': 8.0,
     'L0_attn_Wp': 8.0,
     'L0_attn_pos_emb_k': 8.0,
     'L0_ffn_Wr': 4.82,
     'L0_ffn_W1': 5.532,
     'L0_ffn_W2': 4.609}
    for name, (base, spread) in spreads.items():
        noise = np.random.default_rng([zlib.crc32(name.encode()), seed]).standard_normal(out[name].shape)
        drawn = base * np.exp(spread * noise) if base else spread * noise
        out[name] = jnp.asarray(drawn.astype(out[name].dtype))
    for name, factor in factors.items():
        out[name] = (out[name] * factor).astype(out[name].dtype)
    return out
```

```python
import concourse.bass as bass
from concourse import mybir
from contextlib import ExitStack


def decoder_layer(nc, x, ctx_in, w_self, pos_emb, w_cross, w_router, w1, w2, out):
    f32, bf16, i32 = mybir.dt.float32, mybir.dt.bfloat16, mybir.dt.int32
    ALU = mybir.AluOpType
    ACT = mybir.ActivationFunctionType
    AX = mybir.AxisListType.X

    P = 128
    B, S, D = x.shape
    TK = ctx_in.shape[1]
    HD = pos_emb.shape[1]
    H = D // HD
    R = pos_emb.shape[0] // 2
    E, _, FF = w1.shape
    ST = S // P
    TT = -(-TK // P)
    LAST0 = TK - P
    OVER = (TT - 1) * P - LAST0
    TP = -(-TK // 4) * 4
    CAP = int(1.25 * B * S / E)
    SCALE = float(HD) ** -0.5
    EPS = 1e-5
    G = 4
    HG = H // G
    NP = 3
    KR = NP * NP * HD
    KM = KR + NP
    V1 = HD + 1
    LAG = 6
    SLOTS = -(-TT // 2)
    BLK = SLOTS * H
    NCH = 4
    C0 = [TK * c // NCH for c in range(NCH + 1)]
    NL1 = H * ST * NCH
    RW = 3 * P
    NEG = -3.0e38
    NTOK = B * ST
    OOB = 65536.0

    uses = []
    def use(s, k, name, arg=0):
        uses.append((s, k, name, arg))
    for s in range(16):
        for k in range(SLOTS):
            if s == 0 and k in (1, 3, 5):
                use(s, k, ("xT", "qk", "v")[k // 2])
            if s == 1 and 1 <= k <= 4:
                use(s, k, "ctxT", k - 1)
            if 5 <= s <= 12 and k == 0:
                use(s, k, "pv", s - 5)
            if 2 <= s <= 5:
                for n in ((0, 1) if k == 0 else (k + 1,)):
                    use(s, k, "qe", (s - 2) * 8 + n)
            if 4 <= s <= 11:
                if k in (1, 2):
                    use(s, k, "sc", 2 * (s - 4) + k - 1)
                if k in (4, 5):
                    use(s, k, "pt", 2 * (s - 4) + k - 4)
            if 6 <= s <= 9 and k in (3, 6):
                use(s, k, ("kp", "vp")[(s - 6) // 2], 2 * ((s - 6) % 2) + (k == 6))
            if s == 12 and k in (1, 2):
                use(s, k, "oT", k - 1)
            if s == 12 and k == 4:
                use(s, k, "wp")
            if s == 13 and k in (1, 3):
                use(s, k, ("x1T", "cq")[k // 2])
    NU = len(uses)
    assert NU % 2 == 0
    index = {(n, a): u for u, (_, _, n, a) in enumerate(uses)}
    slot_uses = {}
    for s, k, n, a in uses:
        slot_uses.setdefault((s, k), []).append((n, a))

    ctx = ExitStack()
    with ctx:
        def sb(name, shape, dt=f32):
            return ctx.enter_context(nc.sbuf_tensor(name, shape, dt))

        def sem(name):
            return ctx.enter_context(nc.semaphore(name))

        d_sq = nc.dram_tensor("d_sq", (B, NP, NP, HD, H, S), bf16).ap()
        d_sk = nc.dram_tensor("d_sk", (B, NP, HD, H, S), bf16).ap()
        d_q = nc.dram_tensor("d_q", (B, NP, NP, HD, H, S), bf16).ap()
        d_k = nc.dram_tensor("d_k", (B, NP, HD, H, TP), bf16).ap()
        d_m = nc.dram_tensor("d_m", (B, NP, H, ST, P), bf16).ap()
        d_e = nc.dram_tensor("d_e", (NP, HD, 4 * P), bf16).ap()
        d_rel = nc.dram_tensor("d_rel", (G, ST, P, HG * RW), f32).ap()
        d_disp = nc.dram_tensor("d_disp", (E * CAP, D), f32).ap()
        d_eout = nc.dram_tensor("d_eout", (E * CAP, D), f32).ap()

        ident = sb("ident", [P, P])
        ones_bf = sb("ones_bf", [P, P], bf16)
        upper = sb("upper", [P, P], bf16)
        vmask = sb("vmask", [P, 1])
        minus_half = sb("minus_half", [P, NTOK])
        rank = sb("rank", [P, E])
        bias_raw = sb("bias_raw", [P, 2 * ST * HG * S])
        bias = bias_raw[:].rearrange("p (a t h s) -> p a t h s", a=2, t=ST, h=HG)
        wraw = bias_raw[:, 0:8 * D].rearrange("p (w d) -> p w d", w=8)
        zeros = bias_raw[:, 8 * D:13 * D]
        etab = bias_raw[0:HD, 13 * D:17 * D]
        etmp = bias_raw[0:HD, 17 * D:21 * D]
        epart = bias_raw[0:HD, 21 * D:27 * D].bitcast(bf16).rearrange("p (c r) -> p c r", c=NP)
        wT = sb("wT", [P, 8, D])
        WQ, WK, WV, WP, XQ, XK, XV, XO = range(8)
        wr = sb("wr", [P, E])
        posr = sb("posr", [P, 2, HD])
        estack = sb("estack", [KR, 4 * P], bf16)
        xin = sb("xin", [P, ST, D])
        xT = sb("xT", [P, S])
        qk32 = sb("qk32", [P, 2 * S])
        qkp = sb("qkp", [P, NP, 2 * S], bf16)
        sq = sb("sq", [KR, H, S], bf16)
        sk = sb("sk", [KR, H, S], bf16)
        sv = sb("sv", [P, ST, H, V1])
        qe = sb("qe", [P, ST, HG * RW])
        zp = sb("zp", [P, 2, ST, S])
        smx = sb("smx", [P, H, ST])
        snb = sb("snb", [P, H, ST])
        pT = sb("pT", [P, 2, 2 * S])
        soraw = sb("soraw", [P, H, ST, V1])
        srec = sb("srec", [P, H, ST])
        so = sb("so", [P, ST, H, HD])
        soT = sb("soT", [P, ST, P])
        y1 = sb("y1", [P, ST, D])
        st1 = sb("st1", [P, ST, 6])
        mv1 = sb("mv1", [P, ST, 2])
        rs1 = sb("rs1", [P, ST])
        x1 = sb("x1", [P, ST, D])
        x1T = sb("x1T", [P, S])
        q32 = sb("q32", [P, S])
        qp = sb("qp", [P, NP, S], bf16)
        ctxs = sb("ctxs", [P, TT, D])
        ctxT = sb("ctxT", [P, TK])
        k32 = sb("k32", [P, TP])
        tmp32 = sb("tmp32", [P, TP])
        kp = sb("kp", [P, NP, TP], bf16)
        vst = sb("vst", [P, G, TT, HG, V1])
        ks_raw = sb("ks_raw", [P, H * TP], bf16)
        ks = ks_raw[0:KM, :].rearrange("p (h t) -> p h t", h=H)
        qs = sb("qs", [KM, H, S], bf16)
        vb = sb("vb", [P, G, TT, HG, V1])
        mx4 = sb("mx4", [P, H, ST, NCH])
        nmx = sb("nmx", [P, H, ST])
        m32 = sb("m32", [HG * ST, P])
        mt = sb("mt", [HG * ST, P])
        mp = sb("mp", [HG * ST, NP, P], bf16)
        pr = sb("pr", [P, 2, 2 * S])
        orec = sb("orec", [P, ST, H])
        o = sb("o", [P, ST, H, HD])
        oT = sb("oT", [P, S])
        y2 = sb("y2", [P, ST, D])
        st2 = sb("st2", [P, ST, 6])
        mv2 = sb("mv2", [P, ST, 2])
        rs2 = sb("rs2", [P, ST])
        x2 = sb("x2", [P, ST, D])
        x2T = sb("x2T", [P, S])
        lmx = sb("lmx", [P, ST])
        pe_ = sb("pe_", [P, ST, E])
        pmx = sb("pmx", [P, ST])
        psm = sb("psm", [P, ST])
        oh = sb("oh", [P, ST, E])
        okk = sb("okk", [P, ST])
        ohb = sb("ohb", [P, ST, E], bf16)
        acc = sb("acc", [P, 2, E], bf16)
        cum = sb("cum", [P, ST, E])
        pos = sb("pos", [P, ST])
        kept = sb("kept", [P, ST])
        koff = sb("koff", [P, ST])
        fac1 = sb("fac1", [P, ST])
        base = sb("base", [P, ST])
        slot_i = sb("slot_i", [P, ST], i32)
        slots = sb("slots", [P, NTOK], i32)
        fac = sb("fac", [P, NTOK])
        xall = sb("xall", [P, NTOK, D])
        NR = -(-CAP // P)
        FT = FF // P
        ks32, over = ks_raw[:].bitcast(f32), [0]

        def later(*shape):
            n, at = 1, over[0]
            for d in shape:
                n *= d
            over[0] += n
            assert over[0] <= H * TP // 2
            names = "abc"[:len(shape)]
            return ks32[:, at:at + n].rearrange(f"p ({' '.join(names)}) -> p {' '.join(names)}",
                                                **dict(zip(names, shape)))

        w1s = later(2, FF)
        w2s = later(2, FT * D).rearrange("p i (f d) -> p i f d", f=FT)
        ein = later(2, NR, D)
        einT = later(2, CAP)
        hT = later(2, FT, CAP)
        eo = later(2, NR, D)
        comb = later(NTOK, D)
        st3 = sb("st3", [P, NTOK, 6])
        mv3 = sb("mv3", [P, NTOK, 2])
        rs3 = sb("rs3", [P, NTOK])

        banks = [ctx.enter_context(nc.psum_tensor(f"bank{i}", [P, 512], f32)) for i in range(8)]
        b_sc = banks[0:2]
        b_mx = banks[2:4]
        b_o = banks[4]
        b_side = banks[5:7]
        b_fin = banks[7]

        NCONST = 9

        s_win = sem("weights_loaded")
        s_const = sem("constants_made")
        s_wt = sem("weights_transposed")
        s_wtc = sem("weight_transposes_kept")
        s_etab = sem("position_table_steps")
        s_ep = sem("position_parts_steps")
        s_ed = sem("position_parts_stored")
        s_est = sem("position_stack_loaded")
        s_zero = sem("dispatch_zeroed")
        s_x = sem("x_loaded")
        s_ctx = sem("ctx_loaded")
        s_full = [sem("side_bank0_written"), sem("side_bank1_written")]
        s_read = [sem("side_bank0_read"), sem("side_bank1_read")]
        s_sqp = sem("self_parts_steps")
        s_sqd = sem("self_parts_stored")
        s_sst = sem("self_stacks_loaded")
        s_rel = [[sem(f"relative_scores_stored_{a}{c}") for c in range(ST)] for a in range(2)]
        s_bias = [[sem(f"bias_loaded_{a}{c}") for c in range(ST)] for a in range(2)]
        s_z = sem("self_scores_maxed")
        s_nb = sem("self_bias_ready")
        s_sp = sem("self_probs_ready")
        s_so = sem("self_outputs_ready")
        s_x1 = sem("x1_ready")
        s_dch = sem("side_vector_steps")
        s_mv1, s_rs1 = sem("moments1_ready"), sem("deviation1_ready")
        s_mv2, s_rs2 = sem("moments2_ready"), sem("deviation2_ready")
        s_mv3, s_rs3 = sem("moments3_ready"), sem("deviation3_ready")
        s_rch = [sem(f"deviation_step_{i}") for i in range(3)]
        s_qp = sem("q_parts_steps")
        s_qd = sem("q_parts_stored")
        s_kp = sem("k_parts_steps")
        s_kd = sem("k_parts_stored")
        s_ql = [sem(f"q_stack_loaded_{g}") for g in range(G)]
        s_kl = [sem(f"k_stack_loaded_{g}") for g in range(G)]
        s_vl = [sem(f"v_loaded_{g}") for g in range(G)]
        s_x1c = sem("x1_kept")
        s_l1 = sem("max_scores_written")
        s_l1r = sem("max_scores_read")
        s_nm = sem("maxima_ready")
        s_mT = sem("maxima_transposed")
        s_m32 = sem("maxima_kept")
        s_mp = sem("maxima_parts_steps")
        s_md = sem("maxima_parts_stored")
        s_ml = [sem(f"maxima_rows_loaded_{g}") for g in range(G)]
        s_l2 = sem("scores_written")
        s_pr = sem("probs_ready")
        s_pv = sem("probs_used")
        s_or = sem("outputs_read")
        s_fw = sem("finish_bank_written")
        s_fr = sem("finish_bank_read")
        s_fch = sem("finish_vector_steps")
        s_x2 = sem("x2_ready")
        s_le = sem("router_exp_ready")
        s_oh = sem("chosen_expert_ready")
        s_disp = sem("dispatch_rows_ready")
        s_x2c = sem("x2_kept")
        s_sct = sem("tokens_dispatched")
        s_ew = [sem("expert_weights_loaded_0"), sem("expert_weights_loaded_1")]
        s_et = sem("expert_rows_transposed")
        s_etc = sem("expert_rows_kept")
        s_eh = sem("expert_hidden_written")
        s_ehs = sem("expert_hidden_kept_scalar")
        s_ehv = sem("expert_hidden_kept_vector")
        s_eow = sem("expert_output_written")
        s_eo = sem("expert_output_kept")
        s_es = sem("expert_output_stored")
        s_cc = sem("combination_rows_filled")
        s_g = sem("combination_rows_gathered")
        s_cch = sem("combination_vector_steps")
        s_res = sem("result_ready")
        s_out = sem("output_stored")

        s_passed = {e: sem(f"waits_passed_{n}") for e, n in (
            (mybir.EngineType.SP, "sp"), (mybir.EngineType.Pool, "pool"), (mybir.EngineType.DVE, "dve"))}

        def wait_alone(eng, s, v):
            eng.wait_ge(s, v).then_inc(s_passed[eng.engine], 1)

        def wait(eng, s, v):
            if isinstance(v, int):
                if v > 0:
                    eng.wait_ge(s, v)
            elif eng.engine in (mybir.EngineType.SP, mybir.EngineType.Pool):
                wait_alone(eng, s, v)
            else:
                eng.wait_ge(s, v)

        class Steps:
            def __init__(self, eng, s, per, alone=False):
                self.eng, self.s, self.per, self.k, self.alone = eng, s, per, 0, alone

            def link(self, b, ins):
                self.k = self.k % self.per + 1
                ins.then_inc(self.s, 1)
                if self.alone and not isinstance(b, int):
                    wait_alone(self.eng, self.s, b * self.per + self.k)
                else:
                    wait(self.eng, self.s, b * self.per + self.k)

        reads = [[u for u in range(i, NU, 2) if uses[u][2] != "sc"] for i in range(2)]

        def use_read(b, u):
            name, arg = uses[u][2:]
            if name == "sc":
                return s_z, (b * H + arg + 1) * ST
            return s_read[u % 2], b * len(reads[u % 2]) + reads[u % 2].index(u) + 1

        def wait_read(eng, b, name, arg=0):
            wait(eng, *use_read(b, index[(name, arg)]))

        def wait_full(eng, b, name, arg=0):
            u = index[(name, arg)]
            wait(eng, s_full[u % 2], b * (NU // 2) + u // 2 + 1)
            return b_side[u % 2], s_read[u % 2]

        def wait_free(eng, b, name, arg=0):
            u = index[(name, arg)]
            if u >= 2:
                wait(eng, *use_read(b, u - 2))
            else:
                wait(eng, *use_read(b - 1, NU + u - 2))
            return b_side[u % 2], s_full[u % 2]

        def run(eng, maxima, attend, finish, side, maxt):
            def period(b, prev=True, cur=True, nxt=True):
                for s in range(H):
                    for k in range(SLOTS):
                        if k == 0 and s == 0 and prev:
                            maxt(b - 1, G - 1)
                        if k == 0 and s in (HG, 2 * HG, 3 * HG) and cur:
                            maxt(b, s // HG - 1)
                        if cur:
                            maxima(b, s, k)
                        if s < LAG and prev:
                            attend(b - 1, H - LAG + s, k)
                        if s >= LAG and cur:
                            attend(b, s - LAG, k)
                        if prev:
                            finish(b - 1, s, k)
                        if nxt:
                            side(b + 1, s, k)
            for s in range(H):
                for k in range(SLOTS):
                    side(0, s, k)
            period(0, prev=False)
            with eng.Fori(1, B - 1) as b:
                period(b)
            period(B - 1, nxt=False)
            period(B, cur=False, nxt=False)

        def nothing(*_):
            pass

        NDC, NFC = 2, 12
        NPC = 4
        NF = 5

        block = ctx.enter_context(nc.Block())

        @block.sync
        def _(sp):
            for i, w in enumerate([*w_self, *w_cross]):
                sp.dma_start(wraw[:, i, :], w).then_inc(s_win, 16)
            sp.dma_start(wr[:], w_router).then_inc(s_win, 16)
            sp.dma_start(posr[:], pos_emb.rearrange("(r p) d -> p r d", p=P)).then_inc(s_win, 16)
            wait(sp, s_ep, NPC)
            sp.dma_start(d_e.rearrange("a d r -> d a r"), epart[:]).then_inc(s_ed, 16)
            wait(sp, s_ed, 16)
            for c in range(NP):
                sp.dma_start(estack[c * NP * HD:(c + 1) * NP * HD, :],
                             d_e.rearrange("a d r -> (a d) r")).then_inc(s_est, 16)
            wait(sp, s_const, NCONST)
            for c in range(E * CAP // (5 * P)):
                sp.dma_start(d_disp[c * 5 * P:(c + 1) * 5 * P].rearrange("(p a) d -> p (a d)", p=P),
                             zeros[:]).then_inc(s_zero, 16)

            def stacks(b, g, q=True, kv=True):
                wait(sp, s_pv, (b - 1) * BLK + (g + 1) * HG * SLOTS)
                if kv:
                    wait(sp, s_kd, 16 * NP * (b + 1))
                    for c in range(NP):
                        sp.dma_start(ks[c * NP * HD:(c + 1) * NP * HD, g * HG:(g + 1) * HG, :]
                                     .rearrange("r h t -> r (h t)"),
                                     d_k[bass.ds(b, 1), :, :, g * HG:(g + 1) * HG, :]
                                     .rearrange("o a d h t -> (o a d) (h t)")).then_inc(s_kl[g], 16)
                    for n in (2, 3):
                        wait_read(sp, b, "vp", n)
                    sp.dma_start(vb[:, g].rearrange("p t h e -> p (t h e)"),
                                 vst[:, g].rearrange("p t h e -> p (t h e)")).then_inc(s_vl[g], 16)
                if q:
                    wait(sp, s_qd, 16 * NP * NP * (b + 1))
                    sp.dma_start(qs[0:KR, g * HG:(g + 1) * HG, :].rearrange("r h s -> r (h s)"),
                                 d_q[bass.ds(b, 1), :, :, :, g * HG:(g + 1) * HG, :]
                                 .rearrange("o c a d h s -> (o c a d) (h s)")).then_inc(s_ql[g], 16)

            def side(b, s, k):
                if (s, k) == (0, 0):
                    wait(sp, s_mv1, b)
                    sp.dma_start(xin[:], x[bass.ds(b, 1)].rearrange("o (t p) d -> p (o t) d", p=P)
                                 ).then_inc(s_x, 16)
                    for n in (2, 3):
                        wait_full(sp, b - 1, "ctxT", n)
                    sp.dma_start(ctxs[:, 0:TT - 1, :], ctx_in[bass.ds(b, 1), 0:(TT - 1) * P, :]
                                 .rearrange("o (t p) d -> p (o t) d", p=P)).then_inc(s_ctx, 16)
                    sp.dma_start(ctxs[:, TT - 1, :], ctx_in[bass.ds(b, 1), LAST0:TK, :]
                                 .rearrange("o p d -> (o p) d")).then_inc(s_ctx, 16)
                if (s, k) == (1, 0):
                    wait(sp, s_sqd, 16 * (NP * NP + NP) * (b + 1))
                    for arg in (H - 2, H - 1):
                        wait_full(sp, b - 1, "sc", arg)
                    sp.dma_start(sq[:].rearrange("r h s -> r (h s)"),
                                 d_sq[bass.ds(b, 1)].rearrange("o c a d h s -> (o c a d) (h s)")
                                 ).then_inc(s_sst, 16)
                    for c in range(NP):
                        sp.dma_start(sk[c * NP * HD:(c + 1) * NP * HD].rearrange("r h s -> r (h s)"),
                                     d_sk[bass.ds(b, 1)].rearrange("o a d h s -> (o a d) (h s)")
                                     ).then_inc(s_sst, 16)
                for g in range(G):
                    for st in range(ST):
                        if (s, k) == ((2 + g, 3), (3 + g, 0))[st]:
                            for n in (2, 3):
                                wait_read(sp, b, "qe", g * 8 + st * HG + n)
                            wait(sp, s_bias[g % 2][st], 16 * (2 * (b - 1) + g // 2 + 1))
                            sp.dma_start(d_rel[g, st], qe[:, st]).then_inc(s_rel[g % 2][st], 16)
                    if (s, k) == ((3, 1), (4, 1), (6, 1), (8, 1))[g]:
                        wait(sp, s_z, ST * (H * b + HG * (g - 1)))
                        for st in range(ST):
                            wait(sp, s_rel[g % 2][st], 16 * (2 * b + g // 2 + 1))
                            sp.dma_start(bias[:, g % 2, st],
                                         bass.AP(tensor=d_rel.tensor, offset=(g * ST + st) * P * HG * RW + P,
                                                 ap=[[HG * RW - 1, P], [RW, HG], [1, S]])
                                         ).then_inc(s_bias[g % 2][st], 16)
                if k == SLOTS - 1:
                    if s == 11:
                        stacks(b, 0, q=False)
                    if s == 13:
                        stacks(b, 1, q=False)
                    if s == 15:
                        stacks(b, 0, kv=False)
                        stacks(b, 1, kv=False)

            def maxima(b, s, k):
                if (s, k) == (1, SLOTS - 1):
                    stacks(b, 2)
                if (s, k) == (5, SLOTS - 1):
                    stacks(b, 3)
                if k == 4 and s in (HG, 2 * HG, 3 * HG):
                    rows(b, s // HG - 1)

            def finish(b, s, k):
                if (s, k) == (0, 4):
                    rows(b, G - 1)

            def rows(b, g):
                wait(sp, s_md, 16 * (G * b + g + 1))
                sp.dma_start(qs[KR:KM, g * HG:(g + 1) * HG, :].rearrange("r h s -> r (h s)"),
                             d_m[bass.ds(b, 1), :, g * HG:(g + 1) * HG]
                             .rearrange("o c h t s -> (o c) (h t s)")).then_inc(s_ml[g], 16)

            run(sp, maxima, nothing, finish, side, nothing)

            wait(sp, s_pv, B * BLK)
            def experts(e2):
                for i in range(2):
                    e = e2 * 2 + i
                    wait(sp, s_eow, e)
                    sp.dma_start(w1s[:, i, :], w1[bass.ds(e, 1)].rearrange("o d f -> (o d) f")
                                 ).then_inc(s_ew[i], 16)
                    sp.dma_start(w2s[:, i], w2[bass.ds(e, 1)].rearrange("o (t p) d -> p (o t) d", p=P)
                                 ).then_inc(s_ew[i], 16)
                    wait(sp, s_sct, 16 * NTOK)
                    for r in range(NR):
                        n = min(P, CAP - r * P)
                        sp.dma_start(ein[0:n, i, r, :], d_disp[bass.ds(e * CAP + r * P, n), :]
                                     ).then_inc(s_ew[i], 16)
                    wait(sp, s_eo, 2 * (e + 1))
                    for r in range(NR):
                        n = min(P, CAP - r * P)
                        sp.dma_start(d_eout[bass.ds(e * CAP + r * P, n), :], eo[0:n, i, r, :]
                                     ).then_inc(s_es, 16)

            experts(0)
            with sp.Fori(1, E // 2) as e2:
                experts(e2)
            for j in range(0, NTOK, 4):
                wait(sp, s_res, j // 4 + 1)
                sp.dma_start(out.rearrange("b (t p) d -> p (b t) d", p=P)[:, j:j + 4, :],
                             comb[:, j:j + 4, :]).then_inc(s_out, 16)
            wait(sp, s_out, 16 * NTOK // 4)

        @block.gpsimd
        def _(pool):
            nc.gpsimd.memset(ident[:], 0.0).then_inc(s_const, 1)
            nc.gpsimd.memset(upper[:], 1.0).then_inc(s_const, 1)
            nc.gpsimd.memset(vmask[:], 1.0).then_inc(s_const, 1)
            nc.gpsimd.memset(zeros[:], 0.0).then_inc(s_const, 1)
            nc.gpsimd.iota(rank[:], pattern=[[-1, E]], base=E, channel_multiplier=0,
                           allow_small_or_imprecise_dtypes=True).then_inc(s_const, 1)
            wait(pool, s_const, 5)
            nc.gpsimd.affine_select(out=ident[:], in_=ident[:], compare_op=ALU.not_equal, fill=1.0, base=0,
                                    pattern=[[-1, P]], channel_multiplier=1).then_inc(s_const, 1)
            nc.gpsimd.affine_select(out=upper[:], in_=upper[:], compare_op=ALU.is_ge, fill=0.0, base=0,
                                    pattern=[[1, P]], channel_multiplier=-1).then_inc(s_const, 1)
            nc.gpsimd.affine_select(out=vmask[:], in_=vmask[:], compare_op=ALU.is_ge, fill=0.0, base=-OVER,
                                    pattern=[[0, 1]], channel_multiplier=1).then_inc(s_const, 1)
            nc.gpsimd.memset(minus_half[:], -0.5)
            nc.gpsimd.memset(ones_bf[:], 1.0).then_inc(s_const, 1)

            def deviation(n, mv, rs, step, done):
                nc.gpsimd.tensor_scalar(rs, mv, EPS, None, ALU.add).then_inc(step, 1)
                wait(pool, step, n + 1)
                nc.gpsimd.tensor_tensor(rs, rs, minus_half[:, 0:rs.shape[1]], ALU.pow).then_inc(done, 1)

            def split(b, src, tmp, part, steps):
                steps.link(b, nc.gpsimd.tensor_copy(part(0), src))
                steps.link(b, nc.gpsimd.tensor_tensor(tmp, src, part(0), ALU.subtract))
                steps.link(b, nc.gpsimd.tensor_copy(part(1), tmp))
                steps.link(b, nc.gpsimd.tensor_tensor(part(2), tmp, part(1), ALU.subtract))

            esteps = Steps(pool, s_ep, NPC)
            wait(pool, s_etab, 6)
            split(0, etab[:], etmp[:], lambda a: epart[:, a, :], esteps)
            self_steps, q_steps = Steps(pool, s_sqp, NPC), Steps(pool, s_qp, NPC)
            k_steps, m_steps = Steps(pool, s_kp, NPC), Steps(pool, s_mp, NPC)

            def side(b, s, k):
                if (s, k) == (0, 5):
                    wait_read(pool, b, "qk")
                    wait(pool, s_sqd, 16 * (NP * NP + NP) * b)
                    split(b, qk32[:], tmp32[:, 0:2 * S], lambda a: qkp[:, a, :], self_steps)
                    for c in range(NP):
                        for a in range(NP):
                            pool.dma_start(d_sq[bass.ds(b, 1), c, a].rearrange("o d h s -> h (o d) s"),
                                           qkp[:, c, 0:S]).then_inc(s_sqd, 16)
                        pool.dma_start(d_sk[bass.ds(b, 1), c].rearrange("o d h s -> h (o d) s"),
                                       qkp[:, c, S:2 * S]).then_inc(s_sqd, 16)
                if (s, k) == (8, 1):
                    for n in (2, 3):
                        wait_read(pool, b, "kp", n)
                    wait(pool, s_kd, 16 * NP * b)
                    split(b, k32[:], tmp32[:], lambda a: kp[:, a, :], k_steps)
                    for c in range(NP):
                        pool.dma_start(d_k[bass.ds(b, 1), c].rearrange("o d h t -> h (o d) t"),
                                       kp[:, c, :]).then_inc(s_kd, 16)
                if (s, k) == (12, 5):
                    wait(pool, s_mv1, b + 1)
                    deviation(b, mv1[:, :, 1], rs1[:], s_rch[0], s_rs1)
                if (s, k) == (13, 3):
                    wait_read(pool, b, "cq")
                    wait(pool, s_qd, 16 * NP * NP * b)
                    split(b, q32[:], tmp32[:, 0:S], lambda a: qp[:, a, :], q_steps)
                    for c in range(NP):
                        for a in range(NP):
                            pool.dma_start(d_q[bass.ds(b, 1), c, a].rearrange("o d h s -> h (o d) s"),
                                           qp[:, c, :]).then_inc(s_qd, 16)
                    wait(pool, s_x1, 1 * (b + 1))
                    nc.gpsimd.tensor_copy(xall[:, bass.ds(b * ST, ST), :], x1[:]).then_inc(s_x1c, 1)

            def maxt(b, g):
                wait(pool, s_m32, G * b + g + 1)
                wait(pool, s_md, 16 * (G * b + g))
                split(G * b + g, m32[:], mt[:], lambda a: mp[:, a, :], m_steps)
                pool.dma_start(d_m[bass.ds(b, 1), :, g * HG:(g + 1) * HG].rearrange("o c h t s -> (h t) (o c) s"),
                               mp[:]).then_inc(s_md, 16)

            def finish(b, s, k):
                if (s, k) == (6, 6):
                    wait(pool, s_mv2, b + 1)
                    deviation(b, mv2[:, :, 1], rs2[:], s_rch[1], s_rs2)
                if (s, k) == (10, 4):
                    wait(pool, s_disp, b + 1)
                    wait(pool, s_zero, 16 * (E * CAP // (5 * P)))
                    for st in range(ST):
                        nc.gpsimd.indirect_dma_start(
                            out=d_disp, out_offset=bass.IndirectOffsetOnAxis(ap=slot_i[:, st:st + 1], axis=0),
                            in_=x2[:, st, :], in_offset=None, bounds_check=E * CAP - 1,
                            oob_is_err=False).then_inc(s_sct, 16)
                    nc.gpsimd.tensor_copy(xall[:, bass.ds(b * ST, ST), :], x2[:])
                    nc.gpsimd.tensor_copy(slots[:, bass.ds(b * ST, ST)], slot_i[:])
                    nc.gpsimd.tensor_copy(fac[:, bass.ds(b * ST, ST)], fac1[:]).then_inc(s_x2c, 1)
                    wait(pool, s_sct, 16 * ST * (b + 1))

            run(pool, nothing, nothing, finish, side, maxt)

            wait(pool, s_x2c, B)
            wait(pool, s_pv, B * BLK)
            nc.gpsimd.tensor_copy(comb[:].rearrange("p t d -> p (t d)"),
                                  xall[:].rearrange("p t d -> p (t d)")).then_inc(s_cc, 1)
            wait(pool, s_cc, 1)
            wait(pool, s_es, 16 * NR * E)
            for j in range(NTOK):
                nc.gpsimd.indirect_dma_start(
                    out=comb[:, j, :], out_offset=None, in_=d_eout,
                    in_offset=bass.IndirectOffsetOnAxis(ap=slots[:, j:j + 1], axis=0),
                    bounds_check=E * CAP - 1, oob_is_err=False).then_inc(s_g, 16)
            wait(pool, s_g, 16 * NTOK)
            for n in range(NTOK // 4):
                wait(pool, s_mv3, n + 1)
                deviation(n, mv3[:, 4 * n:4 * n + 4, 1], rs3[:, 4 * n:4 * n + 4], s_rch[2], s_rs3)

        @block.scalar
        def _(act):
            for w in range(2):
                act.wait_ge(s_wt, w + 1)
                nc.scalar.copy(wT[:, 4 * w:4 * w + 4, :].rearrange("p w d -> p (w d)"),
                               banks[w][:, :]).then_inc(s_wtc, 1)

            def keep(b, name, arg, dst, n):
                bank, read = wait_full(act, b, name, arg)
                nc.scalar.copy(dst, bank[:, 0:n]).then_inc(read, 1)

            def side(b, s, k):
                for name, arg in slot_uses.get((s, k), ()):
                    if name == "xT":
                        keep(b, name, arg, xT[:], S)
                    if name == "qk":
                        keep(b, name, arg, qk32[:], 2 * S)
                    if name == "ctxT":
                        bank, read = wait_full(act, b, name, arg)
                        if arg < 3:
                            nc.scalar.copy(ctxT[:, arg * 4 * P:(arg + 1) * 4 * P], bank[:, :]).then_inc(read, 1)
                        else:
                            nc.scalar.copy(ctxT[:, (TT - 1) * P:TK], bank[:, OVER:P]).then_inc(read, 1)
                    if name == "kp":
                        keep(b, name, arg, k32[:, C0[arg]:C0[arg + 1]], C0[arg + 1] - C0[arg])
                    if name == "qe":
                        g, st, n = arg // 8, arg % 8 // HG, arg % HG
                        if n == 0:
                            wait(act, s_rel[(g - 1) % 2][st], 16 * (2 * b + (g - 1) // 2 + 1))
                        keep(b, name, arg, qe[:, st, n * RW:(n + 1) * RW], RW)
                    if name == "oT":
                        keep(b, name, arg, soT[:, arg, :], P)
                    if name == "x1T":
                        keep(b, name, arg, x1T[:], S)
                    if name == "cq":
                        keep(b, name, arg, q32[:], S)
                if 4 <= s <= 11 and k in (3, 4):
                    h = 2 * (s - 4) + k - 3
                    act.wait_ge(s_nb, H * b + h + 1)
                    for st in range(ST):
                        nc.scalar.activation(zp[:, h % 2, st, :], zp[:, h % 2, st, :], ACT.Exp,
                                             bias=snb[:, h, st:st + 1], scale=SCALE).then_inc(s_sp, 1)

            def attend(b, h, k):
                n = b * BLK + h * SLOTS + k
                w = S * min(2, TT - 2 * k)
                act.wait_ge(s_l2, n + 1)
                wait(act, s_pv, n - 1)
                i = h * SLOTS + k
                nc.scalar.activation(pr[:, i % 2, 0:w], b_sc[i % 2][:, 0:w], ACT.Exp,
                                     scale=SCALE).then_inc(s_pr, 1)

            def maxt(b, g):
                act.wait_ge(s_mT, G * b + g + 1)
                wait(act, s_mp, NPC * (G * b + g))
                nc.scalar.copy(m32[:], b_fin[0:HG * ST, 0:P]).then_inc(s_m32, 1)

            def finish(b, s, k):
                if (s, k) == (6, 3):
                    act.wait_ge(s_fw, NF * b + 1)
                    nc.scalar.copy(oT[:], b_fin[:, 0:S]).then_inc(s_fr, 1)
                if (s, k) == (8, 2):
                    act.wait_ge(s_fw, NF * b + 3)
                    nc.scalar.copy(x2T[:], b_fin[:, 0:S]).then_inc(s_fr, 1)
                if (s, k) == (8, 6):
                    act.wait_ge(s_fr, NF * b + 4)
                    nc.scalar.activation(pe_[:], pe_[:], ACT.Exp).then_inc(s_le, 1)

            run(act, nothing, attend, finish, side, maxt)

            def experts(e2):
                for i in range(2):
                    e = e2 * 2 + i
                    act.wait_ge(s_et, e + 1)
                    nc.scalar.copy(einT[:, i, :], banks[0][:, 0:CAP]).then_inc(s_etc, 1)
                    for f in range(0, FT, 2):
                        act.wait_ge(s_eh, e * FT + f + 1)
                        nc.scalar.activation(hT[:, i, f, :], banks[1 + f][:, 0:CAP], ACT.Relu).then_inc(s_ehs, 1)

            experts(0)
            with act.Fori(1, E // 2) as e2:
                experts(e2)
        @block.vector
        def _(dve):
            dch, fch = Steps(dve, s_dch, NDC, alone=True), Steps(dve, s_fch, NFC, alone=True)
            dve.wait_ge(s_const, NCONST)
            nc.vector.memset(ks[64:KM, :, :], 1.0)
            nc.vector.memset(k32[:, TK:TP], 0.0)
            nc.vector.memset(acc[:], 0.0)
            nc.vector.memset(sv[:, :, :, HD], 1.0)
            nc.vector.memset(vst[:, :, :, :, HD], 1.0).then_inc(s_etab, 1)
            dve.wait_ge(s_etab, 1)
            nc.vector.tensor_scalar(vst[:, :, TT - 1, :, HD],
                                    vst[:, :, TT - 1, :, HD],
                                    vmask[:, 0:1], None, ALU.mult).then_inc(s_etab, 1)
            dve.wait_ge(s_wt, 3)
            pT_neg, pT_pos = banks[2][0:HD, P:2 * P], banks[2][0:HD, 0:P]
            nc.vector.tensor_scalar(etab[:, P:2 * P], pT_neg, 2.0, None, ALU.mult).then_inc(s_etab, 1)
            nc.vector.tensor_scalar(etab[:, 2 * P:3 * P], pT_pos, 2.0, None, ALU.mult).then_inc(s_etab, 1)
            dve.wait_ge(s_etab, 4)
            nc.vector.tensor_copy(etab[:, 0:P], etab[:, P:P + 1].to_broadcast([HD, P])).then_inc(s_etab, 1)
            nc.vector.tensor_copy(etab[:, 3 * P:4 * P],
                                  etab[:, 3 * P - 1:3 * P].to_broadcast([HD, P])).then_inc(s_etab, 1)

            def moments(b, steps, y, stats, mv, done, tiles):
                for t in tiles:
                    last = nc.vector.bn_stats(stats[:, t, :], y[:, t, :])
                steps.link(b, last)
                for t in tiles:
                    last = nc.vector.bn_aggr(mv[:, t, :], stats[:, t, :])
                last.then_inc(done, 1)

            def normalize(y, mv, rs, dst, tiles):
                for t in tiles:
                    last = nc.vector.tensor_scalar(dst[:, t, :], y[:, t, :], mv[:, t, 0:1], rs[:, t:t + 1],
                                                   ALU.subtract, ALU.mult)
                return last

            def side(b, s, k):
                for name, arg in slot_uses.get((s, k), ()):
                    if name == "v":
                        bank, read = wait_full(dve, b, name, arg)
                        nc.vector.tensor_copy(sv[:, :, :, 0:HD],
                                              bank[:, 0:ST * D].rearrange("p (t h d) -> p t h d", t=ST, h=H)
                                              ).then_inc(read, 1)
                    if name == "vp":
                        wait(dve, s_vl[G - 1], 16 * b)
                        bank, read = wait_full(dve, b, name, arg)
                        for t in range(4 * arg, min(4 * arg + 4, TT)):
                            src = bank[:, (t % 4) * D:(t % 4 + 1) * D].rearrange("p (g h d) -> p g h d", g=G, h=HG)
                            if t < TT - 1:
                                last = nc.vector.tensor_copy(vst[:, :, t, :, 0:HD], src)
                            else:
                                last = nc.vector.tensor_scalar(vst[:, :, t, :, 0:HD], src, vmask[:, 0:1], None,
                                                               ALU.mult)
                        last.then_inc(read, 1)
                    if name == "sc":
                        h, g = arg, arg // HG
                        bank, _ = wait_full(dve, b, name, arg)
                        if h >= 2:
                            wait_full(dve, b, "pt", h - 2)
                        wait_alone(dve, s_bias[g % 2][0], 16 * (2 * b + g // 2 + 1))
                        for st in range(ST):
                            if h % HG == 0:
                                wait_alone(dve, s_bias[g % 2][st], 16 * (2 * b + g // 2 + 1))
                            nc.vector.tensor_tensor_reduce(
                                out=zp[:, h % 2, st, :], in0=bank[:, st * S:(st + 1) * S],
                                in1=bias[:, g % 2, st, h % HG, :], scale=1.0, scalar=NEG, op0=ALU.add,
                                op1=ALU.max, accum_out=smx[:, h, st:st + 1]).then_inc(s_z, 1)
                        dve.wait_ge(s_z, ST * (H * b + h + 1))
                        nc.vector.tensor_scalar(snb[:, h, :], smx[:, h, :], -SCALE, None, ALU.mult).then_inc(s_nb, 1)
                    if name == "pt":
                        bank, read = wait_full(dve, b, name, arg)
                        if arg >= 2:
                            wait_full(dve, b, "pv", arg // 2 - 1)
                        nc.vector.tensor_copy(pT[:, arg % 2, :], bank[:, :]).then_inc(read, 1)
                    if name == "pv":
                        bank, read = wait_full(dve, b, name, arg)
                        nc.vector.tensor_copy(soraw[:, 2 * arg:2 * arg + 2].rearrange("p h t e -> p (h t e)"),
                                              bank[:, 0:2 * ST * V1]).then_inc(read, 1)
                        if arg == H // 2 - 1:
                            wait_read(dve, b, "pv", arg)
                            dch.link(b, nc.vector.reciprocal(srec[:], soraw[:, :, :, HD]))
                            nc.vector.tensor_tensor(so[:].rearrange("p t h d -> p h t d"), soraw[:, :, :, 0:HD],
                                                    srec[:].unsqueeze(3).to_broadcast([P, H, ST, HD]),
                                                    ALU.mult).then_inc(s_so, 1)
                    if name == "wp":
                        bank, read = wait_full(dve, b, name, arg)
                        nc.vector.tensor_tensor(y1[:].rearrange("p t d -> p (t d)"), bank[:, 0:ST * D],
                                                xin[:].rearrange("p t d -> p (t d)"), ALU.add).then_inc(read, 1)
                        wait_read(dve, b, "wp")
                        moments(b, dch, y1, st1, mv1, s_mv1, range(ST))
                if (s, k) == (12, 6):
                    dve.wait_ge(s_rs1, b + 1)
                    wait(dve, s_x1c, b)
                    normalize(y1, mv1, rs1, x1, range(ST)).then_inc(s_x1, 1)

            def maxima(b, h, k):
                for i in ((k,) if k < SLOTS - 1 else (k, k + 1)):
                    st, c = i // NCH, i % NCH
                    dve.wait_ge(s_l1, NL1 * b + 8 * h + i + 1)
                    nc.vector.tensor_reduce(mx4[:, h, st, c:c + 1], b_mx[i % 2][:, 0:C0[c + 1] - C0[c]], AX,
                                            ALU.max).then_inc(s_l1r, 1)
                if k == SLOTS - 1 and h % HG == HG - 1:
                    g = h // HG
                    dve.wait_ge(s_l1r, NL1 * b + 8 * h + 8)
                    nc.vector.tensor_reduce(nmx[:, g * HG:(g + 1) * HG, :], mx4[:, g * HG:(g + 1) * HG], AX,
                                            ALU.max, negate=True).then_inc(s_nm, 1)

            def finish(b, s, k):
                if (s, k) == (6, 0):
                    dve.wait_ge(s_pv, BLK * (b + 1))
                    raw = b_o[:, 0:ST * H * V1].rearrange("p (t h e) -> p t h e", t=ST, h=H)
                    fch.link(b, nc.vector.reciprocal(orec[:], raw[:, :, :, HD]))
                    nc.vector.tensor_tensor(o[:], raw[:, :, :, 0:HD],
                                            orec[:].unsqueeze(3).to_broadcast([P, ST, H, HD]),
                                            ALU.mult).then_inc(s_or, 1)
                if (s, k) == (6, 6):
                    dve.wait_ge(s_fw, NF * b + 2)
                    dve.wait_ge(s_x1c, b + 1)
                    nc.vector.tensor_tensor(y2[:], b_fin[:, 0:ST * D].rearrange("p (t d) -> p t d", t=ST),
                                            xall[:, bass.ds(b * ST, ST), :], ALU.add).then_inc(s_fr, 1)
                    dve.wait_ge(s_fr, NF * b + 2)
                    moments(b, fch, y2, st2, mv2, s_mv2, range(ST))
                if (s, k) == (7, 1):
                    dve.wait_ge(s_rs2, b + 1)
                    normalize(y2, mv2, rs2, x2, range(ST)).then_inc(s_x2, 1)
                if (s, k) == (8, 5):
                    dve.wait_ge(s_fw, NF * b + 4)
                    logits = b_fin[:, 0:ST * E].rearrange("p (t e) -> p t e", t=ST)
                    fch.link(b, nc.vector.tensor_reduce(lmx[:], logits, AX, ALU.max))
                    nc.vector.tensor_tensor(pe_[:], logits, lmx[:].unsqueeze(2).to_broadcast([P, ST, E]),
                                            ALU.subtract).then_inc(s_fr, 1)
                if (s, k) == (9, 1):
                    dve.wait_ge(s_le, b + 1)
                    nc.vector.tensor_reduce(pmx[:], pe_[:], AX, ALU.max)
                    fch.link(b, nc.vector.tensor_reduce(psm[:], pe_[:], AX, ALU.add))
                    fch.link(b, nc.vector.tensor_tensor(oh[:], pe_[:], pmx[:].unsqueeze(2).to_broadcast([P, ST, E]),
                                                        ALU.is_equal))
                    fch.link(b, nc.vector.tensor_tensor(oh[:], oh[:],
                                                        rank[:].unsqueeze(1).to_broadcast([P, ST, E]), ALU.mult))
                    nc.vector.reciprocal(psm[:], psm[:])
                    fch.link(b, nc.vector.tensor_reduce(okk[:], oh[:], AX, ALU.max))
                    nc.vector.tensor_tensor(fac1[:], pmx[:], psm[:], ALU.mult)
                    nc.vector.tensor_tensor(ohb[:], oh[:], okk[:].unsqueeze(2).to_broadcast([P, ST, E]),
                                            ALU.is_equal).then_inc(s_oh, 1)
                if (s, k) == (10, 2):
                    dve.wait_ge(s_fw, NF * b + 5)
                    nc.vector.tensor_tensor(cum[:], b_fin[:, 0:ST * E].rearrange("p (t e) -> p t e", t=ST), ohb[:],
                                            ALU.mult).then_inc(s_fr, 1)
                    dve.wait_ge(s_fr, NF * b + 5)
                    nc.vector.tensor_reduce(pos[:], cum[:], AX, ALU.add)
                    fch.link(b, nc.vector.tensor_tensor(acc[:, 0], acc[:, 0], ohb[:, 0, :], ALU.add))
                    nc.vector.tensor_scalar(kept[:], pos[:], float(CAP), None, ALU.is_le)
                    nc.vector.tensor_scalar(base[:], okk[:], -float(CAP), float(E * CAP - 1), ALU.mult, ALU.add)
                    fch.link(b, nc.vector.tensor_tensor(acc[:, 0], acc[:, 0], ohb[:, 1, :], ALU.add))
                    nc.vector.tensor_tensor(base[:], base[:], pos[:], ALU.add)
                    fch.link(b, nc.vector.tensor_scalar(koff[:], kept[:], -OOB, OOB, ALU.mult, ALU.add))
                    nc.vector.tensor_scalar(fac1[:], fac1[:], -1.0, None, ALU.add)
                    fch.link(b, nc.vector.tensor_tensor(slot_i[:], base[:], koff[:], ALU.add))
                    fch.link(b, nc.vector.tensor_tensor(fac1[:], fac1[:], kept[:], ALU.mult))
                    nc.vector.tensor_scalar(fac1[:], fac1[:], 1.0, None, ALU.add).then_inc(s_disp, 1)

            run(dve, maxima, nothing, finish, side, nothing)

            def experts(e2):
                for i in range(2):
                    e = e2 * 2 + i
                    for f in range(1, FT, 2):
                        dve.wait_ge(s_eh, e * FT + f + 1)
                        nc.vector.tensor_scalar(hT[:, i, f, :], banks[1 + f][:, 0:CAP], 0.0, None,
                                                ALU.max).then_inc(s_ehv, 1)
                    dve.wait_ge(s_eow, e + 1)
                    full = CAP // P
                    nc.vector.tensor_copy(eo[:, i, 0:full, :],
                                          banks[5 + i][:, 0:full * D].rearrange("p (t d) -> p t d", t=full)
                                          ).then_inc(s_eo, 1)
                    n = CAP - full * P
                    nc.vector.tensor_copy(eo[0:n, i, full, :], banks[5 + i][0:n, full * D:(full + 1) * D]
                                          ).then_inc(s_eo, 1)

            experts(0)
            with dve.Fori(1, E // 2) as e2:
                experts(e2)
            cch = Steps(dve, s_cch, 2)
            for n in range(NTOK // 4):
                tiles = range(4 * n, 4 * n + 4)
                dve.wait_ge(s_g, 16 * NTOK)
                for t in tiles:
                    last = nc.vector.scalar_tensor_tensor(comb[:, t, :], comb[:, t, :], fac[:, t:t + 1],
                                                          xall[:, t, :], ALU.mult, ALU.add)
                cch.link(n, last)
                moments(n, cch, comb, st3, mv3, s_mv3, tiles)
            for n in range(NTOK // 4):
                dve.wait_ge(s_rs3, n + 1)
                normalize(comb, mv3, rs3, comb, range(4 * n, 4 * n + 4)).then_inc(s_res, 1)

        @block.tensor
        def _(pe):
            pe.wait_ge(s_const, NCONST)
            pe.wait_ge(s_win, 16 * 10)
            for w in range(8):
                last = nc.tensor.transpose(banks[w // 4][:, (w % 4) * D:(w % 4 + 1) * D], wraw[:, w, :], ident[:])
                if w % 4 == 3:
                    last.then_inc(s_wt, 1)
            for r in range(2):
                last = nc.tensor.transpose(banks[2][0:HD, r * P:(r + 1) * P], posr[:, r, :], ident[:])
            last.then_inc(s_wt, 1)
            pe.wait_ge(s_wtc, 2)
            pe.wait_ge(s_etab, 6)

            def mm(dst, lhsT, rhs, start=True, stop=True, shared=False):
                return nc.tensor.matmul(dst, lhsT, rhs, start=start, stop=stop, skip_group_check=shared)

            def product(b, name, arg):
                if name == "xT":
                    pe.wait_ge(s_x, 16 * (b + 1))
                if name == "ctxT" and arg == 0:
                    pe.wait_ge(s_ctx, 32 * (b + 1))
                if name == "qk":
                    wait_read(pe, b, "xT")
                if name == "kp" and arg == 0:
                    for n in (2, 3):
                        wait_read(pe, b, "ctxT", n)
                if name == "qe" and arg == 0:
                    pe.wait_ge(s_sst, 16 * (1 + NP) * (b + 1))
                    pe.wait_ge(s_est, 16 * NP)
                if name == "pt":
                    pe.wait_ge(s_sp, ST * (H * b + arg + 1))
                if name == "pv":
                    for n in (0, 1):
                        wait_read(pe, b, "pt", 2 * arg + n)
                    if arg == 0:
                        wait_read(pe, b, "v")
                if name == "oT":
                    pe.wait_ge(s_so, b + 1)
                if name == "wp":
                    for n in (0, 1):
                        wait_read(pe, b, "oT", n)
                if name == "x1T":
                    pe.wait_ge(s_x1, b + 1)
                if name == "cq":
                    wait_read(pe, b, "x1T")
                bank, full = wait_free(pe, b, name, arg)
                if name == "xT":
                    for st in range(ST):
                        last = nc.tensor.transpose(bank[:, st * P:(st + 1) * P], xin[:, st, :], ident[:])
                if name == "qk":
                    for i, w in enumerate((WQ, WK)):
                        last = mm(bank[:, i * S:(i + 1) * S], wT[:, w, :], xT[:])
                if name == "v":
                    for st in range(ST):
                        last = mm(bank[:, st * D:(st + 1) * D], xT[:, st * P:(st + 1) * P], wT[:, WV, :])
                if name == "ctxT":
                    for t in range(4 * arg, min(4 * arg + 4, TT)):
                        last = nc.tensor.transpose(bank[:, (t % 4) * P:(t % 4 + 1) * P], ctxs[:, t, :], ident[:])
                if name == "kp":
                    last = mm(bank[:, 0:C0[arg + 1] - C0[arg]], wT[:, XK, :], ctxT[:, C0[arg]:C0[arg + 1]])
                if name == "vp":
                    for t in range(4 * arg, min(4 * arg + 4, TT)):
                        t0 = t * P if t < TT - 1 else LAST0
                        last = mm(bank[:, (t % 4) * D:(t % 4 + 1) * D], ctxT[:, t0:t0 + P], wT[:, XV, :])
                if name == "qe":
                    g, st, n = arg // 8, arg % 8 // HG, arg % HG
                    e0 = (ST - 1 - st) * P
                    last = mm(bank[:, 0:RW], sq[:, g * HG + n, st * P:(st + 1) * P], estack[:, e0:e0 + RW])
                if name == "sc":
                    for st in range(ST):
                        last = mm(bank[:, st * S:(st + 1) * S], sq[:, arg, st * P:(st + 1) * P], sk[:, arg, :])
                if name == "pt":
                    for st in range(ST):
                        for jt in range(ST):
                            last = nc.tensor.transpose(bank[:, jt * S + st * P:jt * S + (st + 1) * P],
                                                       zp[:, arg % 2, st, jt * P:(jt + 1) * P], ident[:])
                if name == "pv":
                    for n in range(2):
                        for st in range(ST):
                            for jt in range(ST):
                                c = (n * ST + st) * V1
                                last = mm(bank[:, c:c + V1], pT[:, n, jt * S + st * P:jt * S + (st + 1) * P],
                                          sv[:, jt, 2 * arg + n, :], start=jt == 0, stop=jt == ST - 1)
                if name == "oT":
                    last = nc.tensor.transpose(bank[:, 0:P], so[:, arg].rearrange("p h d -> p (h d)"), ident[:])
                if name == "wp":
                    for st in range(ST):
                        last = mm(bank[:, st * D:(st + 1) * D], soT[:, st, :], wT[:, WP, :])
                if name == "x1T":
                    for st in range(ST):
                        last = nc.tensor.transpose(bank[:, st * P:(st + 1) * P], x1[:, st, :], ident[:])
                if name == "cq":
                    last = mm(bank[:, 0:S], wT[:, XQ, :], x1T[:])
                last.then_inc(full, 1)

            def side(b, s, k):
                for name, arg in slot_uses.get((s, k), ()):
                    product(b, name, arg)

            def maxima(b, h, k):
                if k == 0 and h % HG == 0:
                    g = h // HG
                    pe.wait_ge(s_kl[g], 16 * NP * (b + 1))
                    pe.wait_ge(s_ql[g], 16 * (b + 1))
                for i in ((k,) if k < SLOTS - 1 else (k, k + 1)):
                    st, c = i // NCH, i % NCH
                    wait(pe, s_l1r, NL1 * b + 8 * h + i - 1)
                    mm(b_mx[i % 2][:, 0:C0[c + 1] - C0[c]], qs[0:KR, h, st * P:(st + 1) * P],
                       ks[0:KR, h, C0[c]:C0[c + 1]]).then_inc(s_l1, 1)

            def maxt(b, g):
                pe.wait_ge(s_nm, G * b + g + 1)
                wait(pe, s_m32, G * b + g)
                if g in (1, 2):
                    wait(pe, s_fr, NF * (b - 1) + (2 if g == 1 else NF))
                nc.tensor.transpose(b_fin[0:HG * ST, 0:P],
                                    nmx[:, g * HG:(g + 1) * HG, :].rearrange("p h t -> p (h t)"),
                                    ident[:]).then_inc(s_mT, 1)

            def scores(b, h, k):
                n = b * BLK + h * SLOTS + k
                i, g = h * SLOTS + k, h // HG
                if k == 0 and h % HG == 0:
                    pe.wait_ge(s_ml[g], 16 * (b + 1))
                wait(pe, s_pr, n - 1)
                for t in range(2 * k, min(2 * k + 2, TT)):
                    t0 = t * P if t < TT - 1 else LAST0
                    last = mm(b_sc[i % 2][:, (t % 2) * S:(t % 2 + 1) * S], ks[:, h, t0:t0 + P], qs[:, h, :])
                last.then_inc(s_l2, 1)

            def attend(b, h, k):
                n = b * BLK + h * SLOTS + k
                i, g = h * SLOTS + k, h // HG
                if isinstance(b, int) and (b, h, k) == (0, 0, 0):
                    scores(b, h, k)
                if k < SLOTS - 1:
                    scores(b, h, k + 1)
                elif h < H - 1:
                    scores(b, h + 1, 0)
                elif not (isinstance(b, int) and b == B - 1):
                    scores(b + 1, 0, 0)
                if k == 0 and h == 0:
                    wait(pe, s_or, b)
                if k == 0 and h % HG == 0:
                    pe.wait_ge(s_vl[g], 16 * (b + 1))
                pe.wait_ge(s_pr, n + 1)
                for t in range(2 * k, min(2 * k + 2, TT)):
                    for st in range(ST):
                        c = (st * H + h) * V1
                        last = mm(b_o[:, c:c + V1], pr[:, i % 2, (t % 2) * S + st * P:(t % 2) * S + (st + 1) * P],
                                  vb[:, g, t, h % HG, :], start=t == 0 and st == 0, stop=t == TT - 1, shared=True)
                last.then_inc(s_pv, 1)

            def finish(b, s, k):
                def bank_free(j, maxima_done):
                    if j:
                        wait(pe, s_fr, NF * b + j)
                    if maxima_done is not None:
                        wait(pe, s_m32, maxima_done)
                if (s, k) == (6, 2):
                    pe.wait_ge(s_or, b + 1)
                    bank_free(0, last_maxt(b, 1))
                    for st in range(ST):
                        last = nc.tensor.transpose(b_fin[:, st * P:(st + 1) * P],
                                                   o[:, st].rearrange("p h d -> p (h d)"), ident[:])
                    last.then_inc(s_fw, 1)
                if (s, k) == (6, 5):
                    bank_free(1, None)
                    for st in range(ST):
                        last = mm(b_fin[:, st * D:(st + 1) * D], oT[:, st * P:(st + 1) * P], wT[:, XO, :])
                    last.then_inc(s_fw, 1)
                if (s, k) == (8, 1):
                    pe.wait_ge(s_x2, b + 1)
                    bank_free(2, last_maxt(b, 2))
                    for st in range(ST):
                        last = nc.tensor.transpose(b_fin[:, st * P:(st + 1) * P], x2[:, st, :], ident[:])
                    last.then_inc(s_fw, 1)
                if (s, k) == (8, 4):
                    bank_free(3, None)
                    for st in range(ST):
                        last = mm(b_fin[:, st * E:(st + 1) * E], x2T[:, st * P:(st + 1) * P], wr[:])
                    last.then_inc(s_fw, 1)
                if (s, k) == (10, 1):
                    pe.wait_ge(s_oh, b + 1)
                    bank_free(4, None)
                    mm(b_fin[:, 0:E], upper[:], ohb[:, 0, :], stop=False)
                    mm(b_fin[:, 0:E], ones_bf[:], acc[:, 0], start=False)
                    mm(b_fin[:, E:2 * E], upper[:], ohb[:, 1, :], stop=False)
                    mm(b_fin[:, E:2 * E], ones_bf[:], ohb[:, 0, :], start=False, stop=False)
                    mm(b_fin[:, E:2 * E], ones_bf[:], acc[:, 0], start=False).then_inc(s_fw, 1)

            def last_maxt(b, n):
                if isinstance(b, int) and b == B - 1:
                    return G * B
                return G * (b + 1) + n

            run(pe, maxima, attend, finish, side, maxt)

            def experts(e2):
                for i in range(2):
                    e = e2 * 2 + i
                    pe.wait_ge(s_ew[i], 16 * (2 + NR) * (e2 + 1))
                    wait(pe, s_etc, e)
                    for r in range(NR):
                        n = min(P, CAP - r * P)
                        last = nc.tensor.transpose(banks[0][:, r * P:r * P + n], ein[0:n, i, r, :], ident[0:n, 0:n])
                    last.then_inc(s_et, 1)
                    pe.wait_ge(s_etc, e + 1)
                    wait(pe, s_ehs, e * (FT // 2))
                    wait(pe, s_ehv, e * (FT // 2))
                    for f in range(FT):
                        mm(banks[1 + f][:, 0:CAP], w1s[:, i, f * P:(f + 1) * P], einT[:, i, :]).then_inc(s_eh, 1)
                    pe.wait_ge(s_ehs, (e + 1) * (FT // 2))
                    pe.wait_ge(s_ehv, (e + 1) * (FT // 2))
                    wait(pe, s_eo, 2 * e)
                    for r in range(NR):
                        n = min(P, CAP - r * P)
                        for f in range(FT):
                            last = mm(banks[5 + i][0:n, r * D:(r + 1) * D], hT[:, i, f, r * P:r * P + n],
                                      w2s[:, i, f, :], start=f == 0, stop=f == FT - 1)
                    last.then_inc(s_eow, 1)

            experts(0)
            with pe.Fori(1, E // 2) as e2:
                experts(e2)
_INS = ['x', 'ctx_1024', 'L0_attn_Wq', 'L0_attn_Wk', 'L0_attn_Wv', 'L0_attn_Wp', 'L0_attn_pos_emb_k',
        'L0_xattn_Wq', 'L0_xattn_Wk', 'L0_xattn_Wv', 'L0_xattn_Wo', 'L0_ffn_Wr', 'L0_ffn_W1', 'L0_ffn_W2']


def kernel(**inputs):
    import numpy as _np
    import concourse.bacc as _bacc
    from concourse import mybir as _mybir
    from concourse.bass_utils import run_bass_kernel_spmd as _run

    nc = _bacc.Bacc("TRN2", target_bir_lowering=False, num_devices=1)
    arrays, ap = {}, {}
    for name in _INS:
        a = _np.ascontiguousarray(inputs[name])
        arrays[f"in_{name}_dram"] = a
        ap[name] = nc.dram_tensor(f"in_{name}_dram", a.shape, _mybir.dt.from_np(a.dtype), kind="ExternalInput").ap()
    out = nc.dram_tensor("out_0_dram", inputs["x"].shape, _mybir.dt.float32, kind="ExternalOutput").ap()
    decoder_layer(nc, ap['x'], ap['ctx_1024'],
                  [ap[f'L0_attn_{n}'] for n in ('Wq', 'Wk', 'Wv', 'Wp')], ap['L0_attn_pos_emb_k'],
                  [ap[f'L0_xattn_{n}'] for n in ('Wq', 'Wk', 'Wv', 'Wo')],
                  ap['L0_ffn_Wr'], ap['L0_ffn_W1'], ap['L0_ffn_W2'], out)
    r = _run(nc, [arrays], core_ids=[0])
    return r.results[0]["out_0_dram"]
```

```python
import concourse.bass as bass
from concourse import mybir
from contextlib import ExitStack


def decoder_layer(nc, x, ctx_in, w_self, pos_emb, w_cross, w_router, w1, w2, out):
    f32, bf16, i32 = mybir.dt.float32, mybir.dt.bfloat16, mybir.dt.int32
    ALU = mybir.AluOpType
    ACT = mybir.ActivationFunctionType
    AX = mybir.AxisListType.X

    P = 128
    B, S, D = x.shape
    TK = ctx_in.shape[1]
    HD = pos_emb.shape[1]
    H = D // HD
    R = pos_emb.shape[0] // 2
    E, _, FF = w1.shape
    ST = S // P
    TT = -(-TK // P)
    LAST0 = TK - P
    OVER = (TT - 1) * P - LAST0
    TP = -(-TK // 4) * 4
    CAP = int(1.25 * B * S / E)
    SCALE = float(HD) ** -0.5
    EPS = 1e-5
    G = 4
    HG = H // G
    NP = 3
    KR = NP * NP * HD
    KM = KR + NP
    V1 = HD + 1
    LAG = 6
    SLOTS = -(-TT // 2)
    BLK = SLOTS * H
    NCH = 4
    C0 = [TK * c // NCH for c in range(NCH + 1)]
    NL1 = H * ST * NCH
    RW = 3 * P
    NEG = -3.0e38
    NTOK = B * ST
    OOB = 65536.0

    uses = []
    def use(s, k, name, arg=0):
        uses.append((s, k, name, arg))
    for s in range(16):
        for k in range(SLOTS):
            if s == 0 and k in (1, 3, 5):
                use(s, k, ("xT", "qk", "v")[k // 2])
            if s == 1 and 1 <= k <= 4:
                use(s, k, "ctxT", k - 1)
            if 5 <= s <= 12 and k == 0:
                use(s, k, "pv", s - 5)
            if 2 <= s <= 5:
                for n in ((0, 1) if k == 0 else (k + 1,)):
                    use(s, k, "qe", (s - 2) * 8 + n)
            if 4 <= s <= 11:
                if k in (1, 2):
                    use(s, k, "sc", 2 * (s - 4) + k - 1)
                if k in (4, 5):
                    use(s, k, "pt", 2 * (s - 4) + k - 4)
            if 6 <= s <= 9 and k in (3, 6):
                use(s, k, ("kp", "vp")[(s - 6) // 2], 2 * ((s - 6) % 2) + (k == 6))
            if s == 12 and k == 6:
                use(s, k, "wp")
            if s == 13 and k in (2, 4):
                use(s, k, ("x1T", "cq")[k // 2 - 1])
    NU = len(uses)
    assert NU % 2 == 0
    index = {(n, a): u for u, (_, _, n, a) in enumerate(uses)}
    slot_uses = {}
    for s, k, n, a in uses:
        slot_uses.setdefault((s, k), []).append((n, a))

    ctx = ExitStack()
    with ctx:
        def sb(name, shape, dt=f32):
            return ctx.enter_context(nc.sbuf_tensor(name, shape, dt))

        def sem(name):
            return ctx.enter_context(nc.semaphore(name))

        d_sq = nc.dram_tensor("d_sq", (B, NP, HD, H, S), bf16).ap()
        d_sk = nc.dram_tensor("d_sk", (B, NP, HD, H, S), bf16).ap()
        d_q = nc.dram_tensor("d_q", (B, NP, HD, H, S), bf16).ap()
        d_k = nc.dram_tensor("d_k", (B, NP, HD, H, TP), bf16).ap()
        d_m = nc.dram_tensor("d_m", (B, NP, H, ST, P), bf16).ap()
        d_e = nc.dram_tensor("d_e", (NP, HD, 4 * P), bf16).ap()
        d_rel = nc.dram_tensor("d_rel", (G, ST, P, HG * RW), f32).ap()
        d_so = nc.dram_tensor("d_so", (B, H, V1, S), f32).ap()
        d_o = nc.dram_tensor("d_o", (B, H, V1, S), f32).ap()
        d_disp = nc.dram_tensor("d_disp", (E * CAP, D), f32).ap()
        d_eout = nc.dram_tensor("d_eout", (E * CAP, D), f32).ap()

        ident = sb("ident", [P, P])
        ones_bf = sb("ones_bf", [P, P], bf16)
        upper = sb("upper", [P, P], bf16)
        vmask = sb("vmask", [P, 1])
        minus_half = sb("minus_half", [P, NTOK])
        rank = sb("rank", [P, E])
        bias_raw = sb("bias_raw", [P, 2 * ST * HG * S])
        bias = bias_raw[:].rearrange("p (a t h s) -> p a t h s", a=2, t=ST, h=HG)
        wraw = bias_raw[:, 0:8 * D].rearrange("p (w d) -> p w d", w=8)
        zeros = bias_raw[:, 8 * D:13 * D]
        etab = bias_raw[0:HD, 13 * D:17 * D]
        etmp = bias_raw[0:HD, 17 * D:21 * D]
        epart = bias_raw[0:HD, 21 * D:27 * D].bitcast(bf16).rearrange("p (c r) -> p c r", c=NP)
        wT = sb("wT", [P, 8, D])
        WQ, WK, WV, WP, XQ, XK, XV, XO = range(8)
        wr = sb("wr", [P, E])
        posr = sb("posr", [P, 2, HD])
        estack = sb("estack", [KR, 4 * P], bf16)
        xin = sb("xin", [P, ST, D])
        xT = sb("xT", [P, S])
        qk32 = sb("qk32", [P, 2 * S])
        sq = sb("sq", [KR, H, S], bf16)
        sk = sb("sk", [KR, H, S], bf16)
        sv = sb("sv", [P, ST, H, V1])
        qe = sb("qe", [P, ST, HG * RW])
        zp = sb("zp", [P, 2, ST, S])
        smx = sb("smx", [P, H, ST])
        snb = sb("snb", [P, H, ST])
        pT = sb("pT", [P, 2, 2 * S])
        soraw = sb("soraw", [V1, 2, 2, S])
        sonum = sb("sonum", [P, S])
        soden = sb("soden", [P, S])
        soT = sb("soT", [P, S])
        y1 = sb("y1", [P, ST, D])
        st1 = sb("st1", [P, ST, 6])
        mv1 = sb("mv1", [P, ST, 2])
        rs1 = sb("rs1", [P, ST])
        x1 = sb("x1", [P, ST, D])
        x1T = sb("x1T", [P, S])
        q32 = qk32[:, 0:S]
        ctxs = sb("ctxs", [P, TT, D])
        ctxT = sb("ctxT", [P, TK])
        k32 = sb("k32", [P, TP])
        tmp32 = sb("tmp32", [P, TP])
        kp = sb("kp", [P, NP, TP], bf16)
        qkp, qp = kp[:, :, 0:2 * S], kp[:, :, 0:S]
        vst = sb("vst", [P, G, TT, HG, V1])
        ks_raw = sb("ks_raw", [P, H * TP], bf16)
        ks = ks_raw[0:KM, :].rearrange("p (h t) -> p h t", h=H)
        qs = sb("qs", [KM, H, S], bf16)
        vb = sb("vb", [P, G, TT, HG, V1])
        mx4 = sb("mx4", [P, H, ST, NCH])
        nmx = sb("nmx", [P, H, ST])
        m32 = sb("m32", [HG * ST, P])
        mt = sb("mt", [HG * ST, P])
        mp = sb("mp", [HG * ST, NP, P], bf16)
        pr = sb("pr", [P, 2, 2 * S])
        oraw = sb("oraw", [V1, 2, 2, S])
        onum = sb("onum", [P, S])
        oden = sb("oden", [P, S])
        oT = sb("oT", [P, S])
        y2 = sb("y2", [P, ST, D])
        st2 = sb("st2", [P, ST, 6])
        mv2 = sb("mv2", [P, ST, 2])
        rs2 = sb("rs2", [P, ST])
        x2 = sb("x2", [P, ST, D])
        x2T = sb("x2T", [P, S])
        lmx = sb("lmx", [P, ST])
        pe_ = sb("pe_", [P, ST, E])
        pmx = sb("pmx", [P, ST])
        psm = sb("psm", [P, ST])
        oh = sb("oh", [P, ST, E])
        okk = sb("okk", [P, ST])
        ohb = sb("ohb", [P, ST, E], bf16)
        acc = sb("acc", [P, 2, E], bf16)
        cum = sb("cum", [P, ST, E])
        pos = sb("pos", [P, ST])
        kept = sb("kept", [P, ST])
        koff = sb("koff", [P, ST])
        fac1 = sb("fac1", [P, ST])
        base = sb("base", [P, ST])
        slot_i = sb("slot_i", [P, ST], i32)
        slots = sb("slots", [P, NTOK], i32)
        fac = sb("fac", [P, NTOK])
        xall = sb("xall", [P, NTOK, D])
        NR = -(-CAP // P)
        FT = FF // P
        ks32, over = ks_raw[:].bitcast(f32), [0]

        def later(*shape):
            n, at = 1, over[0]
            for d in shape:
                n *= d
            over[0] += n
            assert over[0] <= H * TP // 2
            names = "abc"[:len(shape)]
            return ks32[:, at:at + n].rearrange(f"p ({' '.join(names)}) -> p {' '.join(names)}",
                                                **dict(zip(names, shape)))

        w1s = later(2, FF)
        w2s = later(2, FT * D).rearrange("p i (f d) -> p i f d", f=FT)
        ein = later(2, NR, D)
        einT = later(2, CAP)
        hT = later(2, FT, CAP)
        eo = later(2, NR, D)
        comb = later(NTOK, D)
        st3 = sb("st3", [P, NTOK, 6])
        mv3 = sb("mv3", [P, NTOK, 2])
        rs3 = sb("rs3", [P, NTOK])

        banks = [ctx.enter_context(nc.psum_tensor(f"bank{i}", [P, 512], f32)) for i in range(8)]
        b_sc = banks[0:2]
        b_mx = banks[2:4]
        b_o = banks[4]
        b_side = banks[5:7]
        b_fin = banks[7]

        NET = 4
        NCONST = 9

        s_win = sem("weights_loaded")
        s_const = sem("constants_made")
        s_wt = sem("weights_transposed")
        s_wtc = sem("weight_transposes_kept")
        s_etab = sem("position_table_steps")
        s_ones = sem("ones_made")
        s_ep = sem("position_parts_steps")
        s_ed = sem("position_parts_stored")
        s_est = sem("position_stack_loaded")
        s_zero = sem("dispatch_zeroed")
        s_x = sem("x_loaded")
        s_ctx = sem("ctx_loaded")
        s_full = [sem("side_bank0_written"), sem("side_bank1_written")]
        s_read = [sem("side_bank0_read"), sem("side_bank1_read")]
        s_sqp = sem("self_parts_steps")
        s_sqd = sem("self_parts_stored")
        s_sst = sem("self_stacks_loaded")
        s_rel = [[sem(f"relative_scores_stored_{a}{c}") for c in range(ST)] for a in range(2)]
        s_bias = [[sem(f"bias_loaded_{a}{c}") for c in range(ST)] for a in range(2)]
        s_z = sem("self_scores_maxed")
        s_nb = sem("self_bias_ready")
        s_sp = sem("self_probs_ready")
        s_sod = [sem("self_outputs_stored_even"), sem("self_outputs_stored_odd")]
        s_son = sem("self_outputs_by_row")
        s_so = sem("self_outputs_ready")
        s_x1 = sem("x1_ready")
        s_dch = sem("side_vector_steps")
        s_mv1, s_rs1 = sem("moments1_ready"), sem("deviation1_ready")
        s_mv2, s_rs2 = sem("moments2_ready"), sem("deviation2_ready")
        s_mv3, s_rs3 = sem("moments3_ready"), sem("deviation3_ready")
        s_rch = [sem(f"deviation_step_{i}") for i in range(3)]
        s_qp = sem("q_parts_steps")
        s_qd = sem("q_parts_stored")
        s_kp = sem("k_parts_steps")
        s_kd = sem("k_parts_stored")
        s_ql = [sem(f"q_stack_loaded_{g}") for g in range(G)]
        s_kl = [sem(f"k_stack_loaded_{g}") for g in range(G)]
        s_vl = [sem(f"v_loaded_{g}") for g in range(G)]
        s_x1c = sem("x1_kept")
        s_l1 = sem("max_scores_written")
        s_l1r = sem("max_scores_read")
        s_nm = sem("maxima_ready")
        s_mT = sem("maxima_transposed")
        s_m32 = sem("maxima_kept")
        s_mp = sem("maxima_parts_steps")
        s_md = sem("maxima_parts_stored")
        s_ml = [sem(f"maxima_rows_loaded_{g}") for g in range(G)]
        s_l2 = sem("scores_written")
        s_pr = sem("probs_ready")
        s_pv = sem("probs_used")
        s_oc = sem("head_outputs_kept")
        s_od = [sem("outputs_stored_even"), sem("outputs_stored_odd")]
        s_on = sem("outputs_by_row")
        s_or = sem("outputs_ready")
        s_fw = sem("finish_bank_written")
        s_fr = sem("finish_bank_read")
        s_fch = sem("finish_vector_steps")
        s_x2 = sem("x2_ready")
        s_le = sem("router_exp_ready")
        s_oh = sem("chosen_expert_ready")
        s_disp = sem("dispatch_rows_ready")
        s_x2c = sem("x2_kept")
        s_sct = sem("tokens_dispatched")
        s_ew = [sem("expert_weights_loaded_0"), sem("expert_weights_loaded_1")]
        s_et = sem("expert_rows_transposed")
        s_etc = sem("expert_rows_kept")
        s_eh = sem("expert_hidden_written")
        s_ehs = sem("expert_hidden_kept_scalar")
        s_ehv = sem("expert_hidden_kept_vector")
        s_eow = sem("expert_output_written")
        s_eo = sem("expert_output_kept")
        s_es = [sem("expert_output_stored_0"), sem("expert_output_stored_1")]
        s_cc = sem("combination_rows_filled")
        s_g = sem("combination_rows_gathered")
        s_cch = sem("combination_vector_steps")
        s_res = sem("result_ready")
        s_out = sem("output_stored")

        s_passed = {e: sem(f"waits_passed_{n}") for e, n in (
            (mybir.EngineType.SP, "sp"), (mybir.EngineType.Pool, "pool"), (mybir.EngineType.DVE, "dve"))}

        def wait_alone(eng, s, v):
            eng.wait_ge(s, v).then_inc(s_passed[eng.engine], 1)

        def wait(eng, s, v):
            if isinstance(v, int):
                if v > 0:
                    eng.wait_ge(s, v)
            elif eng.engine in (mybir.EngineType.SP, mybir.EngineType.Pool):
                wait_alone(eng, s, v)
            else:
                eng.wait_ge(s, v)

        class Steps:
            def __init__(self, eng, s, per, alone=False):
                self.eng, self.s, self.per, self.k, self.alone = eng, s, per, 0, alone

            def link(self, b, ins):
                self.k = self.k % self.per + 1
                ins.then_inc(self.s, 1)
                if self.alone and not isinstance(b, int):
                    wait_alone(self.eng, self.s, b * self.per + self.k)
                else:
                    wait(self.eng, self.s, b * self.per + self.k)

        reads = [[u for u in range(i, NU, 2) if uses[u][2] != "sc"] for i in range(2)]

        def use_read(b, u):
            name, arg = uses[u][2:]
            if name == "sc":
                return s_z, (b * H + arg + 1) * ST
            return s_read[u % 2], b * len(reads[u % 2]) + reads[u % 2].index(u) + 1

        def wait_read(eng, b, name, arg=0):
            wait(eng, *use_read(b, index[(name, arg)]))

        def wait_full(eng, b, name, arg=0):
            u = index[(name, arg)]
            wait(eng, s_full[u % 2], b * (NU // 2) + u // 2 + 1)
            return b_side[u % 2], s_read[u % 2]

        def wait_free(eng, b, name, arg=0):
            u = index[(name, arg)]
            if u >= 2:
                wait(eng, *use_read(b, u - 2))
            else:
                wait(eng, *use_read(b - 1, NU + u - 2))
            return b_side[u % 2], s_full[u % 2]

        def run(eng, maxima, attend, finish, side, maxt):
            def period(b, prev=True, cur=True, nxt=True):
                for s in range(H):
                    for k in range(SLOTS):
                        if k == 0 and s == 0 and prev:
                            maxt(b - 1, G - 1)
                        if k == 0 and s in (HG, 2 * HG, 3 * HG) and cur:
                            maxt(b, s // HG - 1)
                        if cur:
                            maxima(b, s, k)
                        if s < LAG and prev:
                            attend(b - 1, H - LAG + s, k)
                        if s >= LAG and cur:
                            attend(b, s - LAG, k)
                        if prev:
                            finish(b - 1, s, k)
                        if nxt:
                            side(b + 1, s, k)
            for s in range(H):
                for k in range(SLOTS):
                    side(0, s, k)
            period(0, prev=False)
            with eng.Fori(1, B - 1) as b:
                period(b)
            period(B - 1, nxt=False)
            period(B, cur=False, nxt=False)

        def nothing(*_):
            pass

        NDC, NFC = 2, 12
        NPC = 4
        NF = 4

        block = ctx.enter_context(nc.Block())

        @block.sync
        def _(sp):
            for i, w in enumerate([*w_self, *w_cross]):
                sp.dma_start(wraw[:, i, :], w).then_inc(s_win, 16)
            sp.dma_start(wr[:], w_router).then_inc(s_win, 16)
            sp.dma_start(posr[:], pos_emb.rearrange("(r p) d -> p r d", p=P)).then_inc(s_win, 16)
            wait(sp, s_ep, NPC)
            sp.dma_start(d_e.rearrange("a d r -> d a r"), epart[:]).then_inc(s_ed, 16)
            wait(sp, s_ed, 16)
            for c in range(NP):
                sp.dma_start(estack[c * NP * HD:(c + 1) * NP * HD, :],
                             d_e.rearrange("a d r -> (a d) r")).then_inc(s_est, 16)
            wait(sp, s_const, NCONST)
            for c in range(E * CAP // (5 * P)):
                sp.dma_start(d_disp[c * 5 * P:(c + 1) * 5 * P].rearrange("(p a) d -> p (a d)", p=P),
                             zeros[:]).then_inc(s_zero, 16)

            def store_part(b, scratch, part, c, steps, done):
                if steps is not None:
                    wait(sp, steps, NPC * b + (1, 3, 4)[c])
                sp.dma_start(scratch[bass.ds(b, 1), c].rearrange("o d h s -> h (o d) s"), part).then_inc(done, 16)

            def load_by_first(b, rows, scratch, done):
                for c in range(NP):
                    sp.dma_start(rows[c * NP * HD:(c + 1) * NP * HD].rearrange("r h s -> r (h s)"),
                                 scratch[bass.ds(b, 1), c].rearrange("o d h s -> (o d) (h s)").unsqueeze(0)
                                 .to_broadcast([NP, HD, rows.shape[1] * rows.shape[2]])).then_inc(done, 16)

            def load_by_second(b, rows, scratch, done):
                sp.dma_start(rows.rearrange("r h s -> r (h s)"),
                             scratch[bass.ds(b, 1)].rearrange("o a d h s -> (o a d) (h s)").unsqueeze(0)
                             .to_broadcast([NP, NP * HD, rows.shape[1] * rows.shape[2]])).then_inc(done, 16)

            def stacks(b, g, q=True, kv=True):
                wait(sp, s_pv, (b - 1) * BLK + (g + 1) * HG * SLOTS)
                if kv:
                    wait(sp, s_ones, 2)
                    wait(sp, s_kd, 16 * NP * (b + 1))
                    load_by_second(b, ks[0:KR, g * HG:(g + 1) * HG, :], d_k[:, :, :, g * HG:(g + 1) * HG, :],
                                   s_kl[g])
                    for n in (2, 3):
                        wait_read(sp, b, "vp", n)
                    sp.dma_start(vb[:, g].rearrange("p t h e -> p (t h e)"),
                                 vst[:, g].rearrange("p t h e -> p (t h e)")).then_inc(s_vl[g], 16)
                if q:
                    wait(sp, s_qd, 16 * NP * (b + 1))
                    load_by_first(b, qs[0:KR, g * HG:(g + 1) * HG, :], d_q[:, :, :, g * HG:(g + 1) * HG, :],
                                  s_ql[g])

            def side(b, s, k):
                if (s, k) == (0, 0):
                    wait(sp, s_mv1, b)
                    sp.dma_start(xin[:], x[bass.ds(b, 1)].rearrange("o (t p) d -> p (o t) d", p=P)
                                 ).then_inc(s_x, 16)
                    for n in (2, 3):
                        wait_full(sp, b - 1, "ctxT", n)
                    sp.dma_start(ctxs[:, 0:TT - 1, :], ctx_in[bass.ds(b, 1), 0:(TT - 1) * P, :]
                                 .rearrange("o (t p) d -> p (o t) d", p=P)).then_inc(s_ctx, 16)
                    sp.dma_start(ctxs[:, TT - 1, :], ctx_in[bass.ds(b, 1), LAST0:TK, :]
                                 .rearrange("o p d -> (o p) d")).then_inc(s_ctx, 16)
                if (s, k) == (0, 6):
                    for c in range(NP):
                        store_part(b, d_sq, qkp[:, c, 0:S], c, s_sqp, s_sqd)
                        store_part(b, d_sk, qkp[:, c, S:2 * S], c, None, s_sqd)
                    wait(sp, s_sqd, 16 * 2 * NP * (b + 1))
                    for arg in (H - 2, H - 1):
                        wait_full(sp, b - 1, "sc", arg)
                    load_by_first(b, sq[:], d_sq, s_sst)
                    load_by_second(b, sk[:], d_sk, s_sst)
                if (s, k) == (8, 2):
                    for c in range(NP):
                        store_part(b, d_k, kp[:, c, :], c, s_kp, s_kd)
                if (s, k) == (13, 6):
                    for c in range(NP):
                        store_part(b, d_q, qp[:, c, :], c, s_qp, s_qd)
                for g in range(G):
                    for st in range(ST):
                        if (s, k) == ((2 + g, 3), (3 + g, 0))[st]:
                            for n in (2, 3):
                                wait_read(sp, b, "qe", g * 8 + st * HG + n)
                            wait(sp, s_bias[g % 2][st], 16 * (2 * (b - 1) + g // 2 + 1))
                            sp.dma_start(d_rel[g, st], qe[:, st]).then_inc(s_rel[g % 2][st], 16)
                    if (s, k) == ((3, 1), (4, 1), (6, 1), (8, 1))[g]:
                        wait(sp, s_z, ST * (H * b + HG * (g - 1)))
                        for st in range(ST):
                            wait(sp, s_rel[g % 2][st], 16 * (2 * b + g // 2 + 1))
                            sp.dma_start(bias[:, g % 2, st],
                                         bass.AP(tensor=d_rel.tensor, offset=(g * ST + st) * P * HG * RW + P,
                                                 ap=[[HG * RW - 1, P], [RW, HG], [1, S]])
                                         ).then_inc(s_bias[g % 2][st], 16)
                if k == 2 and 5 <= s < 5 + H // 2:
                    p = s - 5
                    wait_read(sp, b, "pv", p)
                    store(b, soraw, d_so, p, s_sod)
                    if p == H // 2 - 1:
                        wait(sp, s_so, b)
                        spread(b, sonum, soden, d_so, s_sod, s_son)
                if k == SLOTS - 1:
                    if s == 11:
                        stacks(b, 0, q=False)
                    if s == 13:
                        stacks(b, 1, q=False)
                    if s == 15:
                        stacks(b, 0, kv=False)
                        stacks(b, 1, kv=False)

            def store(b, raw, scratch, p, done):
                sp.dma_start(scratch[bass.ds(b, 1), 2 * p:2 * p + 2].rearrange("o h e s -> e (o h) s"),
                             raw[:, p % 2]).then_inc(done[p % 2], 16)

            def spread(b, num, den, scratch, stored, done):
                for i in range(2):
                    wait(sp, stored[i], 16 * H // 4 * (b + 1))
                sp.dma_start(num[:], scratch[bass.ds(b, 1), :, 0:HD].rearrange("o h d s -> (o h) d s")
                             ).then_inc(done, 16)
                sp.dma_start(den[:], scratch[bass.ds(b, 1), :, HD].rearrange("o h s -> (o h) s").unsqueeze(1)
                             .to_broadcast([H, HD, S])).then_inc(done, 16)

            def attend(b, h, k):
                if k == 4 and h % 2 == 0 and h:
                    wait(sp, s_oc, H * b + h)
                    store(b, oraw, d_o, h // 2 - 1, s_od)

            def maxima(b, s, k):
                if (s, k) == (1, SLOTS - 1):
                    stacks(b, 2)
                if (s, k) == (5, SLOTS - 1):
                    stacks(b, 3)
                if k == 4 and s in (HG, 2 * HG, 3 * HG):
                    rows(b, s // HG - 1)

            def finish(b, s, k):
                if (s, k) == (0, 4):
                    rows(b, G - 1)
                if (s, k) == (6, 2):
                    wait(sp, s_oc, H * (b + 1))
                    store(b, oraw, d_o, H // 2 - 1, s_od)
                    wait(sp, s_or, b)
                    spread(b, onum, oden, d_o, s_od, s_on)

            def rows(b, g):
                wait(sp, s_md, 16 * (G * b + g + 1))
                sp.dma_start(qs[KR:KM, g * HG:(g + 1) * HG, :].rearrange("r h s -> r (h s)"),
                             d_m[bass.ds(b, 1), :, g * HG:(g + 1) * HG]
                             .rearrange("o c h t s -> (o c) (h t s)")).then_inc(s_ml[g], 16)

            run(sp, maxima, attend, finish, side, nothing)

            wait(sp, s_pv, B * BLK)
            def experts(e2):
                for i in range(2):
                    e = e2 * 2 + i
                    wait(sp, s_eow, e - 1)
                    sp.dma_start(w1s[:, i, :], w1[bass.ds(e, 1)].rearrange("o d f -> (o d) f")
                                 ).then_inc(s_ew[i], 16)
                    sp.dma_start(w2s[:, i], w2[bass.ds(e, 1)].rearrange("o (t p) d -> p (o t) d", p=P)
                                 ).then_inc(s_ew[i], 16)
                    wait(sp, s_sct, 16 * NTOK)
                    for r in range(NR):
                        n = min(P, CAP - r * P)
                        sp.dma_start(ein[0:n, i, r, :], d_disp[bass.ds(e * CAP + r * P, n), :]
                                     ).then_inc(s_ew[i], 16)
            experts(0)
            with sp.Fori(1, E // 2) as e2:
                experts(e2)
            for j in range(0, NTOK, 4):
                wait(sp, s_res, j // 4 + 1)
                sp.dma_start(out.rearrange("b (t p) d -> p (b t) d", p=P)[:, j:j + 4, :],
                             comb[:, j:j + 4, :]).then_inc(s_out, 16)
            wait(sp, s_out, 16 * NTOK // 4)

        @block.gpsimd
        def _(pool):
            nc.gpsimd.memset(ident[:], 0.0).then_inc(s_const, 1)
            nc.gpsimd.memset(upper[:], 1.0).then_inc(s_const, 1)
            nc.gpsimd.memset(vmask[:], 1.0).then_inc(s_const, 1)
            nc.gpsimd.memset(zeros[:], 0.0).then_inc(s_const, 1)
            nc.gpsimd.iota(rank[:], pattern=[[-1, E]], base=E, channel_multiplier=0,
                           allow_small_or_imprecise_dtypes=True).then_inc(s_const, 1)
            wait(pool, s_const, 5)
            nc.gpsimd.affine_select(out=ident[:], in_=ident[:], compare_op=ALU.not_equal, fill=1.0, base=0,
                                    pattern=[[-1, P]], channel_multiplier=1).then_inc(s_const, 1)
            nc.gpsimd.affine_select(out=upper[:], in_=upper[:], compare_op=ALU.is_ge, fill=0.0, base=0,
                                    pattern=[[1, P]], channel_multiplier=-1).then_inc(s_const, 1)
            nc.gpsimd.affine_select(out=vmask[:], in_=vmask[:], compare_op=ALU.is_ge, fill=0.0, base=-OVER,
                                    pattern=[[0, 1]], channel_multiplier=1).then_inc(s_const, 1)
            nc.gpsimd.memset(minus_half[:], -0.5)
            nc.gpsimd.memset(ones_bf[:], 1.0).then_inc(s_const, 1)

            def deviation(n, mv, rs, step, done):
                nc.gpsimd.tensor_scalar(rs, mv, EPS, None, ALU.add).then_inc(step, 1)
                wait(pool, step, n + 1)
                nc.gpsimd.tensor_tensor(rs, rs, minus_half[:, 0:rs.shape[1]], ALU.pow).then_inc(done, 1)

            def split(b, src, tmp, part, steps):
                steps.link(b, nc.gpsimd.tensor_copy(part(0), src))
                steps.link(b, nc.gpsimd.tensor_tensor(tmp, src, part(0), ALU.subtract))
                steps.link(b, nc.gpsimd.tensor_copy(part(1), tmp))
                steps.link(b, nc.gpsimd.tensor_tensor(part(2), tmp, part(1), ALU.subtract))

            esteps = Steps(pool, s_ep, NPC)
            wait(pool, s_etab, NET)
            split(0, etab[:], etmp[:], lambda a: epart[:, a, :], esteps)
            self_steps, q_steps = Steps(pool, s_sqp, NPC), Steps(pool, s_qp, NPC)
            k_steps, m_steps = Steps(pool, s_kp, NPC), Steps(pool, s_mp, NPC)

            def side(b, s, k):
                if (s, k) == (0, 5):
                    wait_read(pool, b, "qk")
                    wait(pool, s_qd, 16 * NP * b)
                    split(b, qk32[:], tmp32[:, 0:2 * S], lambda a: qkp[:, a, :], self_steps)
                if (s, k) == (8, 1):
                    for n in (2, 3):
                        wait_read(pool, b, "kp", n)
                    wait(pool, s_sqd, 16 * 2 * NP * (b + 1))
                    split(b, k32[:], tmp32[:], lambda a: kp[:, a, :], k_steps)
                if (s, k) == (13, 0):
                    wait(pool, s_mv1, b + 1)
                    deviation(b, mv1[:, :, 1], rs1[:], s_rch[0], s_rs1)
                if (s, k) == (13, 5):
                    wait_read(pool, b, "cq")
                    wait(pool, s_kd, 16 * NP * (b + 1))
                    split(b, q32, tmp32[:, 0:S], lambda a: qp[:, a, :], q_steps)
                    wait(pool, s_x1, 1 * (b + 1))
                    nc.gpsimd.tensor_copy(xall[:, bass.ds(b * ST, ST), :], x1[:]).then_inc(s_x1c, 1)

            def maxt(b, g):
                wait(pool, s_m32, G * b + g + 1)
                wait(pool, s_md, 16 * (G * b + g))
                split(G * b + g, m32[:], mt[:], lambda a: mp[:, a, :], m_steps)
                pool.dma_start(d_m[bass.ds(b, 1), :, g * HG:(g + 1) * HG].rearrange("o c h t s -> (h t) (o c) s"),
                               mp[:]).then_inc(s_md, 16)

            def finish(b, s, k):
                if (s, k) == (7, 6):
                    wait(pool, s_mv2, b + 1)
                    deviation(b, mv2[:, :, 1], rs2[:], s_rch[1], s_rs2)
                if (s, k) == (10, 4):
                    wait(pool, s_disp, b + 1)
                    wait(pool, s_zero, 16 * (E * CAP // (5 * P)))
                    for st in range(ST):
                        nc.gpsimd.indirect_dma_start(
                            out=d_disp, out_offset=bass.IndirectOffsetOnAxis(ap=slot_i[:, st:st + 1], axis=0),
                            in_=x2[:, st, :], in_offset=None, bounds_check=E * CAP - 1,
                            oob_is_err=False).then_inc(s_sct, 16)
                    nc.gpsimd.tensor_copy(xall[:, bass.ds(b * ST, ST), :], x2[:])
                    nc.gpsimd.tensor_copy(slots[:, bass.ds(b * ST, ST)], slot_i[:])
                    nc.gpsimd.tensor_copy(fac[:, bass.ds(b * ST, ST)], fac1[:]).then_inc(s_x2c, 1)
                    wait(pool, s_sct, 16 * ST * (b + 1))

            run(pool, nothing, nothing, finish, side, maxt)

            wait(pool, s_x2c, B)
            wait(pool, s_pv, B * BLK)
            nc.gpsimd.tensor_copy(comb[:].rearrange("p t d -> p (t d)"),
                                  xall[:].rearrange("p t d -> p (t d)")).then_inc(s_cc, 1)
            wait(pool, s_cc, 1)

            def experts(e2):
                for i in range(2):
                    e = e2 * 2 + i
                    wait(pool, s_eo, 2 * (e + 1))
                    for r in range(NR):
                        n = min(P, CAP - r * P)
                        pool.dma_start(d_eout[bass.ds(e * CAP + r * P, n), :], eo[0:n, i, r, :]
                                       ).then_inc(s_es[i], 16)

            experts(0)
            with pool.Fori(1, E // 2) as e2:
                experts(e2)
            for i in range(2):
                wait(pool, s_es[i], 16 * NR * E // 2)
            for j in range(NTOK):
                nc.gpsimd.indirect_dma_start(
                    out=comb[:, j, :], out_offset=None, in_=d_eout,
                    in_offset=bass.IndirectOffsetOnAxis(ap=slots[:, j:j + 1], axis=0),
                    bounds_check=E * CAP - 1, oob_is_err=False).then_inc(s_g, 16)
            wait(pool, s_g, 16 * NTOK)
            for n in range(NTOK // 4):
                wait(pool, s_mv3, n + 1)
                deviation(n, mv3[:, 4 * n:4 * n + 4, 1], rs3[:, 4 * n:4 * n + 4], s_rch[2], s_rs3)

        @block.scalar
        def _(act):
            for w in range(2):
                act.wait_ge(s_wt, w + 1)
                nc.scalar.copy(wT[:, 4 * w:4 * w + 4, :].rearrange("p w d -> p (w d)"),
                               banks[w][:, :]).then_inc(s_wtc, 1)

            def keep(b, name, arg, dst, n):
                bank, read = wait_full(act, b, name, arg)
                nc.scalar.copy(dst, bank[:, 0:n]).then_inc(read, 1)

            def side(b, s, k):
                for name, arg in slot_uses.get((s, k), ()):
                    if name == "xT":
                        keep(b, name, arg, xT[:], S)
                    if name == "qk":
                        wait(act, s_qp, NPC * b)
                        keep(b, name, arg, qk32[:], 2 * S)
                    if name == "ctxT":
                        bank, read = wait_full(act, b, name, arg)
                        if arg < 3:
                            nc.scalar.copy(ctxT[:, arg * 4 * P:(arg + 1) * 4 * P], bank[:, :]).then_inc(read, 1)
                        else:
                            nc.scalar.copy(ctxT[:, (TT - 1) * P:TK], bank[:, OVER:P]).then_inc(read, 1)
                    if name == "kp":
                        keep(b, name, arg, k32[:, C0[arg]:C0[arg + 1]], C0[arg + 1] - C0[arg])
                    if name == "qe":
                        g, st, n = arg // 8, arg % 8 // HG, arg % HG
                        if n == 0:
                            wait(act, s_rel[(g - 1) % 2][st], 16 * (2 * b + (g - 1) // 2 + 1))
                        keep(b, name, arg, qe[:, st, n * RW:(n + 1) * RW], RW)
                    if name == "x1T":
                        keep(b, name, arg, x1T[:], S)
                    if name == "cq":
                        keep(b, name, arg, q32, S)
                if 4 <= s <= 11 and k in (3, 4):
                    h = 2 * (s - 4) + k - 3
                    act.wait_ge(s_nb, H * b + h + 1)
                    for st in range(ST):
                        nc.scalar.activation(zp[:, h % 2, st, :], zp[:, h % 2, st, :], ACT.Exp,
                                             bias=snb[:, h, st:st + 1], scale=SCALE).then_inc(s_sp, 1)

            def attend(b, h, k):
                if isinstance(b, int) and (b, h, k) == (0, 0, 0):
                    probs(b, h, k)
                if k < SLOTS - 1:
                    probs(b, h, k + 1)
                elif h < H - 1:
                    probs(b, h + 1, 0)
                elif not (isinstance(b, int) and b == B - 1):
                    probs(b + 1, 0, 0)
                if k == 2 and h:
                    keep_head(b, h - 1)

            def probs(b, h, k):
                n = b * BLK + h * SLOTS + k
                w = S * min(2, TT - 2 * k)
                act.wait_ge(s_l2, n + 1)
                wait(act, s_pv, n - 1)
                i = h * SLOTS + k
                nc.scalar.activation(pr[:, i % 2, 0:w], b_sc[i % 2][:, 0:w], ACT.Exp,
                                     scale=SCALE).then_inc(s_pr, 1)

            def keep_head(b, h):
                act.wait_ge(s_pv, b * BLK + (h + 1) * SLOTS)
                if h % 2 == 0:
                    wait(act, s_od[h // 2 % 2], 16 * (H // 4 * b + h // 4))
                nc.scalar.copy(oraw[:, h // 2 % 2, h % 2, :],
                               b_o[h % 2 * 32:h % 2 * 32 + V1, 0:S]).then_inc(s_oc, 1)

            def maxt(b, g):
                act.wait_ge(s_mT, G * b + g + 1)
                wait(act, s_mp, NPC * (G * b + g))
                nc.scalar.copy(m32[:], b_fin[0:HG * ST, 0:P]).then_inc(s_m32, 1)

            def finish(b, s, k):
                if (s, k) == (6, 0):
                    keep_head(b, H - 1)
                if (s, k) == (8, 4):
                    act.wait_ge(s_fw, NF * b + 2)
                    nc.scalar.copy(x2T[:], b_fin[:, 0:S]).then_inc(s_fr, 1)
                if (s, k) == (9, 1):
                    act.wait_ge(s_fr, NF * b + 3)
                    nc.scalar.activation(pe_[:], pe_[:], ACT.Exp).then_inc(s_le, 1)

            run(act, nothing, attend, finish, side, maxt)

            def experts(e2):
                for i in range(2):
                    e = e2 * 2 + i
                    act.wait_ge(s_et, e + 1)
                    nc.scalar.copy(einT[:, i, :], banks[0][:, 0:CAP]).then_inc(s_etc, 1)
                    for f in range(0, FT, 2):
                        act.wait_ge(s_eh, e * FT + f + 1)
                        nc.scalar.activation(hT[:, i, f, :], banks[1 + f][:, 0:CAP], ACT.Relu).then_inc(s_ehs, 1)

            experts(0)
            with act.Fori(1, E // 2) as e2:
                experts(e2)
        @block.vector
        def _(dve):
            dch, fch = Steps(dve, s_dch, NDC, alone=True), Steps(dve, s_fch, NFC, alone=True)
            dve.wait_ge(s_const, NCONST)
            dve.wait_ge(s_wt, 3)
            pT_neg, pT_pos = banks[2][0:HD, P:2 * P], banks[2][0:HD, 0:P]
            nc.vector.tensor_scalar(etab[:, P:2 * P], pT_neg, 2.0, None, ALU.mult).then_inc(s_etab, 1)
            nc.vector.tensor_scalar(etab[:, 2 * P:3 * P], pT_pos, 2.0, None, ALU.mult).then_inc(s_etab, 1)
            dve.wait_ge(s_etab, 2)
            nc.vector.tensor_copy(etab[:, 0:P], etab[:, P:P + 1].to_broadcast([HD, P])).then_inc(s_etab, 1)
            nc.vector.tensor_copy(etab[:, 3 * P:4 * P],
                                  etab[:, 3 * P - 1:3 * P].to_broadcast([HD, P])).then_inc(s_etab, 1)
            nc.vector.memset(sv[:, :, :, HD], 1.0)
            nc.vector.memset(k32[:, TK:TP], 0.0)
            nc.vector.memset(acc[:], 0.0)
            nc.vector.memset(vst[:, :, :, :, HD], 1.0).then_inc(s_ones, 1)
            dve.wait_ge(s_ones, 1)
            nc.vector.tensor_scalar(vst[:, :, TT - 1, :, HD], vst[:, :, TT - 1, :, HD],
                                    vmask[:, 0:1], None, ALU.mult)
            nc.vector.memset(ks[64:KM, :, :], 1.0).then_inc(s_ones, 1)

            def moments(b, steps, y, stats, mv, done, tiles):
                for t in tiles:
                    last = nc.vector.bn_stats(stats[:, t, :], y[:, t, :])
                steps.link(b, last)
                for t in tiles:
                    last = nc.vector.bn_aggr(mv[:, t, :], stats[:, t, :])
                last.then_inc(done, 1)

            def normalize(y, mv, rs, dst, tiles):
                for t in tiles:
                    last = nc.vector.tensor_scalar(dst[:, t, :], y[:, t, :], mv[:, t, 0:1], rs[:, t:t + 1],
                                                   ALU.subtract, ALU.mult)
                return last

            def side(b, s, k):
                if (s, k) == (12, 5):
                    dve.wait_ge(s_son, 32 * (b + 1))
                    dch.link(b, nc.vector.reciprocal(soden[:], soden[:]))
                    nc.vector.tensor_tensor(soT[:], sonum[:], soden[:], ALU.mult).then_inc(s_so, 1)
                for name, arg in slot_uses.get((s, k), ()):
                    if name == "v":
                        bank, read = wait_full(dve, b, name, arg)
                        nc.vector.tensor_copy(sv[:, :, :, 0:HD],
                                              bank[:, 0:ST * D].rearrange("p (t h d) -> p t h d", t=ST, h=H)
                                              ).then_inc(read, 1)
                    if name == "vp":
                        wait(dve, s_vl[G - 1], 16 * b)
                        bank, read = wait_full(dve, b, name, arg)
                        for t in range(4 * arg, min(4 * arg + 4, TT)):
                            src = bank[:, (t % 4) * D:(t % 4 + 1) * D].rearrange("p (g h d) -> p g h d", g=G, h=HG)
                            if t < TT - 1:
                                last = nc.vector.tensor_copy(vst[:, :, t, :, 0:HD], src)
                            else:
                                last = nc.vector.tensor_scalar(vst[:, :, t, :, 0:HD], src, vmask[:, 0:1], None,
                                                               ALU.mult)
                        last.then_inc(read, 1)
                    if name == "sc":
                        h, g = arg, arg // HG
                        bank, _ = wait_full(dve, b, name, arg)
                        if h >= 2:
                            wait_full(dve, b, "pt", h - 2)
                        wait_alone(dve, s_bias[g % 2][0], 16 * (2 * b + g // 2 + 1))
                        for st in range(ST):
                            if h % HG == 0:
                                wait_alone(dve, s_bias[g % 2][st], 16 * (2 * b + g // 2 + 1))
                            nc.vector.tensor_tensor_reduce(
                                out=zp[:, h % 2, st, :], in0=bank[:, st * S:(st + 1) * S],
                                in1=bias[:, g % 2, st, h % HG, :], scale=1.0, scalar=NEG, op0=ALU.add,
                                op1=ALU.max, accum_out=smx[:, h, st:st + 1]).then_inc(s_z, 1)
                        dve.wait_ge(s_z, ST * (H * b + h + 1))
                        nc.vector.tensor_scalar(snb[:, h, :], smx[:, h, :], -SCALE, None, ALU.mult).then_inc(s_nb, 1)
                    if name == "pt":
                        bank, read = wait_full(dve, b, name, arg)
                        if arg >= 2:
                            wait_full(dve, b, "pv", arg // 2 - 1)
                        nc.vector.tensor_copy(pT[:, arg % 2, :], bank[:, :]).then_inc(read, 1)
                    if name == "pv":
                        bank, read = wait_full(dve, b, name, arg)
                        wait(dve, s_sod[arg % 2], 16 * (H // 4 * b + arg // 2))
                        nc.vector.tensor_copy(soraw[:, arg % 2].rearrange("p h s -> p (h s)"),
                                              bank[0:V1, :]).then_inc(read, 1)
                    if name == "wp":
                        bank, read = wait_full(dve, b, name, arg)
                        nc.vector.tensor_tensor(y1[:].rearrange("p t d -> p (t d)"), bank[:, 0:ST * D],
                                                xin[:].rearrange("p t d -> p (t d)"), ALU.add).then_inc(read, 1)
                        wait_read(dve, b, "wp")
                        moments(b, dch, y1, st1, mv1, s_mv1, range(ST))
                if (s, k) == (13, 1):
                    dve.wait_ge(s_rs1, b + 1)
                    wait(dve, s_x1c, b)
                    normalize(y1, mv1, rs1, x1, range(ST)).then_inc(s_x1, 1)

            def maxima(b, h, k):
                for i in ((k,) if k < SLOTS - 1 else (k, k + 1)):
                    st, c = i // NCH, i % NCH
                    dve.wait_ge(s_l1, NL1 * b + 8 * h + i + 1)
                    nc.vector.tensor_reduce(mx4[:, h, st, c:c + 1], b_mx[i % 2][:, 0:C0[c + 1] - C0[c]], AX,
                                            ALU.max).then_inc(s_l1r, 1)
                if k == SLOTS - 1 and h % HG == HG - 1:
                    g = h // HG
                    dve.wait_ge(s_l1r, NL1 * b + 8 * h + 8)
                    nc.vector.tensor_reduce(nmx[:, g * HG:(g + 1) * HG, :], mx4[:, g * HG:(g + 1) * HG], AX,
                                            ALU.max, negate=True).then_inc(s_nm, 1)

            def finish(b, s, k):
                if (s, k) == (7, 1):
                    dve.wait_ge(s_on, 32 * (b + 1))
                    fch.link(b, nc.vector.reciprocal(oden[:], oden[:]))
                    nc.vector.tensor_tensor(oT[:], onum[:], oden[:], ALU.mult).then_inc(s_or, 1)
                if (s, k) == (7, 5):
                    dve.wait_ge(s_fw, NF * b + 1)
                    dve.wait_ge(s_x1c, b + 1)
                    nc.vector.tensor_tensor(y2[:], b_fin[:, 0:ST * D].rearrange("p (t d) -> p t d", t=ST),
                                            xall[:, bass.ds(b * ST, ST), :], ALU.add).then_inc(s_fr, 1)
                    dve.wait_ge(s_fr, NF * b + 1)
                    moments(b, fch, y2, st2, mv2, s_mv2, range(ST))
                if (s, k) == (8, 1):
                    dve.wait_ge(s_rs2, b + 1)
                    normalize(y2, mv2, rs2, x2, range(ST)).then_inc(s_x2, 1)
                if (s, k) == (9, 0):
                    dve.wait_ge(s_fw, NF * b + 3)
                    logits = b_fin[:, 0:ST * E].rearrange("p (t e) -> p t e", t=ST)
                    fch.link(b, nc.vector.tensor_reduce(lmx[:], logits, AX, ALU.max))
                    nc.vector.tensor_tensor(pe_[:], logits, lmx[:].unsqueeze(2).to_broadcast([P, ST, E]),
                                            ALU.subtract).then_inc(s_fr, 1)
                if (s, k) == (9, 3):
                    dve.wait_ge(s_le, b + 1)
                    nc.vector.tensor_reduce(pmx[:], pe_[:], AX, ALU.max)
                    fch.link(b, nc.vector.tensor_reduce(psm[:], pe_[:], AX, ALU.add))
                    fch.link(b, nc.vector.tensor_tensor(oh[:], pe_[:], pmx[:].unsqueeze(2).to_broadcast([P, ST, E]),
                                                        ALU.is_equal))
                    fch.link(b, nc.vector.tensor_tensor(oh[:], oh[:],
                                                        rank[:].unsqueeze(1).to_broadcast([P, ST, E]), ALU.mult))
                    nc.vector.reciprocal(psm[:], psm[:])
                    fch.link(b, nc.vector.tensor_reduce(okk[:], oh[:], AX, ALU.max))
                    nc.vector.tensor_tensor(fac1[:], pmx[:], psm[:], ALU.mult)
                    nc.vector.tensor_tensor(ohb[:], oh[:], okk[:].unsqueeze(2).to_broadcast([P, ST, E]),
                                            ALU.is_equal).then_inc(s_oh, 1)
                if (s, k) == (10, 2):
                    dve.wait_ge(s_fw, NF * b + 4)
                    nc.vector.tensor_tensor(cum[:], b_fin[:, 0:ST * E].rearrange("p (t e) -> p t e", t=ST), ohb[:],
                                            ALU.mult).then_inc(s_fr, 1)
                    dve.wait_ge(s_fr, NF * b + 4)
                    nc.vector.tensor_reduce(pos[:], cum[:], AX, ALU.add)
                    fch.link(b, nc.vector.tensor_tensor(acc[:, 0], acc[:, 0], ohb[:, 0, :], ALU.add))
                    nc.vector.tensor_scalar(kept[:], pos[:], float(CAP), None, ALU.is_le)
                    nc.vector.tensor_scalar(base[:], okk[:], -float(CAP), float(E * CAP - 1), ALU.mult, ALU.add)
                    fch.link(b, nc.vector.tensor_tensor(acc[:, 0], acc[:, 0], ohb[:, 1, :], ALU.add))
                    nc.vector.tensor_tensor(base[:], base[:], pos[:], ALU.add)
                    fch.link(b, nc.vector.tensor_scalar(koff[:], kept[:], -OOB, OOB, ALU.mult, ALU.add))
                    nc.vector.tensor_scalar(fac1[:], fac1[:], -1.0, None, ALU.add)
                    fch.link(b, nc.vector.tensor_tensor(slot_i[:], base[:], koff[:], ALU.add))
                    fch.link(b, nc.vector.tensor_tensor(fac1[:], fac1[:], kept[:], ALU.mult))
                    nc.vector.tensor_scalar(fac1[:], fac1[:], 1.0, None, ALU.add).then_inc(s_disp, 1)

            run(dve, maxima, nothing, finish, side, nothing)

            def experts(e2):
                for i in range(2):
                    e = e2 * 2 + i
                    for f in range(1, FT, 2):
                        dve.wait_ge(s_eh, e * FT + f + 1)
                        nc.vector.tensor_scalar(hT[:, i, f, :], banks[1 + f][:, 0:CAP], 0.0, None,
                                                ALU.max).then_inc(s_ehv, 1)
                    wait(dve, s_es[i], 16 * NR * e2)
                    dve.wait_ge(s_eow, e + 1)
                    full = CAP // P
                    nc.vector.tensor_copy(eo[:, i, 0:full, :],
                                          banks[5 + i][:, 0:full * D].rearrange("p (t d) -> p t d", t=full)
                                          ).then_inc(s_eo, 1)
                    n = CAP - full * P
                    nc.vector.tensor_copy(eo[0:n, i, full, :], banks[5 + i][0:n, full * D:(full + 1) * D]
                                          ).then_inc(s_eo, 1)

            experts(0)
            with dve.Fori(1, E // 2) as e2:
                experts(e2)
            cch = Steps(dve, s_cch, 2)
            for n in range(NTOK // 4):
                tiles = range(4 * n, 4 * n + 4)
                dve.wait_ge(s_g, 16 * NTOK)
                for t in tiles:
                    last = nc.vector.scalar_tensor_tensor(comb[:, t, :], comb[:, t, :], fac[:, t:t + 1],
                                                          xall[:, t, :], ALU.mult, ALU.add)
                cch.link(n, last)
                moments(n, cch, comb, st3, mv3, s_mv3, tiles)
            for n in range(NTOK // 4):
                dve.wait_ge(s_rs3, n + 1)
                normalize(comb, mv3, rs3, comb, range(4 * n, 4 * n + 4)).then_inc(s_res, 1)

        @block.tensor
        def _(pe):
            pe.wait_ge(s_const, NCONST)
            pe.wait_ge(s_win, 16 * 10)
            for w in range(8):
                last = nc.tensor.transpose(banks[w // 4][:, (w % 4) * D:(w % 4 + 1) * D], wraw[:, w, :], ident[:])
                if w % 4 == 3:
                    last.then_inc(s_wt, 1)
            for r in range(2):
                last = nc.tensor.transpose(banks[2][0:HD, r * P:(r + 1) * P], posr[:, r, :], ident[:])
            last.then_inc(s_wt, 1)
            pe.wait_ge(s_wtc, 2)

            def mm(dst, lhsT, rhs, start=True, stop=True, shared=False):
                return nc.tensor.matmul(dst, lhsT, rhs, start=start, stop=stop, skip_group_check=shared)

            def product(b, name, arg):
                if name == "xT":
                    pe.wait_ge(s_x, 16 * (b + 1))
                if name == "ctxT" and arg == 0:
                    pe.wait_ge(s_ctx, 32 * (b + 1))
                if name == "qk":
                    wait_read(pe, b, "xT")
                if name == "kp" and arg == 0:
                    for n in (2, 3):
                        wait_read(pe, b, "ctxT", n)
                if name == "qe" and arg == 0:
                    pe.wait_ge(s_sst, 16 * (1 + NP) * (b + 1))
                    pe.wait_ge(s_est, 16 * NP)
                if name == "pt":
                    pe.wait_ge(s_sp, ST * (H * b + arg + 1))
                if name == "pv":
                    for n in (0, 1):
                        wait_read(pe, b, "pt", 2 * arg + n)
                    if arg == 0:
                        wait_read(pe, b, "v")
                if name == "wp":
                    pe.wait_ge(s_so, b + 1)
                if name == "x1T":
                    pe.wait_ge(s_x1, b + 1)
                if name == "cq":
                    wait_read(pe, b, "x1T")
                bank, full = wait_free(pe, b, name, arg)
                if name == "xT":
                    for st in range(ST):
                        last = nc.tensor.transpose(bank[:, st * P:(st + 1) * P], xin[:, st, :], ident[:])
                if name == "qk":
                    for i, w in enumerate((WQ, WK)):
                        last = mm(bank[:, i * S:(i + 1) * S], wT[:, w, :], xT[:])
                if name == "v":
                    for st in range(ST):
                        last = mm(bank[:, st * D:(st + 1) * D], xT[:, st * P:(st + 1) * P], wT[:, WV, :])
                if name == "ctxT":
                    for t in range(4 * arg, min(4 * arg + 4, TT)):
                        last = nc.tensor.transpose(bank[:, (t % 4) * P:(t % 4 + 1) * P], ctxs[:, t, :], ident[:])
                if name == "kp":
                    last = mm(bank[:, 0:C0[arg + 1] - C0[arg]], wT[:, XK, :], ctxT[:, C0[arg]:C0[arg + 1]])
                if name == "vp":
                    for t in range(4 * arg, min(4 * arg + 4, TT)):
                        t0 = t * P if t < TT - 1 else LAST0
                        last = mm(bank[:, (t % 4) * D:(t % 4 + 1) * D], ctxT[:, t0:t0 + P], wT[:, XV, :])
                if name == "qe":
                    g, st, n = arg // 8, arg % 8 // HG, arg % HG
                    e0 = (ST - 1 - st) * P
                    last = mm(bank[:, 0:RW], sq[:, g * HG + n, st * P:(st + 1) * P], estack[:, e0:e0 + RW])
                if name == "sc":
                    for st in range(ST):
                        last = mm(bank[:, st * S:(st + 1) * S], sq[:, arg, st * P:(st + 1) * P], sk[:, arg, :])
                if name == "pt":
                    for st in range(ST):
                        for jt in range(ST):
                            last = nc.tensor.transpose(bank[:, jt * S + st * P:jt * S + (st + 1) * P],
                                                       zp[:, arg % 2, st, jt * P:(jt + 1) * P], ident[:])
                if name == "pv":
                    for n in range(2):
                        for jt in range(ST):
                            last = mm(bank[0:V1, n * S:(n + 1) * S], sv[:, jt, 2 * arg + n, :],
                                      pT[:, n, jt * S:(jt + 1) * S], start=jt == 0, stop=jt == ST - 1)
                if name == "wp":
                    for st in range(ST):
                        last = mm(bank[:, st * D:(st + 1) * D], soT[:, st * P:(st + 1) * P], wT[:, WP, :])
                if name == "x1T":
                    for st in range(ST):
                        last = nc.tensor.transpose(bank[:, st * P:(st + 1) * P], x1[:, st, :], ident[:])
                if name == "cq":
                    last = mm(bank[:, 0:S], wT[:, XQ, :], x1T[:])
                last.then_inc(full, 1)

            def side(b, s, k):
                for name, arg in slot_uses.get((s, k), ()):
                    product(b, name, arg)

            def maxima(b, h, k):
                if isinstance(b, int) and (b, h, k) == (0, 0, 0):
                    pe.wait_ge(s_etab, NET)
                if k == 0 and h % HG == 0:
                    g = h // HG
                    pe.wait_ge(s_kl[g], 16 * (b + 1))
                    pe.wait_ge(s_ql[g], 16 * NP * (b + 1))
                for i in ((k,) if k < SLOTS - 1 else (k, k + 1)):
                    st, c = i // NCH, i % NCH
                    wait(pe, s_l1r, NL1 * b + 8 * h + i - 1)
                    mm(b_mx[i % 2][:, 0:C0[c + 1] - C0[c]], qs[0:KR, h, st * P:(st + 1) * P],
                       ks[0:KR, h, C0[c]:C0[c + 1]]).then_inc(s_l1, 1)

            def maxt(b, g):
                pe.wait_ge(s_nm, G * b + g + 1)
                wait(pe, s_m32, G * b + g)
                if g in (1, 2):
                    wait(pe, s_fr, NF * (b - 1) + (1 if g == 1 else NF))
                nc.tensor.transpose(b_fin[0:HG * ST, 0:P],
                                    nmx[:, g * HG:(g + 1) * HG, :].rearrange("p h t -> p (h t)"),
                                    ident[:]).then_inc(s_mT, 1)

            def scores(b, h, k):
                n = b * BLK + h * SLOTS + k
                i, g = h * SLOTS + k, h // HG
                if k == 0 and h % HG == 0:
                    pe.wait_ge(s_ml[g], 16 * (b + 1))
                wait(pe, s_pr, n - 1)
                for t in range(2 * k, min(2 * k + 2, TT)):
                    t0 = t * P if t < TT - 1 else LAST0
                    last = mm(b_sc[i % 2][:, (t % 2) * S:(t % 2 + 1) * S], ks[:, h, t0:t0 + P], qs[:, h, :])
                last.then_inc(s_l2, 1)

            def attend(b, h, k):
                n = b * BLK + h * SLOTS + k
                i, g = h * SLOTS + k, h // HG
                if isinstance(b, int) and (b, h, k) == (0, 0, 0):
                    scores(b, h, k)
                if k < SLOTS - 1:
                    scores(b, h, k + 1)
                elif h < H - 1:
                    scores(b, h + 1, 0)
                elif not (isinstance(b, int) and b == B - 1):
                    scores(b + 1, 0, 0)
                if k == 0:
                    wait(pe, s_oc, H * b + h - 1)
                if k == 0 and h % HG == 0:
                    pe.wait_ge(s_vl[g], 16 * (b + 1))
                pe.wait_ge(s_pr, n + 1)
                for t in range(2 * k, min(2 * k + 2, TT)):
                    last = mm(b_o[h % 2 * 32:h % 2 * 32 + V1, 0:S], vb[:, g, t, h % HG, :],
                              pr[:, i % 2, (t % 2) * S:(t % 2 + 1) * S], start=t == 0, stop=t == TT - 1, shared=True)
                last.then_inc(s_pv, 1)

            def finish(b, s, k):
                def bank_free(j, maxima_done):
                    if j:
                        wait(pe, s_fr, NF * b + j)
                    if maxima_done is not None:
                        wait(pe, s_m32, maxima_done)
                if (s, k) == (7, 3):
                    pe.wait_ge(s_or, b + 1)
                    bank_free(0, last_maxt(b, 1))
                    for st in range(ST):
                        last = mm(b_fin[:, st * D:(st + 1) * D], oT[:, st * P:(st + 1) * P], wT[:, XO, :])
                    last.then_inc(s_fw, 1)
                if (s, k) == (8, 3):
                    pe.wait_ge(s_x2, b + 1)
                    bank_free(1, last_maxt(b, 2))
                    for st in range(ST):
                        last = nc.tensor.transpose(b_fin[:, st * P:(st + 1) * P], x2[:, st, :], ident[:])
                    last.then_inc(s_fw, 1)
                if (s, k) == (8, 6):
                    bank_free(2, None)
                    for st in range(ST):
                        last = mm(b_fin[:, st * E:(st + 1) * E], x2T[:, st * P:(st + 1) * P], wr[:])
                    last.then_inc(s_fw, 1)
                if (s, k) == (10, 1):
                    pe.wait_ge(s_oh, b + 1)
                    bank_free(3, None)
                    mm(b_fin[:, 0:E], upper[:], ohb[:, 0, :], stop=False)
                    mm(b_fin[:, 0:E], ones_bf[:], acc[:, 0], start=False)
                    mm(b_fin[:, E:2 * E], upper[:], ohb[:, 1, :], stop=False)
                    mm(b_fin[:, E:2 * E], ones_bf[:], ohb[:, 0, :], start=False, stop=False)
                    mm(b_fin[:, E:2 * E], ones_bf[:], acc[:, 0], start=False).then_inc(s_fw, 1)

            def last_maxt(b, n):
                if isinstance(b, int) and b == B - 1:
                    return G * B
                return G * (b + 1) + n

            run(pe, maxima, attend, finish, side, maxt)

            def experts(e2):
                for i in range(2):
                    e = e2 * 2 + i
                    pe.wait_ge(s_ew[i], 16 * (2 + NR) * (e2 + 1))
                    wait(pe, s_etc, e)
                    for r in range(NR):
                        n = min(P, CAP - r * P)
                        last = nc.tensor.transpose(banks[0][:, r * P:r * P + n], ein[0:n, i, r, :], ident[0:n, 0:n])
                    last.then_inc(s_et, 1)
                    pe.wait_ge(s_etc, e + 1)
                    wait(pe, s_ehs, e * (FT // 2))
                    wait(pe, s_ehv, e * (FT // 2))
                    for f in range(FT):
                        mm(banks[1 + f][:, 0:CAP], w1s[:, i, f * P:(f + 1) * P], einT[:, i, :]).then_inc(s_eh, 1)
                    pe.wait_ge(s_ehs, (e + 1) * (FT // 2))
                    pe.wait_ge(s_ehv, (e + 1) * (FT // 2))
                    wait(pe, s_eo, 2 * e)
                    for r in range(NR):
                        n = min(P, CAP - r * P)
                        for f in range(FT):
                            last = mm(banks[5 + i][0:n, r * D:(r + 1) * D], hT[:, i, f, r * P:r * P + n],
                                      w2s[:, i, f, :], start=f == 0, stop=f == FT - 1)
                    last.then_inc(s_eow, 1)

            experts(0)
            with pe.Fori(1, E // 2) as e2:
                experts(e2)
_INS = ['x', 'ctx_1024', 'L0_attn_Wq', 'L0_attn_Wk', 'L0_attn_Wv', 'L0_attn_Wp', 'L0_attn_pos_emb_k',
        'L0_xattn_Wq', 'L0_xattn_Wk', 'L0_xattn_Wv', 'L0_xattn_Wo', 'L0_ffn_Wr', 'L0_ffn_W1', 'L0_ffn_W2']


def kernel(**inputs):
    import numpy as _np
    import concourse.bacc as _bacc
    from concourse import mybir as _mybir
    from concourse.bass_utils import run_bass_kernel_spmd as _run

    nc = _bacc.Bacc("TRN2", target_bir_lowering=False, num_devices=1)
    arrays, ap = {}, {}
    for name in _INS:
        a = _np.ascontiguousarray(inputs[name])
        arrays[f"in_{name}_dram"] = a
        ap[name] = nc.dram_tensor(f"in_{name}_dram", a.shape, _mybir.dt.from_np(a.dtype), kind="ExternalInput").ap()
    out = nc.dram_tensor("out_0_dram", inputs["x"].shape, _mybir.dt.float32, kind="ExternalOutput").ap()
    decoder_layer(nc, ap['x'], ap['ctx_1024'],
                  [ap[f'L0_attn_{n}'] for n in ('Wq', 'Wk', 'Wv', 'Wp')], ap['L0_attn_pos_emb_k'],
                  [ap[f'L0_xattn_{n}'] for n in ('Wq', 'Wk', 'Wv', 'Wo')],
                  ap['L0_ffn_Wr'], ap['L0_ffn_W1'], ap['L0_ffn_W2'], out)
    r = _run(nc, [arrays], core_ids=[0])
    return r.results[0]["out_0_dram"]
```

```python
import concourse.bass as bass
from concourse import mybir
from contextlib import ExitStack


def decoder_layer(nc, x, ctx_in, w_self, pos_emb, w_cross, w_router, w1, w2, out):
    f32, bf16, i32 = mybir.dt.float32, mybir.dt.bfloat16, mybir.dt.int32
    ALU = mybir.AluOpType
    ACT = mybir.ActivationFunctionType
    AX = mybir.AxisListType.X

    P = 128
    B, S, D = x.shape
    TK = ctx_in.shape[1]
    HD = pos_emb.shape[1]
    H = D // HD
    R = pos_emb.shape[0] // 2
    E, _, FF = w1.shape
    ST = S // P
    TT = -(-TK // P)
    LAST0 = TK - P
    OVER = (TT - 1) * P - LAST0
    TP = -(-TK // 4) * 4
    CAP = int(1.25 * B * S / E)
    SCALE = float(HD) ** -0.5
    EPS = 1e-5
    G = 4
    HG = H // G
    NP = 3
    KR = NP * NP * HD
    KM = KR + NP
    V1 = HD + 1
    LAG = 6
    SLOTS = -(-TT // 2)
    NPAIR = H // 2
    BLK = TT * NPAIR
    QUAD = 32
    NCH = 4
    C0 = [TK * c // NCH for c in range(NCH + 1)]
    NL1 = H * ST * NCH
    RW = 3 * P
    NEG = -3.0e38
    NTOK = B * ST
    OOB = 65536.0
    assert R == P and H == 16 and S == ST * P

    uses = []
    def use(s, k, name, arg=0):
        uses.append((s, k, name, arg))
    for s in range(H):
        for k in range(SLOTS):
            if s == 0 and k in (1, 2, 4):
                use(s, k, ("xT", "qk", "v")[k // 2])
            if s == 1 and 1 <= k <= 4:
                use(s, k, "ctxT", k - 1)
            if 4 <= s <= 11 and k == 6:
                use(s, k, "pv", s - 4)
            if 2 <= s <= 5:
                for n in ((0, 1) if k == 0 else (k + 1,)):
                    use(s, k, "qe", (s - 2) * 8 + n)
            if 4 <= s <= 11 and k in (1, 2):
                use(s, k, "pt", 2 * (s - 4) + k - 1)
            if 3 <= s <= 10 and k in (4, 5):
                use(s, k, "sc", 2 * (s - 3) + k - 4)
            if 6 <= s <= 9 and k in (3, 6):
                use(s, k, ("kp", "vp")[(s - 6) // 2], 2 * ((s - 6) % 2) + (k == 6))
            if s == 13 and k in (3, 6):
                use(s, k, ("wp", "x1T")[k // 3 - 1])
            if s == 14 and k == 1:
                use(s, k, "cq")
    NU = len(uses)
    assert NU % 2 == 0
    index = {(n, a): u for u, (_, _, n, a) in enumerate(uses)}
    slot_uses = {}
    for s, k, n, a in uses:
        slot_uses.setdefault((s, k), []).append((n, a))

    ctx = ExitStack()
    with ctx:
        def sb(name, shape, dt=f32):
            return ctx.enter_context(nc.sbuf_tensor(name, shape, dt))

        def sem(name):
            return ctx.enter_context(nc.semaphore(name))

        d_sq = nc.dram_tensor("d_sq", (B, NP, HD, H, S), bf16).ap()
        d_sk = nc.dram_tensor("d_sk", (B, NP, HD, H, S), bf16).ap()
        d_q = nc.dram_tensor("d_q", (B, NP, HD, H, S), bf16).ap()
        d_k = nc.dram_tensor("d_k", (B, NP, HD, H, TP), bf16).ap()
        d_m = nc.dram_tensor("d_m", (B, NP, H, ST, P), bf16).ap()
        d_e = nc.dram_tensor("d_e", (NP, HD, 4 * P), bf16).ap()
        d_rel = nc.dram_tensor("d_rel", (G, ST, P, HG * RW), f32).ap()
        d_so = nc.dram_tensor("d_so", (B, H, V1, S), f32).ap()
        d_o = nc.dram_tensor("d_o", (B, H, V1, S), f32).ap()
        d_disp = nc.dram_tensor("d_disp", (E * CAP, D), f32).ap()
        d_eout = nc.dram_tensor("d_eout", (E * CAP, D), f32).ap()

        ident = sb("ident", [P, P])
        ones_bf = sb("ones_bf", [P, P], bf16)
        upper = sb("upper", [P, P], bf16)
        vmask = sb("vmask", [P, 1])
        minus_half = sb("minus_half", [P, NTOK])
        rank = sb("rank", [P, E])
        bias_raw = sb("bias_raw", [P, 2 * ST * HG * S])
        bias = bias_raw[:].rearrange("p (a t h s) -> p a t h s", a=2, t=ST, h=HG)
        wraw = bias_raw[:, 0:8 * D].rearrange("p (w d) -> p w d", w=8)
        zeros = bias_raw[:, 8 * D:13 * D]
        etab = bias_raw[0:HD, 13 * D:17 * D]
        etmp = bias_raw[0:HD, 17 * D:21 * D]
        epart = bias_raw[0:HD, 21 * D:27 * D].bitcast(bf16).rearrange("p (c r) -> p c r", c=NP)
        wT = sb("wT", [P, 8, D])
        WQ, WK, WV, WP, XQ, XK, XV, XO = range(8)
        wr = sb("wr", [P, E])
        posr = sb("posr", [P, 2, HD])
        estack = sb("estack", [KR, 4 * P], bf16)
        xin = sb("xin", [P, ST, D])
        xT = sb("xT", [P, S])
        qk32 = sb("qk32", [P, 2 * S])
        sq = sb("sq", [KR, H, S], bf16)
        sk = sb("sk", [KR, H, S], bf16)
        sv = sb("sv", [P, ST, H, V1])
        qe = sb("qe", [P, ST, HG * RW])
        zp = sb("zp", [P, 2, ST, S])
        smx = sb("smx", [P, H, ST])
        snb = sb("snb", [P, H, ST])
        pT = sb("pT", [P, 2, 2 * S])
        soraw = sb("soraw", [V1, 2, 2, S])
        sonum = sb("sonum", [P, S])
        soden = sb("soden", [P, S])
        soT = sb("soT", [P, S])
        y1 = sb("y1", [P, ST, D])
        st1 = sb("st1", [P, ST, 6])
        mv1 = sb("mv1", [P, ST, 2])
        rs1 = sb("rs1", [P, ST])
        x1 = sb("x1", [P, ST, D])
        x1T = sb("x1T", [P, S])
        q32 = qk32[:, 0:S]
        ctxs = sb("ctxs", [P, TT, D])
        ctxT = sb("ctxT", [P, TK])
        k32 = sb("k32", [P, TP])
        tmp32 = sb("tmp32", [P, TP])
        kp = sb("kp", [P, NP, TP], bf16)
        qkp, qp = kp[:, :, 0:2 * S], kp[:, :, 0:S]
        vst = sb("vst", [P, G, TT, HG, V1])
        ks_raw = sb("ks_raw", [P, H * TP], bf16)
        ks = ks_raw[0:KM, :].rearrange("p (h t) -> p h t", h=H)
        qs = sb("qs", [KM, H, S], bf16)
        vb = sb("vb", [P, G, TT, HG, V1])
        mx4 = sb("mx4", [P, H, ST, NCH])
        nmx = sb("nmx", [P, H, ST])
        m32 = sb("m32", [HG * ST, P])
        mt = sb("mt", [HG * ST, P])
        mp = sb("mp", [HG * ST, NP, P], bf16)
        pr = sb("pr", [P, 2, 2 * S])
        ones_rows = pr[0:NP].rearrange("p i s -> p (i s)").bitcast(bf16)[:, 0:TP]
        oraw = sb("oraw", [V1, 2, 2, S])
        onum = sb("onum", [P, S])
        oden = sb("oden", [P, S])
        oT = sb("oT", [P, S])
        y2 = sb("y2", [P, ST, D])
        st2 = sb("st2", [P, ST, 6])
        mv2 = sb("mv2", [P, ST, 2])
        rs2 = sb("rs2", [P, ST])
        x2 = sb("x2", [P, ST, D])
        x2T = sb("x2T", [P, S])
        lmx = sb("lmx", [P, ST])
        pe_ = sb("pe_", [P, ST, E])
        pmx = sb("pmx", [P, ST])
        psm = sb("psm", [P, ST])
        oh = sb("oh", [P, ST, E])
        okk = sb("okk", [P, ST])
        ohb = sb("ohb", [P, ST, E], bf16)
        acc = sb("acc", [P, 2, E], bf16)
        cum = sb("cum", [P, ST, E])
        pos = sb("pos", [P, ST])
        kept = sb("kept", [P, ST])
        koff = sb("koff", [P, ST])
        fac1 = sb("fac1", [P, ST])
        base = sb("base", [P, ST])
        slot_i = sb("slot_i", [P, ST], i32)
        slots = sb("slots", [P, NTOK], i32)
        fac = sb("fac", [P, NTOK])
        xall = sb("xall", [P, NTOK, D])
        NR = -(-CAP // P)
        FT = FF // P
        ks32, over = ks_raw[:].bitcast(f32), [0]

        def later(*shape):
            n, at = 1, over[0]
            for d in shape:
                n *= d
            over[0] += n
            assert over[0] <= H * TP // 2
            names = "abc"[:len(shape)]
            return ks32[:, at:at + n].rearrange(f"p ({' '.join(names)}) -> p {' '.join(names)}",
                                                **dict(zip(names, shape)))

        w1s = later(2, FF)
        w2s = later(2, FT * D).rearrange("p i (f d) -> p i f d", f=FT)
        ein = later(2, NR, D)
        einT = later(2, CAP)
        hT = later(2, FT, CAP)
        eo = later(2, NR, D)
        comb = later(NTOK, D)
        st3 = sb("st3", [P, NTOK, 6])
        mv3 = sb("mv3", [P, NTOK, 2])
        rs3 = sb("rs3", [P, NTOK])

        banks = [ctx.enter_context(nc.psum_tensor(f"bank{i}", [P, 512], f32)) for i in range(8)]
        b_sc = banks[0:2]
        b_mx = banks[2:4]
        b_o = banks[4]
        b_side = banks[5:7]
        b_fin = banks[7]

        NET = 4
        NCONST = 9

        s_win = sem("weights_loaded")
        s_const = sem("constants_made")
        s_wt = sem("weights_transposed")
        s_wtc = sem("weight_transposes_kept")
        s_etab = sem("position_table_steps")
        s_ones = sem("ones_made")
        s_onesk = sem("ones_rows_in_stack")
        s_ep = sem("position_parts_steps")
        s_ed = sem("position_parts_stored")
        s_est = sem("position_stack_loaded")
        s_zero = sem("dispatch_zeroed")
        s_x = sem("x_loaded")
        s_ctx = sem("ctx_loaded")
        s_full = [sem("side_bank0_written"), sem("side_bank1_written")]
        s_read = [sem("side_bank0_read"), sem("side_bank1_read")]
        s_sqp = sem("self_parts_steps")
        s_sqd = sem("self_parts_stored")
        s_sst = sem("self_stacks_loaded")
        s_rel = [[sem(f"relative_scores_stored_{a}{c}") for c in range(ST)] for a in range(2)]
        s_bias = [[sem(f"bias_loaded_{a}{c}") for c in range(ST)] for a in range(2)]
        s_z = sem("self_scores_maxed")
        s_nb = sem("self_bias_ready")
        s_sp = sem("self_probs_ready")
        s_sod = [sem("self_outputs_stored_even"), sem("self_outputs_stored_odd")]
        s_son = sem("self_outputs_by_row")
        s_so = sem("self_outputs_ready")
        s_x1 = sem("x1_ready")
        s_dch = sem("side_vector_steps")
        s_mv1, s_rs1 = sem("moments1_ready"), sem("deviation1_ready")
        s_mv2, s_rs2 = sem("moments2_ready"), sem("deviation2_ready")
        s_mv3, s_rs3 = sem("moments3_ready"), sem("deviation3_ready")
        s_rch = [sem(f"deviation_step_{i}") for i in range(3)]
        s_qp = sem("q_parts_steps")
        s_qd = sem("q_parts_stored")
        s_kp = sem("k_parts_steps")
        s_kd = sem("k_parts_stored")
        s_ql = [sem(f"q_stack_loaded_{g}") for g in range(G)]
        s_kl = [sem(f"k_stack_loaded_{g}") for g in range(G)]
        s_vl = [sem(f"v_loaded_{g}") for g in range(G)]
        s_x1c = sem("x1_kept")
        s_l1 = sem("max_scores_written")
        s_l1r = sem("max_scores_read")
        s_nm = sem("maxima_ready")
        s_mT = sem("maxima_transposed")
        s_m32 = sem("maxima_kept")
        s_mp = sem("maxima_parts_steps")
        s_md = sem("maxima_parts_stored")
        s_ml = [sem(f"maxima_rows_loaded_{g}") for g in range(G)]
        s_l2 = sem("scores_written")
        s_pr = sem("probs_ready")
        s_pv = sem("probs_used")
        s_oc = sem("head_outputs_kept")
        s_od = [sem("outputs_stored_even"), sem("outputs_stored_odd")]
        s_on = sem("outputs_by_row")
        s_or = sem("outputs_ready")
        s_fw = sem("finish_bank_written")
        s_fr = sem("finish_bank_read")
        s_fch = sem("finish_vector_steps")
        s_x2 = sem("x2_ready")
        s_le = sem("router_exp_ready")
        s_oh = sem("chosen_expert_ready")
        s_disp = sem("dispatch_rows_ready")
        s_x2c = sem("x2_kept")
        s_sct = sem("tokens_dispatched")
        s_ew = [sem("expert_weights_loaded_0"), sem("expert_weights_loaded_1")]
        s_ei = [sem("expert_rows_loaded_0"), sem("expert_rows_loaded_1")]
        s_et = sem("expert_rows_transposed")
        s_etc = sem("expert_rows_kept")
        s_eh = sem("expert_hidden_written")
        s_ehs = sem("expert_hidden_kept_scalar")
        s_ehv = sem("expert_hidden_kept_vector")
        s_eow = sem("expert_output_written")
        s_eo = sem("expert_output_kept")
        s_es = [sem("expert_output_stored_0"), sem("expert_output_stored_1")]
        s_cc = sem("combination_rows_filled")
        s_g = [sem(f"combination_rows_gathered_{n}") for n in range(NTOK // 4)]
        s_cch = sem("combination_vector_steps")
        s_res = sem("result_ready")
        s_out = sem("output_stored")

        s_passed = {e: sem(f"waits_passed_{n}") for e, n in (
            (mybir.EngineType.SP, "sp"), (mybir.EngineType.Pool, "pool"), (mybir.EngineType.DVE, "dve"))}

        def wait_alone(eng, s, v):
            eng.wait_ge(s, v).then_inc(s_passed[eng.engine], 1)

        def wait(eng, s, v):
            if isinstance(v, int):
                if v > 0:
                    eng.wait_ge(s, v)
            elif eng.engine in (mybir.EngineType.SP, mybir.EngineType.Pool):
                wait_alone(eng, s, v)
            else:
                eng.wait_ge(s, v)

        class Steps:
            def __init__(self, eng, s, per, alone=False):
                self.eng, self.s, self.per, self.k, self.alone = eng, s, per, 0, alone

            def link(self, b, ins):
                self.k = self.k % self.per + 1
                ins.then_inc(self.s, 1)
                if self.alone and not isinstance(b, int):
                    wait_alone(self.eng, self.s, b * self.per + self.k)
                else:
                    wait(self.eng, self.s, b * self.per + self.k)

        def split(b, src, tmp, part, steps):
            e = nc.vector if steps.eng.engine == mybir.EngineType.DVE else nc.gpsimd
            steps.link(b, e.tensor_copy(part(0), src))
            steps.link(b, e.tensor_tensor(tmp, src, part(0), ALU.subtract))
            steps.link(b, e.tensor_copy(part(1), tmp))
            steps.link(b, e.tensor_tensor(part(2), tmp, part(1), ALU.subtract))

        def split_qk(b, steps):
            split(b, qk32[:], tmp32[:, 0:2 * S], lambda a: qkp[:, a, :], steps)

        def split_q(b, steps):
            split(b, q32, tmp32[:, 0:S], lambda a: qp[:, a, :], steps)

        def first(b):
            return isinstance(b, int) and b == 0

        reads = [[u for u in range(i, NU, 2) if uses[u][2] != "sc"] for i in range(2)]

        def use_read(b, u):
            name, arg = uses[u][2:]
            if name == "sc":
                return s_z, (b * H + arg + 1) * ST
            return s_read[u % 2], b * len(reads[u % 2]) + reads[u % 2].index(u) + 1

        def wait_read(eng, b, name, arg=0):
            wait(eng, *use_read(b, index[(name, arg)]))

        def wait_full(eng, b, name, arg=0):
            u = index[(name, arg)]
            wait(eng, s_full[u % 2], b * (NU // 2) + u // 2 + 1)
            return b_side[u % 2], s_read[u % 2]

        def freed(u, earlier):
            return (u - earlier) % 2 == 0 and u - 2 >= earlier and uses[u - 2][2] != "sc"

        def wait_free(eng, b, name, arg=0):
            u = index[(name, arg)]
            if u >= 2:
                wait(eng, *use_read(b, u - 2))
            else:
                wait(eng, *use_read(b - 1, NU + u - 2))
            return b_side[u % 2], s_full[u % 2]

        def run(eng, maxima, attend, finish, side, maxt):
            def period(b, prev=True, cur=True, nxt=True):
                for s in range(H):
                    for k in range(SLOTS):
                        if k == 1 and s == 0 and prev:
                            maxt(b - 1, G - 1)
                        if k == 1 and s in (HG, 2 * HG, 3 * HG) and cur:
                            maxt(b, s // HG - 1)
                        if cur and (s, k) == (0, 0):
                            maxima(b, 0, 0)
                        if cur and (s, k) != (H - 1, SLOTS - 1):
                            maxima(b, (s * SLOTS + k + 1) // SLOTS, (k + 1) % SLOTS)
                        if nxt:
                            side(b + 1, s, k)
                        t = s % 2 * SLOTS + k
                        if s < LAG and prev and t < TT:
                            attend(b - 1, (H - LAG + s) // 2, t)
                        if s >= LAG and cur and t < TT:
                            attend(b, (s - LAG) // 2, t)
                        if prev:
                            finish(b - 1, s, k)
            for s in range(H):
                for k in range(SLOTS):
                    side(0, s, k)
            period(0, prev=False)
            with eng.Fori(1, B - 1) as b:
                period(b)
            period(B - 1, nxt=False)
            period(B, cur=False, nxt=False)

        def ahead(work, b, p, t):
            if isinstance(b, int) and (b, p, t) == (0, 0, 0):
                work(b, p, t)
            if t < TT - 1:
                work(b, p, t + 1)
            elif p < NPAIR - 1:
                work(b, p + 1, 0)
            elif not (isinstance(b, int) and b == B - 1):
                work(b + 1, 0, 0)

        def quadrant(bank, q):
            return bank[q * QUAD:q * QUAD + V1, 0:S]

        def nothing(*_):
            pass

        NDC, NFC = 2, 12
        NPC = 4
        NF = 4

        block = ctx.enter_context(nc.Block())

        @block.sync
        def _(sp):
            for i, w in enumerate([*w_self, *w_cross]):
                sp.dma_start(wraw[:, i, :], w).then_inc(s_win, 16)
            sp.dma_start(wr[:], w_router).then_inc(s_win, 16)
            sp.dma_start(posr[:], pos_emb.rearrange("(r p) d -> p r d", p=P)).then_inc(s_win, 16)
            def position_stack():
                wait(sp, s_ep, NPC)
                sp.dma_start(d_e.rearrange("a d r -> d a r"), epart[:]).then_inc(s_ed, 16)
                wait(sp, s_ed, 16)
                for c in range(NP):
                    sp.dma_start(estack[c * NP * HD:(c + 1) * NP * HD, :],
                                 d_e.rearrange("a d r -> (a d) r")).then_inc(s_est, 16)

            def ones_rows_of_stack():
                wait(sp, s_ones, 1)
                sp.dma_start(ks[KR:KM], ones_rows.unsqueeze(1).to_broadcast([NP, H, TP])).then_inc(s_onesk, 16)

            def zero_dispatch():
                wait(sp, s_const, NCONST)
                for c in range(E * CAP // (5 * P)):
                    sp.dma_start(d_disp[c * 5 * P:(c + 1) * 5 * P].rearrange("(p a) d -> p (a d)", p=P),
                                 zeros[:]).then_inc(s_zero, 16)

            def store_part(b, scratch, part, c, steps, done):
                if steps is not None:
                    wait(sp, steps, NPC * b + (1, 3, 4)[c])
                sp.dma_start(scratch[bass.ds(b, 1), c].rearrange("o d h s -> h (o d) s"), part).then_inc(done, 16)

            def load_by_first(b, rows, scratch, done):
                for c in range(NP):
                    sp.dma_start(rows[c * NP * HD:(c + 1) * NP * HD].rearrange("r h s -> r (h s)"),
                                 scratch[bass.ds(b, 1), c].rearrange("o d h s -> (o d) (h s)").unsqueeze(0)
                                 .to_broadcast([NP, HD, rows.shape[1] * rows.shape[2]])).then_inc(done, 16)

            def load_by_second(b, rows, scratch, done):
                sp.dma_start(rows.rearrange("r h s -> r (h s)"),
                             scratch[bass.ds(b, 1)].rearrange("o a d h s -> (o a d) (h s)").unsqueeze(0)
                             .to_broadcast([NP, NP * HD, rows.shape[1] * rows.shape[2]])).then_inc(done, 16)

            def stacks(b, g, q=True, kv=True):
                wait(sp, s_pv, (b - 1) * BLK + (g + 1) * HG // 2 * TT)
                if kv:
                    wait(sp, s_kd, 16 * NP * (b + 1))
                    load_by_second(b, ks[0:KR, g * HG:(g + 1) * HG, :], d_k[:, :, :, g * HG:(g + 1) * HG, :],
                                   s_kl[g])
                    for n in (2, 3):
                        wait_read(sp, b, "vp", n)
                    sp.dma_start(vb[:, g].rearrange("p t h e -> p (t h e)"),
                                 vst[:, g].rearrange("p t h e -> p (t h e)")).then_inc(s_vl[g], 16)
                if q:
                    wait(sp, s_qd, 16 * NP * (b + 1))
                    load_by_first(b, qs[0:KR, g * HG:(g + 1) * HG, :], d_q[:, :, :, g * HG:(g + 1) * HG, :],
                                  s_ql[g])

            def side(b, s, k):
                if (s, k) == (0, 0):
                    wait(sp, s_mv1, b)
                    sp.dma_start(xin[:], x[bass.ds(b, 1)].rearrange("o (t p) d -> p (o t) d", p=P)
                                 ).then_inc(s_x, 16)
                    for n in (2, 3):
                        wait_full(sp, b - 1, "ctxT", n)
                    sp.dma_start(ctxs[:, 0:TT - 1, :], ctx_in[bass.ds(b, 1), 0:(TT - 1) * P, :]
                                 .rearrange("o (t p) d -> p (o t) d", p=P)).then_inc(s_ctx, 16)
                    sp.dma_start(ctxs[:, TT - 1, :], ctx_in[bass.ds(b, 1), LAST0:TK, :]
                                 .rearrange("o p d -> (o p) d")).then_inc(s_ctx, 16)
                if isinstance(b, int) and (b, s, k) == (0, 0, 4):
                    position_stack()
                if (s, k) == (0, 4):
                    for c in range(NP):
                        store_part(b, d_sq, qkp[:, c, 0:S], c, s_sqp, s_sqd)
                        store_part(b, d_sk, qkp[:, c, S:2 * S], c, None, s_sqd)
                    wait(sp, s_sqd, 16 * 2 * NP * (b + 1))
                    for arg in (H - 2, H - 1):
                        wait_full(sp, b - 1, "sc", arg)
                    load_by_first(b, sq[:], d_sq, s_sst)
                    load_by_second(b, sk[:], d_sk, s_sst)
                if isinstance(b, int) and (b, s, k) == (0, 1, 3):
                    zero_dispatch()
                    ones_rows_of_stack()
                if (s, k) == (11, 0):
                    for c in range(NP):
                        store_part(b, d_k, kp[:, c, :], c, s_kp, s_kd)
                if (s, k) == (14, 3):
                    for c in range(NP):
                        store_part(b, d_q, qp[:, c, :], c, s_qp, s_qd)
                for g in range(G):
                    for st in range(ST):
                        if (s, k) == ((2 + g, 3), (3 + g, 0))[st]:
                            for n in (2, 3):
                                wait_read(sp, b, "qe", g * 8 + st * HG + n)
                            wait(sp, s_bias[g % 2][st], 16 * (2 * (b - 1) + g // 2 + 1))
                            sp.dma_start(d_rel[g, st], qe[:, st]).then_inc(s_rel[g % 2][st], 16)
                    if (s, k) == ((3, 1), (4, 1), (5, 1), (7, 1))[g]:
                        wait(sp, s_z, ST * (H * b + HG * (g - 1)))
                        for st in range(ST):
                            wait(sp, s_rel[g % 2][st], 16 * (2 * b + g // 2 + 1))
                            sp.dma_start(bias[:, g % 2, st],
                                         bass.AP(tensor=d_rel.tensor, offset=(g * ST + st) * P * HG * RW + P,
                                                 ap=[[HG * RW - 1, P], [RW, HG], [1, S]])
                                         ).then_inc(s_bias[g % 2][st], 16)
                if k == 0 and 5 <= s < 5 + H // 2:
                    p = s - 5
                    wait_read(sp, b, "pv", p)
                    store(b, soraw, d_so, p, s_sod)
                    if p == H // 2 - 1:
                        wait(sp, s_so, b)
                        spread(b, sonum, soden, d_so, s_sod, s_son)
                if (s, k) in ((12, 4), (13, 6)):
                    stacks(b, s - 12, q=False)
                if (s, k) in ((15, 3), (15, 5)):
                    stacks(b, (k - 3) // 2, kv=False)

            def store(b, raw, scratch, p, done):
                sp.dma_start(scratch[bass.ds(b, 1), 2 * p:2 * p + 2].rearrange("o h e s -> e (o h) s"),
                             raw[:, p % 2]).then_inc(done[p % 2], 16)

            def spread(b, num, den, scratch, stored, done):
                for i in range(2):
                    wait(sp, stored[i], 16 * H // 4 * (b + 1))
                sp.dma_start(num[:], scratch[bass.ds(b, 1), :, 0:HD].rearrange("o h d s -> (o h) d s")
                             ).then_inc(done, 16)
                sp.dma_start(den[:], scratch[bass.ds(b, 1), :, HD].rearrange("o h s -> (o h) s").unsqueeze(1)
                             .to_broadcast([H, HD, S])).then_inc(done, 16)

            def attend(b, p, t):
                if t == 4 and p:
                    wait(sp, s_oc, NPAIR * b + p)
                    store(b, oraw, d_o, p - 1, s_od)

            def maxima(b, s, k):
                if (s, k) == (1, SLOTS - 1):
                    stacks(b, 2)
                if (s, k) == (5, SLOTS - 1):
                    stacks(b, 3)
                if k == 5 and s in (HG, 2 * HG, 3 * HG):
                    rows(b, s // HG - 1)

            def finish(b, s, k):
                if (s, k) == (0, 5):
                    rows(b, G - 1)
                if isinstance(b, int) and (b, s, k) == (B - 1, 1, 0):
                    wait(sp, s_pv, (B - 1) * BLK + G // 2 * HG // 2 * TT)
                    for e in range(2):
                        load_weights(e, e)
                if (s, k) == (6, 2):
                    wait(sp, s_oc, NPAIR * (b + 1))
                    store(b, oraw, d_o, H // 2 - 1, s_od)
                    wait(sp, s_or, b)
                    spread(b, onum, oden, d_o, s_od, s_on)

            def rows(b, g):
                wait(sp, s_md, 16 * (G * b + g + 1))
                sp.dma_start(qs[KR:KM, g * HG:(g + 1) * HG, :].rearrange("r h s -> r (h s)"),
                             d_m[bass.ds(b, 1), :, g * HG:(g + 1) * HG]
                             .rearrange("o c h t s -> (o c) (h t s)")).then_inc(s_ml[g], 16)

            def load_weights(i, e):
                sp.dma_start(w1s[:, i, :], w1[bass.ds(e, 1)].rearrange("o d f -> (o d) f")
                             ).then_inc(s_ew[i], 16)
                sp.dma_start(w2s[:, i], w2[bass.ds(e, 1)].rearrange("o (t p) d -> p (o t) d", p=P)
                             ).then_inc(s_ew[i], 16)

            def load_rows(i, e):
                for r in range(NR):
                    n = min(P, CAP - r * P)
                    sp.dma_start(ein[0:n, i, r, :], d_disp[bass.ds(e * CAP + r * P, n), :]
                                 ).then_inc(s_ei[i], 16)

            run(sp, maxima, attend, finish, side, nothing)

            wait(sp, s_sct, 16 * NTOK)
            for e in range(2):
                load_rows(e, e)
            with sp.Fori(1, E // 2) as e2:
                for i in range(2):
                    wait(sp, s_et, e2 * 2 + i - 1)
                    load_rows(i, e2 * 2 + i)
                    wait(sp, s_eow, e2 * 2 + i - 1)
                    load_weights(i, e2 * 2 + i)
            for j in range(0, NTOK, 4):
                wait(sp, s_res, j // 4 + 1)
                sp.dma_start(out.rearrange("b (t p) d -> p (b t) d", p=P)[:, j:j + 4, :],
                             comb[:, j:j + 4, :]).then_inc(s_out, 16)
            wait(sp, s_out, 16 * NTOK // 4)

        @block.gpsimd
        def _(pool):
            nc.gpsimd.memset(ident[:], 0.0).then_inc(s_const, 1)
            nc.gpsimd.memset(upper[:], 1.0).then_inc(s_const, 1)
            nc.gpsimd.memset(vmask[:], 1.0).then_inc(s_const, 1)
            nc.gpsimd.memset(zeros[:], 0.0).then_inc(s_const, 1)
            nc.gpsimd.iota(rank[:], pattern=[[-1, E]], base=E, channel_multiplier=0,
                           allow_small_or_imprecise_dtypes=True).then_inc(s_const, 1)
            wait(pool, s_const, 5)
            nc.gpsimd.affine_select(out=ident[:], in_=ident[:], compare_op=ALU.not_equal, fill=1.0, base=0,
                                    pattern=[[-1, P]], channel_multiplier=1).then_inc(s_const, 1)
            nc.gpsimd.affine_select(out=upper[:], in_=upper[:], compare_op=ALU.is_ge, fill=0.0, base=0,
                                    pattern=[[1, P]], channel_multiplier=-1).then_inc(s_const, 1)
            nc.gpsimd.affine_select(out=vmask[:], in_=vmask[:], compare_op=ALU.is_ge, fill=0.0, base=-OVER,
                                    pattern=[[0, 1]], channel_multiplier=1).then_inc(s_const, 1)
            nc.gpsimd.memset(minus_half[:], -0.5)
            nc.gpsimd.memset(ones_bf[:], 1.0).then_inc(s_const, 1)

            def deviation(n, mv, rs, step, done):
                nc.gpsimd.tensor_scalar(rs, mv, EPS, None, ALU.add).then_inc(step, 1)
                wait(pool, step, n + 1)
                nc.gpsimd.tensor_tensor(rs, rs, minus_half[:, 0:rs.shape[1]], ALU.pow).then_inc(done, 1)

            q_steps = Steps(pool, s_qp, NPC)
            k_steps, m_steps = Steps(pool, s_kp, NPC), Steps(pool, s_mp, NPC)

            def side(b, s, k):
                if (s, k) == (8, 1):
                    for n in (2, 3):
                        wait_read(pool, b, "kp", n)
                    wait(pool, s_sqd, 16 * 2 * NP * (b + 1))
                    split(b, k32[:], tmp32[:], lambda a: kp[:, a, :], k_steps)
                if (s, k) == (13, 4):
                    wait(pool, s_mv1, b + 1)
                    deviation(b, mv1[:, :, 1], rs1[:], s_rch[0], s_rs1)
                if (s, k) == (14, 2) and not first(b):
                    wait_read(pool, b, "cq")
                    wait(pool, s_kd, 16 * NP * (b + 1))
                    split_q(b, q_steps)
                if (s, k) == (14, 2):
                    wait(pool, s_x1, b + 1)
                    nc.gpsimd.tensor_copy(xall[:, bass.ds(b * ST, ST), :], x1[:]).then_inc(s_x1c, 1)

            def maxt(b, g):
                wait(pool, s_m32, G * b + g + 1)
                wait(pool, s_md, 16 * (G * b + g))
                split(G * b + g, m32[:], mt[:], lambda a: mp[:, a, :], m_steps)
                pool.dma_start(d_m[bass.ds(b, 1), :, g * HG:(g + 1) * HG].rearrange("o c h t s -> (h t) (o c) s"),
                               mp[:]).then_inc(s_md, 16)

            def finish(b, s, k):
                if (s, k) == (7, 6):
                    wait(pool, s_mv2, b + 1)
                    deviation(b, mv2[:, :, 1], rs2[:], s_rch[1], s_rs2)
                if (s, k) == (10, 6):
                    wait(pool, s_disp, b + 1)
                    wait(pool, s_zero, 16 * (E * CAP // (5 * P)))
                    for st in range(ST):
                        nc.gpsimd.indirect_dma_start(
                            out=d_disp, out_offset=bass.IndirectOffsetOnAxis(ap=slot_i[:, st:st + 1], axis=0),
                            in_=x2[:, st, :], in_offset=None, bounds_check=E * CAP - 1,
                            oob_is_err=False).then_inc(s_sct, 16)
                    nc.gpsimd.tensor_copy(xall[:, bass.ds(b * ST, ST), :], x2[:])
                    nc.gpsimd.tensor_copy(slots[:, bass.ds(b * ST, ST)], slot_i[:])
                    nc.gpsimd.tensor_copy(fac[:, bass.ds(b * ST, ST)], fac1[:]).then_inc(s_x2c, 1)
                    wait(pool, s_sct, 16 * ST * (b + 1))

            run(pool, nothing, nothing, finish, side, maxt)

            wait(pool, s_x2c, B)
            wait(pool, s_pv, B * BLK)
            nc.gpsimd.tensor_copy(comb[:].rearrange("p t d -> p (t d)"),
                                  xall[:].rearrange("p t d -> p (t d)")).then_inc(s_cc, 1)
            wait(pool, s_cc, 1)

            def experts(e2):
                for i in range(2):
                    e = e2 * 2 + i
                    wait(pool, s_eo, 2 * (e + 1))
                    for r in range(NR):
                        n = min(P, CAP - r * P)
                        pool.dma_start(d_eout[bass.ds(e * CAP + r * P, n), :], eo[0:n, i, r, :]
                                       ).then_inc(s_es[i], 16)

            experts(0)
            with pool.Fori(1, E // 2) as e2:
                experts(e2)
            for i in range(2):
                wait(pool, s_es[i], 16 * NR * E // 2)
            def gather(n):
                for j in range(4 * n, 4 * n + 4):
                    nc.gpsimd.indirect_dma_start(
                        out=comb[:, j, :], out_offset=None, in_=d_eout,
                        in_offset=bass.IndirectOffsetOnAxis(ap=slots[:, j:j + 1], axis=0),
                        bounds_check=E * CAP - 1, oob_is_err=False).then_inc(s_g[n], 16)

            gather(0)
            gather(1)
            for n in range(NTOK // 4):
                if n + 2 < NTOK // 4:
                    gather(n + 2)
                wait(pool, s_mv3, n + 1)
                deviation(n, mv3[:, 4 * n:4 * n + 4, 1], rs3[:, 4 * n:4 * n + 4], s_rch[2], s_rs3)

        @block.scalar
        def _(act):
            for w in range(2):
                act.wait_ge(s_wt, w + 1)
                nc.scalar.copy(wT[:, 4 * w:4 * w + 4, :].rearrange("p w d -> p (w d)"),
                               banks[w][:, :]).then_inc(s_wtc, 1)

            def keep(b, name, arg, dst, n):
                bank, read = wait_full(act, b, name, arg)
                nc.scalar.copy(dst, bank[:, 0:n]).then_inc(read, 1)

            def side(b, s, k):
                for name, arg in slot_uses.get((s, k), ()):
                    if name == "xT":
                        keep(b, name, arg, xT[:], S)
                    if name == "qk":
                        wait(act, s_qp, NPC * b)
                        keep(b, name, arg, qk32[:], 2 * S)
                    if name == "ctxT":
                        bank, read = wait_full(act, b, name, arg)
                        if arg < 3:
                            nc.scalar.copy(ctxT[:, arg * 4 * P:(arg + 1) * 4 * P], bank[:, :]).then_inc(read, 1)
                        else:
                            nc.scalar.copy(ctxT[:, (TT - 1) * P:TK], bank[:, OVER:P]).then_inc(read, 1)
                    if name == "kp":
                        keep(b, name, arg, k32[:, C0[arg]:C0[arg + 1]], C0[arg + 1] - C0[arg])
                    if name == "qe":
                        g, st, n = arg // 8, arg % 8 // HG, arg % HG
                        if n == 0:
                            wait(act, s_rel[(g - 1) % 2][st], 16 * (2 * b + (g - 1) // 2 + 1))
                        keep(b, name, arg, qe[:, st, n * RW:(n + 1) * RW], RW)
                    if name == "x1T":
                        keep(b, name, arg, x1T[:], S)
                    if name == "cq":
                        keep(b, name, arg, q32, S)
                if (3 <= s <= 10 and k == 6) or (4 <= s <= 11 and k == 0):
                    h = 2 * (s - 3) if k else 2 * (s - 4) + 1
                    act.wait_ge(s_nb, H * b + h + 1)
                    for st in range(ST):
                        nc.scalar.activation(zp[:, h % 2, st, :], zp[:, h % 2, st, :], ACT.Exp,
                                             bias=snb[:, h, st:st + 1], scale=SCALE).then_inc(s_sp, 1)

            def attend(b, p, t):
                ahead(probs, b, p, t)
                if t == 2 and p:
                    keep_pair(b, p - 1)

            def probs(b, p, t):
                i = p * TT + t
                n = b * BLK + i
                act.wait_ge(s_l2, n + 1)
                wait(act, s_pv, n - 1)
                nc.scalar.activation(pr[:, i % 2, :], b_sc[i % 2][:, :], ACT.Exp, scale=SCALE).then_inc(s_pr, 1)

            def keep_pair(b, p):
                act.wait_ge(s_pv, b * BLK + (p + 1) * TT)
                wait(act, s_od[p % 2], 16 * (NPAIR // 2 * b + p // 2))
                for j in range(2):
                    last = nc.scalar.copy(oraw[:, p % 2, j, :], quadrant(b_o, 2 * (p % 2) + j))
                last.then_inc(s_oc, 1)

            def maxt(b, g):
                act.wait_ge(s_mT, G * b + g + 1)
                wait(act, s_mp, NPC * (G * b + g))
                nc.scalar.copy(m32[:], b_fin[0:HG * ST, 0:P]).then_inc(s_m32, 1)

            def finish(b, s, k):
                if (s, k) == (6, 0):
                    keep_pair(b, NPAIR - 1)
                if (s, k) == (8, 4):
                    act.wait_ge(s_fw, NF * b + 2)
                    nc.scalar.copy(x2T[:], b_fin[:, 0:S]).then_inc(s_fr, 1)
                if (s, k) == (9, 1):
                    act.wait_ge(s_fr, NF * b + 3)
                    nc.scalar.activation(pe_[:], pe_[:], ACT.Exp).then_inc(s_le, 1)

            run(act, nothing, attend, finish, side, maxt)

            def experts(e2):
                for i in range(2):
                    e = e2 * 2 + i
                    act.wait_ge(s_et, e + 1)
                    nc.scalar.copy(einT[:, i, :], banks[0][:, 0:CAP]).then_inc(s_etc, 1)
                    for f in range(0, FT, 2):
                        act.wait_ge(s_eh, e * FT + f + 1)
                        nc.scalar.activation(hT[:, i, f, :], banks[1 + f][:, 0:CAP], ACT.Relu).then_inc(s_ehs, 1)

            experts(0)
            with act.Fori(1, E // 2) as e2:
                experts(e2)
        @block.vector
        def _(dve):
            self_steps = Steps(dve, s_sqp, NPC)
            dch, fch = Steps(dve, s_dch, NDC, alone=True), Steps(dve, s_fch, NFC, alone=True)
            dve.wait_ge(s_const, NCONST)
            dve.wait_ge(s_wt, 3)
            pT_neg, pT_pos = banks[2][0:HD, P:2 * P], banks[2][0:HD, 0:P]
            nc.vector.tensor_scalar(etab[:, P:2 * P], pT_neg, 2.0, None, ALU.mult).then_inc(s_etab, 1)
            nc.vector.tensor_scalar(etab[:, 2 * P:3 * P], pT_pos, 2.0, None, ALU.mult).then_inc(s_etab, 1)
            dve.wait_ge(s_etab, 2)
            nc.vector.tensor_copy(etab[:, 0:P], etab[:, P:P + 1].to_broadcast([HD, P])).then_inc(s_etab, 1)
            nc.vector.tensor_copy(etab[:, 3 * P:4 * P],
                                  etab[:, 3 * P - 1:3 * P].to_broadcast([HD, P])).then_inc(s_etab, 1)
            dve.wait_ge(s_etab, NET)
            split(0, etab[:], etmp[:], lambda a: epart[:, a, :], Steps(dve, s_ep, NPC))
            nc.vector.memset(ones_rows, 1.0)
            nc.vector.memset(sv[:, :, :, HD], 1.0)
            nc.vector.memset(k32[:, TK:TP], 0.0)
            nc.vector.memset(acc[:], 0.0)
            nc.vector.memset(vst[:, :, :, :, HD], 1.0).then_inc(s_ones, 1)
            dve.wait_ge(s_ones, 1)
            nc.vector.tensor_scalar(vst[:, :, TT - 1, :, HD], vst[:, :, TT - 1, :, HD],
                                    vmask[:, 0:1], None, ALU.mult)

            def moments(b, steps, y, stats, mv, done, tiles):
                for t in tiles:
                    last = nc.vector.bn_stats(stats[:, t, :], y[:, t, :])
                steps.link(b, last)
                for t in tiles:
                    last = nc.vector.bn_aggr(mv[:, t, :], stats[:, t, :])
                last.then_inc(done, 1)

            def normalize(y, mv, rs, dst, tiles):
                for t in tiles:
                    last = nc.vector.tensor_scalar(dst[:, t, :], y[:, t, :], mv[:, t, 0:1], rs[:, t:t + 1],
                                                   ALU.subtract, ALU.mult)
                return last

            def side(b, s, k):
                if (s, k) == (0, 3):
                    wait_read(dve, b, "qk")
                    wait(dve, s_qd, 16 * NP * b)
                    split_qk(b, self_steps)
                if (s, k) == (14, 2) and first(b):
                    wait_read(dve, b, "cq")
                    wait(dve, s_kd, 16 * NP)
                    split_q(b, Steps(dve, s_qp, NPC))
                if (s, k) == (13, 2):
                    dve.wait_ge(s_son, 32 * (b + 1))
                    dch.link(b, nc.vector.reciprocal(soden[:], soden[:]))
                    nc.vector.tensor_tensor(soT[:], sonum[:], soden[:], ALU.mult).then_inc(s_so, 1)
                for name, arg in slot_uses.get((s, k), ()):
                    if name == "v":
                        bank, read = wait_full(dve, b, name, arg)
                        nc.vector.tensor_copy(sv[:, :, :, 0:HD],
                                              bank[:, 0:ST * D].rearrange("p (t h d) -> p t h d", t=ST, h=H)
                                              ).then_inc(read, 1)
                    if name == "vp":
                        wait(dve, s_vl[G - 1], 16 * b)
                        bank, read = wait_full(dve, b, name, arg)
                        for t in range(4 * arg, min(4 * arg + 4, TT)):
                            src = bank[:, (t % 4) * D:(t % 4 + 1) * D].rearrange("p (g h d) -> p g h d", g=G, h=HG)
                            if t < TT - 1:
                                last = nc.vector.tensor_copy(vst[:, :, t, :, 0:HD], src)
                            else:
                                last = nc.vector.tensor_scalar(vst[:, :, t, :, 0:HD], src, vmask[:, 0:1], None,
                                                               ALU.mult)
                        last.then_inc(read, 1)
                    if name == "sc":
                        h, g = arg, arg // HG
                        bank, _ = wait_full(dve, b, name, arg)
                        if h >= 2:
                            wait_full(dve, b, "pt", h - 2)
                        if h % HG:
                            wait_alone(dve, s_bias[g % 2][0], 16 * (2 * b + g // 2 + 1))
                        for st in range(ST):
                            if h % HG == 0:
                                wait_alone(dve, s_bias[g % 2][st], 16 * (2 * b + g // 2 + 1))
                            nc.vector.tensor_tensor_reduce(
                                out=zp[:, h % 2, st, :], in0=bank[:, st * S:(st + 1) * S],
                                in1=bias[:, g % 2, st, h % HG, :], scale=1.0, scalar=NEG, op0=ALU.add,
                                op1=ALU.max, accum_out=smx[:, h, st:st + 1]).then_inc(s_z, 1)
                        dve.wait_ge(s_z, ST * (H * b + h + 1))
                        nc.vector.tensor_scalar(snb[:, h, :], smx[:, h, :], -SCALE, None, ALU.mult).then_inc(s_nb, 1)
                    if name == "pt":
                        bank, read = wait_full(dve, b, name, arg)
                        if arg >= 2:
                            wait_full(dve, b, "pv", arg // 2 - 1)
                        nc.vector.tensor_copy(pT[:, arg % 2, :], bank[:, :]).then_inc(read, 1)
                    if name == "pv":
                        bank, read = wait_full(dve, b, name, arg)
                        wait(dve, s_sod[arg % 2], 16 * (H // 4 * b + arg // 2))
                        for n in range(2):
                            last = nc.vector.tensor_copy(soraw[:, arg % 2, n, :], quadrant(bank, n))
                        last.then_inc(read, 1)
                    if name == "wp":
                        bank, read = wait_full(dve, b, name, arg)
                        nc.vector.tensor_tensor(y1[:].rearrange("p t d -> p (t d)"), bank[:, 0:ST * D],
                                                xin[:].rearrange("p t d -> p (t d)"), ALU.add).then_inc(read, 1)
                        wait_read(dve, b, "wp")
                        moments(b, dch, y1, st1, mv1, s_mv1, range(ST))
                if (s, k) == (13, 5):
                    dve.wait_ge(s_rs1, b + 1)
                    wait(dve, s_x1c, b)
                    normalize(y1, mv1, rs1, x1, range(ST)).then_inc(s_x1, 1)

            def maxima(b, h, k):
                for i in ((k,) if k < SLOTS - 1 else (k, k + 1)):
                    st, c = i // NCH, i % NCH
                    dve.wait_ge(s_l1, NL1 * b + 8 * h + i + 1)
                    nc.vector.tensor_reduce(mx4[:, h, st, c:c + 1], b_mx[i % 2][:, 0:C0[c + 1] - C0[c]], AX,
                                            ALU.max).then_inc(s_l1r, 1)
                if k == SLOTS - 1 and h % HG == HG - 1:
                    g = h // HG
                    dve.wait_ge(s_l1r, NL1 * b + 8 * h + 8)
                    nc.vector.tensor_reduce(nmx[:, g * HG:(g + 1) * HG, :], mx4[:, g * HG:(g + 1) * HG], AX,
                                            ALU.max, negate=True).then_inc(s_nm, 1)

            def finish(b, s, k):
                if (s, k) == (7, 1):
                    dve.wait_ge(s_on, 32 * (b + 1))
                    fch.link(b, nc.vector.reciprocal(oden[:], oden[:]))
                    nc.vector.tensor_tensor(oT[:], onum[:], oden[:], ALU.mult).then_inc(s_or, 1)
                if (s, k) == (7, 5):
                    dve.wait_ge(s_fw, NF * b + 1)
                    dve.wait_ge(s_x1c, b + 1)
                    nc.vector.tensor_tensor(y2[:], b_fin[:, 0:ST * D].rearrange("p (t d) -> p t d", t=ST),
                                            xall[:, bass.ds(b * ST, ST), :], ALU.add).then_inc(s_fr, 1)
                    dve.wait_ge(s_fr, NF * b + 1)
                    moments(b, fch, y2, st2, mv2, s_mv2, range(ST))
                if (s, k) == (8, 1):
                    dve.wait_ge(s_rs2, b + 1)
                    normalize(y2, mv2, rs2, x2, range(ST)).then_inc(s_x2, 1)
                if (s, k) == (9, 0):
                    dve.wait_ge(s_fw, NF * b + 3)
                    logits = b_fin[:, 0:ST * E].rearrange("p (t e) -> p t e", t=ST)
                    fch.link(b, nc.vector.tensor_reduce(lmx[:], logits, AX, ALU.max))
                    nc.vector.tensor_tensor(pe_[:], logits, lmx[:].unsqueeze(2).to_broadcast([P, ST, E]),
                                            ALU.subtract).then_inc(s_fr, 1)
                if (s, k) == (9, 3):
                    dve.wait_ge(s_le, b + 1)
                    nc.vector.tensor_reduce(pmx[:], pe_[:], AX, ALU.max)
                    fch.link(b, nc.vector.tensor_reduce(psm[:], pe_[:], AX, ALU.add))
                    fch.link(b, nc.vector.tensor_tensor(oh[:], pe_[:], pmx[:].unsqueeze(2).to_broadcast([P, ST, E]),
                                                        ALU.is_equal))
                    fch.link(b, nc.vector.tensor_tensor(oh[:], oh[:],
                                                        rank[:].unsqueeze(1).to_broadcast([P, ST, E]), ALU.mult))
                if (s, k) == (9, 5):
                    nc.vector.reciprocal(psm[:], psm[:])
                    fch.link(b, nc.vector.tensor_reduce(okk[:], oh[:], AX, ALU.max))
                    nc.vector.tensor_tensor(fac1[:], pmx[:], psm[:], ALU.mult)
                    nc.vector.tensor_tensor(ohb[:], oh[:], okk[:].unsqueeze(2).to_broadcast([P, ST, E]),
                                            ALU.is_equal).then_inc(s_oh, 1)
                if (s, k) == (10, 2):
                    dve.wait_ge(s_fw, NF * b + 4)
                    nc.vector.tensor_tensor(cum[:], b_fin[:, 0:ST * E].rearrange("p (t e) -> p t e", t=ST), ohb[:],
                                            ALU.mult).then_inc(s_fr, 1)
                if (s, k) == (10, 3):
                    dve.wait_ge(s_fr, NF * b + 4)
                    nc.vector.tensor_reduce(pos[:], cum[:], AX, ALU.add)
                    fch.link(b, nc.vector.tensor_tensor(acc[:, 0], acc[:, 0], ohb[:, 0, :], ALU.add))
                    nc.vector.tensor_scalar(kept[:], pos[:], float(CAP), None, ALU.is_le)
                    nc.vector.tensor_scalar(base[:], okk[:], -float(CAP), float(E * CAP - 1), ALU.mult, ALU.add)
                if (s, k) == (10, 4):
                    fch.link(b, nc.vector.tensor_tensor(acc[:, 0], acc[:, 0], ohb[:, 1, :], ALU.add))
                    nc.vector.tensor_tensor(base[:], base[:], pos[:], ALU.add)
                if (s, k) == (10, 5):
                    fch.link(b, nc.vector.tensor_scalar(koff[:], kept[:], -OOB, OOB, ALU.mult, ALU.add))
                    nc.vector.tensor_scalar(fac1[:], fac1[:], -1.0, None, ALU.add)
                    fch.link(b, nc.vector.tensor_tensor(slot_i[:], base[:], koff[:], ALU.add))
                    fch.link(b, nc.vector.tensor_tensor(fac1[:], fac1[:], kept[:], ALU.mult))
                    nc.vector.tensor_scalar(fac1[:], fac1[:], 1.0, None, ALU.add).then_inc(s_disp, 1)

            run(dve, maxima, nothing, finish, side, nothing)

            def experts(e2):
                for i in range(2):
                    e = e2 * 2 + i
                    for f in range(1, FT, 2):
                        dve.wait_ge(s_eh, e * FT + f + 1)
                        nc.vector.tensor_scalar(hT[:, i, f, :], banks[1 + f][:, 0:CAP], 0.0, None,
                                                ALU.max).then_inc(s_ehv, 1)
                    wait(dve, s_es[i], 16 * NR * e2)
                    dve.wait_ge(s_eow, e + 1)
                    full = CAP // P
                    nc.vector.tensor_copy(eo[:, i, 0:full, :],
                                          banks[5 + i][:, 0:full * D].rearrange("p (t d) -> p t d", t=full)
                                          ).then_inc(s_eo, 1)
                    n = CAP - full * P
                    nc.vector.tensor_copy(eo[0:n, i, full, :], banks[5 + i][0:n, full * D:(full + 1) * D]
                                          ).then_inc(s_eo, 1)

            experts(0)
            with dve.Fori(1, E // 2) as e2:
                experts(e2)
            cch = Steps(dve, s_cch, 2)

            def result(n):
                dve.wait_ge(s_rs3, n + 1)
                normalize(comb, mv3, rs3, comb, range(4 * n, 4 * n + 4)).then_inc(s_res, 1)

            for n in range(NTOK // 4):
                tiles = range(4 * n, 4 * n + 4)
                dve.wait_ge(s_g[n], 16 * 4)
                for t in tiles:
                    last = nc.vector.scalar_tensor_tensor(comb[:, t, :], comb[:, t, :], fac[:, t:t + 1],
                                                          xall[:, t, :], ALU.mult, ALU.add)
                cch.link(n, last)
                moments(n, cch, comb, st3, mv3, s_mv3, tiles)
                if n:
                    result(n - 1)
            result(NTOK // 4 - 1)

        @block.tensor
        def _(pe):
            pe.wait_ge(s_const, NCONST)
            pe.wait_ge(s_win, 16 * 10)
            for w in range(8):
                last = nc.tensor.transpose(banks[w // 4][:, (w % 4) * D:(w % 4 + 1) * D], wraw[:, w, :], ident[:])
                if w % 4 == 3:
                    last.then_inc(s_wt, 1)
            for r in range(2):
                last = nc.tensor.transpose(banks[2][0:HD, r * P:(r + 1) * P], posr[:, r, :], ident[:])
            last.then_inc(s_wt, 1)
            pe.wait_ge(s_wtc, 2)

            def mm(dst, lhsT, rhs, start=True, stop=True, shared=False):
                return nc.tensor.matmul(dst, lhsT, rhs, start=start, stop=stop, skip_group_check=shared)

            def product(b, name, arg):
                if name == "xT":
                    pe.wait_ge(s_x, 16 * (b + 1))
                if name == "ctxT" and arg == 0:
                    pe.wait_ge(s_ctx, 32 * (b + 1))
                if name == "qk":
                    wait_read(pe, b, "xT")
                if name == "kp" and arg == 0:
                    for n in (2, 3):
                        wait_read(pe, b, "ctxT", n)
                if name == "qe" and arg == 0:
                    pe.wait_ge(s_sst, 16 * (1 + NP) * (b + 1))
                    pe.wait_ge(s_est, 16 * NP)
                if name == "pt":
                    pe.wait_ge(s_sp, ST * (H * b + arg + 1))
                if name == "pv":
                    first, second = index[("pt", 2 * arg)], index[("pt", 2 * arg + 1)]
                    if (second - first) % 2 and not freed(index[(name, arg)], first):
                        wait_read(pe, b, "pt", 2 * arg)
                    if not freed(index[(name, arg)], second):
                        wait_read(pe, b, "pt", 2 * arg + 1)
                if name == "wp":
                    pe.wait_ge(s_so, b + 1)
                if name == "x1T":
                    pe.wait_ge(s_x1, b + 1)
                if name == "cq":
                    wait_read(pe, b, "x1T")
                bank, full = wait_free(pe, b, name, arg)
                if name == "xT":
                    for st in range(ST):
                        last = nc.tensor.transpose(bank[:, st * P:(st + 1) * P], xin[:, st, :], ident[:])
                if name == "qk":
                    for i, w in enumerate((WQ, WK)):
                        last = mm(bank[:, i * S:(i + 1) * S], wT[:, w, :], xT[:])
                if name == "v":
                    for st in range(ST):
                        last = mm(bank[:, st * D:(st + 1) * D], xT[:, st * P:(st + 1) * P], wT[:, WV, :])
                if name == "ctxT":
                    for t in range(4 * arg, min(4 * arg + 4, TT)):
                        last = nc.tensor.transpose(bank[:, (t % 4) * P:(t % 4 + 1) * P], ctxs[:, t, :], ident[:])
                if name == "kp":
                    last = mm(bank[:, 0:C0[arg + 1] - C0[arg]], wT[:, XK, :], ctxT[:, C0[arg]:C0[arg + 1]])
                if name == "vp":
                    for t in range(4 * arg, min(4 * arg + 4, TT)):
                        t0 = t * P if t < TT - 1 else LAST0
                        last = mm(bank[:, (t % 4) * D:(t % 4 + 1) * D], ctxT[:, t0:t0 + P], wT[:, XV, :])
                if name == "qe":
                    g, st, n = arg // 8, arg % 8 // HG, arg % HG
                    e0 = (ST - 1 - st) * P
                    last = mm(bank[:, 0:RW], sq[:, g * HG + n, st * P:(st + 1) * P], estack[:, e0:e0 + RW])
                if name == "sc":
                    for st in range(ST):
                        last = mm(bank[:, st * S:(st + 1) * S], sq[:, arg, st * P:(st + 1) * P], sk[:, arg, :])
                if name == "pt":
                    for st in range(ST):
                        for jt in range(ST):
                            last = nc.tensor.transpose(bank[:, jt * S + st * P:jt * S + (st + 1) * P],
                                                       zp[:, arg % 2, st, jt * P:(jt + 1) * P], ident[:])
                if name == "pv":
                    for jt in range(ST):
                        for n in range(2):
                            last = mm(quadrant(bank, n), sv[:, jt, 2 * arg + n, :],
                                      pT[:, n, jt * S:(jt + 1) * S], start=jt == 0, stop=jt == ST - 1, shared=True)
                if name == "wp":
                    for st in range(ST):
                        last = mm(bank[:, st * D:(st + 1) * D], soT[:, st * P:(st + 1) * P], wT[:, WP, :])
                if name == "x1T":
                    for st in range(ST):
                        last = nc.tensor.transpose(bank[:, st * P:(st + 1) * P], x1[:, st, :], ident[:])
                if name == "cq":
                    last = mm(bank[:, 0:S], wT[:, XQ, :], x1T[:])
                last.then_inc(full, 1)

            def side(b, s, k):
                for name, arg in slot_uses.get((s, k), ()):
                    product(b, name, arg)

            def maxima(b, h, k):
                if isinstance(b, int) and (b, h, k) == (0, 0, 0):
                    pe.wait_ge(s_etab, NET)
                if k == 0 and h % HG == 0:
                    g = h // HG
                    pe.wait_ge(s_kl[g], 16 * (b + 1))
                    pe.wait_ge(s_ql[g], 16 * NP * (b + 1))
                for i in ((k,) if k < SLOTS - 1 else (k, k + 1)):
                    st, c = i // NCH, i % NCH
                    wait(pe, s_l1r, NL1 * b + 8 * h + i - 1)
                    mm(b_mx[i % 2][:, 0:C0[c + 1] - C0[c]], qs[0:KR, h, st * P:(st + 1) * P],
                       ks[0:KR, h, C0[c]:C0[c + 1]]).then_inc(s_l1, 1)

            def maxt(b, g):
                pe.wait_ge(s_nm, G * b + g + 1)
                wait(pe, s_m32, G * b + g)
                if g in (1, 2):
                    wait(pe, s_fr, NF * (b - 1) + (1 if g == 1 else NF))
                nc.tensor.transpose(b_fin[0:HG * ST, 0:P],
                                    nmx[:, g * HG:(g + 1) * HG, :].rearrange("p h t -> p (h t)"),
                                    ident[:]).then_inc(s_mT, 1)

            def scores(b, p, t):
                i = p * TT + t
                n = b * BLK + i
                g = 2 * p // HG
                if isinstance(b, int) and (b, p, t) == (0, 0, 0):
                    pe.wait_ge(s_onesk, 16)
                if t == 0 and 2 * p % HG == 0:
                    pe.wait_ge(s_ml[g], 16 * (b + 1))
                wait(pe, s_pr, n - 1)
                t0 = t * P if t < TT - 1 else LAST0
                for j in range(2):
                    last = mm(b_sc[i % 2][:, j * S:(j + 1) * S], ks[:, 2 * p + j, t0:t0 + P], qs[:, 2 * p + j, :])
                last.then_inc(s_l2, 1)

            def attend(b, p, t):
                i = p * TT + t
                n = b * BLK + i
                g = 2 * p // HG
                ahead(scores, b, p, t)
                if t == 0:
                    wait(pe, s_oc, NPAIR * b + p - 1)
                if t == 0 and 2 * p % HG == 0:
                    pe.wait_ge(s_vl[g], 16 * (b + 1))
                pe.wait_ge(s_pr, n + 1)
                for j in range(2):
                    last = mm(quadrant(b_o, 2 * (p % 2) + j), vb[:, g, t, (2 * p + j) % HG, :],
                              pr[:, i % 2, j * S:(j + 1) * S], start=t == 0, stop=t == TT - 1, shared=True)
                last.then_inc(s_pv, 1)

            def finish(b, s, k):
                def bank_free(j, maxima_done):
                    if j:
                        wait(pe, s_fr, NF * b + j)
                    if maxima_done is not None:
                        wait(pe, s_m32, maxima_done)
                if (s, k) == (7, 3):
                    pe.wait_ge(s_or, b + 1)
                    bank_free(0, last_maxt(b, 1))
                    for st in range(ST):
                        last = mm(b_fin[:, st * D:(st + 1) * D], oT[:, st * P:(st + 1) * P], wT[:, XO, :])
                    last.then_inc(s_fw, 1)
                if (s, k) == (8, 3):
                    pe.wait_ge(s_x2, b + 1)
                    bank_free(1, last_maxt(b, 2))
                    for st in range(ST):
                        last = nc.tensor.transpose(b_fin[:, st * P:(st + 1) * P], x2[:, st, :], ident[:])
                    last.then_inc(s_fw, 1)
                if (s, k) == (8, 6):
                    bank_free(2, None)
                    for st in range(ST):
                        last = mm(b_fin[:, st * E:(st + 1) * E], x2T[:, st * P:(st + 1) * P], wr[:])
                    last.then_inc(s_fw, 1)
                if (s, k) == (10, 1):
                    pe.wait_ge(s_oh, b + 1)
                    bank_free(3, None)
                    mm(b_fin[:, 0:E], upper[:], ohb[:, 0, :], stop=False)
                    mm(b_fin[:, 0:E], ones_bf[:], acc[:, 0], start=False)
                    mm(b_fin[:, E:2 * E], upper[:], ohb[:, 1, :], stop=False)
                    mm(b_fin[:, E:2 * E], ones_bf[:], ohb[:, 0, :], start=False, stop=False)
                    mm(b_fin[:, E:2 * E], ones_bf[:], acc[:, 0], start=False).then_inc(s_fw, 1)

            def last_maxt(b, n):
                if isinstance(b, int) and b == B - 1:
                    return G * B
                return G * (b + 1) + n

            run(pe, maxima, attend, finish, side, maxt)

            def transposes(i, e, n):
                pe.wait_ge(s_ei[i], 16 * NR * n)
                wait(pe, s_etc, e)
                for r in range(NR):
                    w = min(P, CAP - r * P)
                    last = nc.tensor.transpose(banks[0][:, r * P:r * P + w], ein[0:w, i, r, :], ident[0:w, 0:w])
                last.then_inc(s_et, 1)

            def experts(e2):
                for i in range(2):
                    e = e2 * 2 + i
                    pe.wait_ge(s_ew[i], 16 * 2 * (e2 + 1))
                    pe.wait_ge(s_etc, e + 1)
                    for f in range(FT):
                        mm(banks[1 + f][:, 0:CAP], w1s[:, i, f * P:(f + 1) * P], einT[:, i, :]).then_inc(s_eh, 1)
                    if not (isinstance(e, int) and e == E - 1):
                        transposes(1 - i, e + 1, e2 + 1 + i)
                    pe.wait_ge(s_ehs, (e + 1) * (FT // 2))
                    pe.wait_ge(s_ehv, (e + 1) * (FT // 2))
                    wait(pe, s_eo, 2 * (e - 1))
                    for r in range(NR):
                        n = min(P, CAP - r * P)
                        for f in range(FT):
                            last = mm(banks[5 + i][0:n, r * D:(r + 1) * D], hT[:, i, f, r * P:r * P + n],
                                      w2s[:, i, f, :], start=f == 0, stop=f == FT - 1)
                    last.then_inc(s_eow, 1)

            transposes(0, 0, 1)
            experts(0)
            with pe.Fori(1, E // 2 - 1) as e2:
                experts(e2)
            experts(E // 2 - 1)


_INS = ['x', 'ctx_1024', 'L0_attn_Wq', 'L0_attn_Wk', 'L0_attn_Wv', 'L0_attn_Wp', 'L0_attn_pos_emb_k',
        'L0_xattn_Wq', 'L0_xattn_Wk', 'L0_xattn_Wv', 'L0_xattn_Wo', 'L0_ffn_Wr', 'L0_ffn_W1', 'L0_ffn_W2']


def kernel(**inputs):
    import numpy as _np
    import concourse.bacc as _bacc
    from concourse import mybir as _mybir
    from concourse.bass_utils import run_bass_kernel_spmd as _run

    nc = _bacc.Bacc("TRN2", target_bir_lowering=False, num_devices=1)
    arrays, ap = {}, {}
    for name in _INS:
        a = _np.ascontiguousarray(inputs[name])
        arrays[f"in_{name}_dram"] = a
        ap[name] = nc.dram_tensor(f"in_{name}_dram", a.shape, _mybir.dt.from_np(a.dtype), kind="ExternalInput").ap()
    out = nc.dram_tensor("out_0_dram", inputs["x"].shape, _mybir.dt.float32, kind="ExternalOutput").ap()
    decoder_layer(nc, ap['x'], ap['ctx_1024'],
                  [ap[f'L0_attn_{n}'] for n in ('Wq', 'Wk', 'Wv', 'Wp')], ap['L0_attn_pos_emb_k'],
                  [ap[f'L0_xattn_{n}'] for n in ('Wq', 'Wk', 'Wv', 'Wo')],
                  ap['L0_ffn_Wr'], ap['L0_ffn_W1'], ap['L0_ffn_W2'], out)
    r = _run(nc, [arrays], core_ids=[0])
    return r.results[0]["out_0_dram"]
```
